# Optimizing a Trainium2 kernel written in Bass

```python
import numpy as np
import jax
import jax.numpy as jnp

def _softmax(x, axis=-1):
    return jax.nn.softmax(x, axis=axis)

def _gelu(x):
    return jax.nn.gelu(x, approximate=True)

def _silu(x):
    return jax.nn.silu(x)

def _sigmoid(x):
    return jax.nn.sigmoid(x)

def _layernorm(x, axis=-1, eps=1e-05):
    m = jnp.mean(x, axis=axis, keepdims=True)
    v = jnp.var(x, axis=axis, keepdims=True)
    return (x - m) / jnp.sqrt(v + eps)

def _scatter_add(tgt, idx, src, axis=0):
    return tgt.at[idx].add(src)

def _segment_sum(src, seg, n):
    return jax.ops.segment_sum(src, seg, n)
kernel_name = 'mk_adj_ffn_d4_adj_r2_b0928f'

def setup_inputs(seed: int=0):
    np.random.seed(seed)
    _w = jnp.asarray

    def _rec_inputs():
        import jax
        import jax.numpy as jnp
        _gk = jax.random.key(seed)
        x = -8.776e-05 + 1 * jax.random.normal(jax.random.fold_in(_gk, 1), (4096, 128), jnp.float32)
        _w = (1.0 + jnp.arange(4096, dtype=jnp.float32)) ** (-0.5)
        _w = _w / _w.mean()
        _pij = jnp.clip(0.00195312 * _w[:, None] * _w[None, :], 0.0, 1.0)
        _a = jax.random.uniform(jax.random.fold_in(_gk, 2), (4096, 4096)) < _pij
        _a = jnp.logical_or(_a, jnp.eye(4096, dtype=bool))
        _af = _a.astype(jnp.float32)
        _af = _af * jax.random.uniform(jax.random.fold_in(_gk, 3), (4096, 4096), jnp.float32, 0.05, 1)
        adj = _af
        return (x, adj)
    x, adj = _rec_inputs()

    def _L0_gnn_setup():
        import jax, jax.numpy as jnp
        import numpy as np
        N = 10000
        D = 128
        F = 128
        K = F // 8
        key = jax.random.key(seed)
        k1, k2, k3, k4, k5 = jax.random.split(key, 5)
        h = jax.random.normal(k1, (N, D), dtype=jnp.float32)
        adj = jax.random.uniform(k2, (N, N), dtype=jnp.float32)
        W1 = jax.random.normal(k3, (D, K), dtype=jnp.float32) * 0.05
        W2 = jax.random.normal(k4, (K, D, F), dtype=jnp.float32) * 0.05
        b = jax.random.normal(k5, (K, F), dtype=jnp.float32) * 0.05
        return {'h': h, 'adj': adj, 'W1': W1, 'W2': W2, 'b': b}
    _L0_gnn_all = _L0_gnn_setup()
    _L0_gnn_in = {k: v for k, v in _L0_gnn_all.items() if k in ('W1', 'W2', 'b')}
    del _L0_gnn_all

    def _L0_ffn_setup():
        import jax, jax.numpy as jnp
        import numpy as np
        B, S, D, E, H, K = (4, 2048, 128, 8, 256, 2)
        key = jax.random.key(seed)
        ks = jax.random.split(key, 6)
        x = jax.random.normal(ks[0], (B, S, D), jnp.float32)
        Wg = jax.random.normal(ks[1], (D, E), jnp.float32) * 0.02
        bg = jnp.zeros((E,), jnp.float32)
        W1 = jax.random.normal(ks[2], (E, D, H), jnp.float32) * 0.02
        b1 = jnp.zeros((E, H), jnp.float32)
        W2 = jax.random.normal(ks[3], (E, H, D), jnp.float32) * 0.02
        b2 = jnp.zeros((E, D), jnp.float32)
        return {'x': x, 'Wg': Wg, 'bg': bg, 'W1': W1, 'b1': b1, 'W2': W2, 'b2': b2}
    _L0_ffn_all = _L0_ffn_setup()
    _L0_ffn_in = {k: v for k, v in _L0_ffn_all.items() if k in ('Wg', 'bg', 'W1', 'b1', 'W2', 'b2')}
    del _L0_ffn_all

    def _L1_gnn_setup():
        import jax, jax.numpy as jnp
        import numpy as np
        NEG_INF = -9000000000000000.0
        NEG_SLOPE = 0.2
        key = jax.random.key(seed)
        k1, k2, k3, k4 = jax.random.split(key, 4)
        N, d_in, d_out = (4096, 128, 128)
        x = jax.random.normal(k1, (N, d_in), dtype=jnp.float32)
        adj = jax.random.randint(k2, (N, N), 0, 2).astype(jnp.float32)
        W = jax.random.normal(k3, (d_in, d_out), dtype=jnp.float32) * (1.0 / np.sqrt(d_in))
        a = jax.random.normal(k4, (2 * d_out,), dtype=jnp.float32) * (1.0 / np.sqrt(2 * d_out))
        return {'x': x, 'adj': adj, 'W': W, 'a': a}
    _L1_gnn_all = _L1_gnn_setup()
    _L1_gnn_in = {k: v for k, v in _L1_gnn_all.items() if k in ('W', 'a')}
    del _L1_gnn_all

    def _L1_ffn_setup():
        import jax, jax.numpy as jnp
        import numpy as np
        B, S, H, NH, NE = (4, 512, 128, 4, 4)
        D = H // NH
        EPS = 1e-08

        def layernorm(x, g, b):
            m = jnp.mean(x, axis=-1, keepdims=True)
            v = jnp.mean((x - m) ** 2, axis=-1, keepdims=True)
            return (x - m) / jnp.sqrt(v + EPS) * g + b
        key = jax.random.key(seed)
        ks = jax.random.split(key, 18)
        sc = 0.05
        return {'x': jax.random.normal(ks[0], (B, S, H), jnp.float32), 'hl_w': jax.random.normal(ks[1], (NH, D, H), jnp.float32) * sc, 'hl_b': jax.random.normal(ks[2], (NH, D), jnp.float32) * sc, 'wq': jax.random.normal(ks[3], (NH, NE, D, D), jnp.float32) * sc, 'wk': jax.random.normal(ks[4], (NH, D, D), jnp.float32) * sc, 'wv': jax.random.normal(ks[5], (NH, D, D), jnp.float32) * sc, 'gate_w': jax.random.normal(ks[6], (NH, NE, NE * D), jnp.float32) * sc, 'gate_b': jax.random.normal(ks[7], (NH, NE), jnp.float32) * sc, 'ln_g': jnp.ones((D,), jnp.float32), 'ln_b': jnp.zeros((D,), jnp.float32), 'fc1_w': jax.random.normal(ks[8], (D, D), jnp.float32) * sc, 'fc1_b': jax.random.normal(ks[9], (D,), jnp.float32) * sc, 'fc2_w': jax.random.normal(ks[10], (D, D), jnp.float32) * sc, 'fc2_b': jax.random.normal(ks[11], (D,), jnp.float32) * sc, 'fnorm_g': jnp.ones((D,), jnp.float32), 'fnorm_b': jnp.zeros((D,), jnp.float32), 'fgate_w': jax.random.normal(ks[12], (NH, H), jnp.float32) * sc}
    _L1_ffn_all = _L1_ffn_setup()
    _L1_ffn_in = {k: v for k, v in _L1_ffn_all.items() if k in ('hl_w', 'hl_b', 'wq', 'wk', 'wv', 'gate_w', 'gate_b', 'ln_g', 'ln_b', 'fc1_w', 'fc1_b', 'fc2_w', 'fc2_b', 'fnorm_g', 'fnorm_b', 'fgate_w')}
    del _L1_ffn_all

    def _L2_gnn_setup():
        import jax, jax.numpy as jnp
        import numpy as np
        N = 4096
        D = 128
        DENSITY = 0.02
        key = jax.random.key(seed)
        k1, k2, k3, k4 = jax.random.split(key, 4)
        inputs = jax.random.normal(k1, (N, D), dtype=jnp.float32)
        vals = jax.random.uniform(k2, (N, N), dtype=jnp.float32, minval=0.1, maxval=1.0)
        mask = jax.random.uniform(k3, (N, N), dtype=jnp.float32) < DENSITY
        adj = jnp.where(mask, vals, 0.0)
        H_v = 0.1 * jax.random.normal(k4, (D, 1), dtype=jnp.float32)
        return {'inputs': inputs, 'adj': adj, 'H_v': H_v}
    _L2_gnn_all = _L2_gnn_setup()
    _L2_gnn_in = {k: v for k, v in _L2_gnn_all.items() if k in ('H_v',)}
    del _L2_gnn_all

    def _L2_ffn_setup():
        import jax, jax.numpy as jnp
        import numpy as np
        E, D, H, TOP_K = (6, 128, 128, 2)
        ROUTER_H = D // 2
        key = jax.random.key(seed)
        ks = jax.random.split(key, 12)
        s = 1.0 / np.sqrt(D)
        sh = 1.0 / np.sqrt(H)
        sr = 1.0 / np.sqrt(ROUTER_H)
        return {'features': jax.random.normal(ks[0], (8, 2048, D), dtype=jnp.float32), 'router_w1': jax.random.uniform(ks[1], (D, ROUTER_H), jnp.float32, -s, s), 'router_b1': jnp.zeros((ROUTER_H,), jnp.float32), 'router_w2': jax.random.uniform(ks[2], (ROUTER_H, E), jnp.float32, -sr, sr), 'router_b2': jnp.zeros((E,), jnp.float32), 'expert_w1': jax.random.uniform(ks[3], (E, D, H), jnp.float32, -s, s), 'expert_b1': jnp.zeros((E, H), jnp.float32), 'expert_w2': jax.random.uniform(ks[4], (E, H, H), jnp.float32, -sh, sh), 'expert_b2': jnp.zeros((E, H), jnp.float32), 'expert_w3': jax.random.uniform(ks[5], (E, H, D), jnp.float32, -sh, sh), 'expert_b3': jnp.zeros((E, D), jnp.float32)}
    _L2_ffn_all = _L2_ffn_setup()
    _L2_ffn_in = {k: v for k, v in _L2_ffn_all.items() if k in ('router_w1', 'router_b1', 'router_w2', 'router_b2', 'expert_w1', 'expert_b1', 'expert_w2', 'expert_b2', 'expert_w3', 'expert_b3')}
    del _L2_ffn_all

    def _L3_gnn_setup():
        import jax, jax.numpy as jnp
        import numpy as np
        key = jax.random.key(seed)
        k1, k2, k3, k4 = jax.random.split(key, 4)
        N, F_in, F_out = (4096, 128, 128)
        x = jax.random.normal(k1, (N, F_in), dtype=jnp.float32)
        adj = jax.random.uniform(k2, (N, N), dtype=jnp.float32)
        lim = 1.0 / np.sqrt(F_in)
        W = jax.random.uniform(k3, (F_out, F_in), dtype=jnp.float32, minval=-lim, maxval=lim)
        b = jax.random.uniform(k4, (F_out,), dtype=jnp.float32, minval=-lim, maxval=lim)
        return {'x': x, 'adj': adj, 'W': W, 'b': b}
    _L3_gnn_all = _L3_gnn_setup()
    _L3_gnn_in = {k: v for k, v in _L3_gnn_all.items() if k in ('W', 'b')}
    del _L3_gnn_all

    def _L3_ffn_setup():
        import jax, jax.numpy as jnp
        import numpy as np
        N_EXPERTS = 8
        TOP_K = 2
        key = jax.random.key(seed)
        ks = jax.random.split(key, 5)
        B, T, C, E, H = (8, 1024, 128, 8, 341)
        scale = 1.0 / np.sqrt(C)
        return {'x': jax.random.normal(ks[0], (B, T, C), dtype=jnp.float32), 'router_w': jax.random.normal(ks[1], (E, C), dtype=jnp.float32) * scale, 'w1': jax.random.normal(ks[2], (E, H, C), dtype=jnp.float32) * scale, 'w2': jax.random.normal(ks[3], (E, C, H), dtype=jnp.float32) * (1.0 / np.sqrt(H)), 'w3': jax.random.normal(ks[4], (E, H, C), dtype=jnp.float32) * scale}
    _L3_ffn_all = _L3_ffn_setup()
    _L3_ffn_in = {k: v for k, v in _L3_ffn_all.items() if k in ('router_w', 'w1', 'w2', 'w3')}
    del _L3_ffn_all
    return {'x': x, 'adj': adj, 'L0_gnn_W1': _L0_gnn_in['W1'], 'L0_gnn_W2': _L0_gnn_in['W2'], 'L0_gnn_b': _L0_gnn_in['b'], 'L0_ffn_Wg': _L0_ffn_in['Wg'], 'L0_ffn_bg': _L0_ffn_in['bg'], 'L0_ffn_W1': _L0_ffn_in['W1'], 'L0_ffn_b1': _L0_ffn_in['b1'], 'L0_ffn_W2': _L0_ffn_in['W2'], 'L0_ffn_b2': _L0_ffn_in['b2'], 'L1_gnn_W': _L1_gnn_in['W'], 'L1_gnn_a': _L1_gnn_in['a'], 'L1_ffn_hl_w': _L1_ffn_in['hl_w'], 'L1_ffn_hl_b': _L1_ffn_in['hl_b'], 'L1_ffn_wq': _L1_ffn_in['wq'], 'L1_ffn_wk': _L1_ffn_in['wk'], 'L1_ffn_wv': _L1_ffn_in['wv'], 'L1_ffn_gate_w': _L1_ffn_in['gate_w'], 'L1_ffn_gate_b': _L1_ffn_in['gate_b'], 'L1_ffn_ln_g': _L1_ffn_in['ln_g'], 'L1_ffn_ln_b': _L1_ffn_in['ln_b'], 'L1_ffn_fc1_w': _L1_ffn_in['fc1_w'], 'L1_ffn_fc1_b': _L1_ffn_in['fc1_b'], 'L1_ffn_fc2_w': _L1_ffn_in['fc2_w'], 'L1_ffn_fc2_b': _L1_ffn_in['fc2_b'], 'L1_ffn_fnorm_g': _L1_ffn_in['fnorm_g'], 'L1_ffn_fnorm_b': _L1_ffn_in['fnorm_b'], 'L1_ffn_fgate_w': _L1_ffn_in['fgate_w'], 'L2_gnn_H_v': _L2_gnn_in['H_v'], 'L2_ffn_router_w1': _L2_ffn_in['router_w1'], 'L2_ffn_router_b1': _L2_ffn_in['router_b1'], 'L2_ffn_router_w2': _L2_ffn_in['router_w2'], 'L2_ffn_router_b2': _L2_ffn_in['router_b2'], 'L2_ffn_expert_w1': _L2_ffn_in['expert_w1'], 'L2_ffn_expert_b1': _L2_ffn_in['expert_b1'], 'L2_ffn_expert_w2': _L2_ffn_in['expert_w2'], 'L2_ffn_expert_b2': _L2_ffn_in['expert_b2'], 'L2_ffn_expert_w3': _L2_ffn_in['expert_w3'], 'L2_ffn_expert_b3': _L2_ffn_in['expert_b3'], 'L3_gnn_W': _L3_gnn_in['W'], 'L3_gnn_b': _L3_gnn_in['b'], 'L3_ffn_router_w': _L3_ffn_in['router_w'], 'L3_ffn_w1': _L3_ffn_in['w1'], 'L3_ffn_w2': _L3_ffn_in['w2'], 'L3_ffn_w3': _L3_ffn_in['w3']}

def reference(x, adj, L0_gnn_W1, L0_gnn_W2, L0_gnn_b, L0_ffn_Wg, L0_ffn_bg, L0_ffn_W1, L0_ffn_b1, L0_ffn_W2, L0_ffn_b2, L1_gnn_W, L1_gnn_a, L1_ffn_hl_w, L1_ffn_hl_b, L1_ffn_wq, L1_ffn_wk, L1_ffn_wv, L1_ffn_gate_w, L1_ffn_gate_b, L1_ffn_ln_g, L1_ffn_ln_b, L1_ffn_fc1_w, L1_ffn_fc1_b, L1_ffn_fc2_w, L1_ffn_fc2_b, L1_ffn_fnorm_g, L1_ffn_fnorm_b, L1_ffn_fgate_w, L2_gnn_H_v, L2_ffn_router_w1, L2_ffn_router_b1, L2_ffn_router_w2, L2_ffn_router_b2, L2_ffn_expert_w1, L2_ffn_expert_b1, L2_ffn_expert_w2, L2_ffn_expert_b2, L2_ffn_expert_w3, L2_ffn_expert_b3, L3_gnn_W, L3_gnn_b, L3_ffn_router_w, L3_ffn_w1, L3_ffn_w2, L3_ffn_w3):
    import jax
    import jax.numpy as jnp

    def _L0_gnn_ref(h, adj, W1, W2, b):
        import jax, jax.numpy as jnp
        import numpy as np
        N = 10000
        D = 128
        F = 128
        K = F // 8
        node = h @ W1
        hw = jnp.einsum('nc,kcf->nkf', h, W2)
        x = jnp.einsum('nk,nkf->nf', node, hw)
        x = adj @ x
        x = x + node @ b
        return jax.nn.relu(x)

    def _L0_ffn_ref(x, Wg, bg, W1, b1, W2, b2):
        import jax, jax.numpy as jnp
        import numpy as np
        B, S, D, E, H, K = (4, 2048, 128, 8, 256, 2)
        Bv, Sv, Dv = x.shape
        gate_scores = x @ Wg + bg
        _, idx = jax.lax.top_k(gate_scores, K)
        mask = jax.nn.one_hot(idx, E, dtype=x.dtype).sum(axis=-2)
        xf = x.reshape(-1, Dv)
        mf = mask.reshape(-1, E)
        h = jax.nn.gelu(jnp.einsum('td,edh->teh', xf, W1) + b1[None], approximate=False)
        y = jnp.einsum('teh,ehd->ted', h, W2) + b2[None]
        out = jnp.einsum('ted,te->td', y, mf)
        return out.reshape(Bv, Sv, Dv)

    def _L1_gnn_ref(x, adj, W, a):
        import jax, jax.numpy as jnp
        import numpy as np
        NEG_INF = -9000000000000000.0
        NEG_SLOPE = 0.2
        d_out = W.shape[1]
        Wh = x @ W
        e_src = Wh @ a[:d_out]
        e_dst = Wh @ a[d_out:]
        e = jax.nn.leaky_relu(e_src[:, None] + e_dst[None, :], NEG_SLOPE)
        N = Wh.shape[0]
        mask = (adj > 0) | jnp.eye(N, dtype=bool)
        e = jnp.where(mask, e, NEG_INF)
        alpha = jax.nn.softmax(e, axis=1)
        h = alpha @ Wh
        return h

    def _L1_ffn_ref(x, hl_w, hl_b, wq, wk, wv, gate_w, gate_b, ln_g, ln_b, fc1_w, fc1_b, fc2_w, fc2_b, fnorm_g, fnorm_b, fgate_w):
        import jax, jax.numpy as jnp
        import numpy as np
        B, S, H, NH, NE = (4, 512, 128, 4, 4)
        D = H // NH
        EPS = 1e-08

        def layernorm(x, g, b):
            m = jnp.mean(x, axis=-1, keepdims=True)
            v = jnp.mean((x - m) ** 2, axis=-1, keepdims=True)
            return (x - m) / jnp.sqrt(v + EPS) * g + b
        b, s, h = x.shape
        nh, d, _ = wk.shape
        ne = wq.shape[1]
        sx = jnp.einsum('bsh,ndh->bnsd', x, hl_w) + hl_b[None, :, None, :]
        pad = sx == 0
        q = jnp.einsum('bnsd,neod->bneso', sx, wq)
        k = jnp.einsum('bnsd,nod->bnso', sx, wk)
        v = jnp.einsum('bnsd,nod->bnso', sx, wv)
        causal = jnp.where(jnp.tril(jnp.ones((s, s), bool)), 0.0, -jnp.inf).astype(x.dtype)
        scores = jnp.einsum('bnesd,bntd->bnest', q, k) * d ** 0.5 + causal
        att = jax.nn.softmax(scores, axis=-1)
        qkv = jnp.einsum('bnest,bntd->bnesd', att, v)
        qkv = jnp.where(pad[:, :, None], 0.0, qkv)
        out = jnp.transpose(qkv, (0, 1, 3, 2, 4)).reshape(b, nh, s, ne * d)
        gs = jax.nn.softmax(jnp.einsum('bnsf,nef->bnse', out, gate_w) + gate_b[None, :, None, :], axis=-1)
        mixed = jnp.einsum('bnsed,bnse->bnsd', out.reshape(b, nh, s, ne, d), gs)
        resid = sx[jnp.arange(nh), jnp.arange(nh)]
        hn = layernorm(mixed + resid, ln_g, ln_b)
        f_n = jnp.transpose(hn, (0, 2, 1, 3)).reshape(b, s, h)
        fx = f_n.reshape(b, s, nh, d)
        pm = fx == 0
        hx = jnp.where(pm, 0.0, fx @ fc1_w.T + fc1_b)
        hx = jax.nn.relu(hx)
        hx = jnp.where(pm, 0.0, hx @ fc2_w.T + fc2_b)
        hx = layernorm(hx + fx, fnorm_g, fnorm_b)
        fout = hx.reshape(b, s, h)
        fg = jax.nn.softmax(fout @ fgate_w.T, axis=-1)
        return (fout.reshape(b, s, nh, d) * fg[..., None]).reshape(b, s, h)

    def _L2_gnn_ref(inputs, adj, H_v):
        import jax, jax.numpy as jnp
        import numpy as np
        N = 4096
        D = 128
        DENSITY = 0.02
        scores = jnp.squeeze(inputs @ H_v, -1)
        mask = adj != 0.0
        logits = adj * scores[None, :]
        neg = jnp.asarray(jnp.finfo(logits.dtype).min, logits.dtype)
        logits = jnp.where(mask, logits, neg)
        m = jnp.max(logits, axis=1, keepdims=True)
        e = jnp.where(mask, jnp.exp(logits - m), 0.0)
        s = jnp.sum(e, axis=1, keepdims=True)
        weights = e / jnp.where(s > 0, s, 1.0)
        return weights @ inputs

    def _L2_ffn_ref(features, router_w1, router_b1, router_w2, router_b2, expert_w1, expert_b1, expert_w2, expert_b2, expert_w3, expert_b3):
        import jax, jax.numpy as jnp
        import numpy as np
        E, D, H, TOP_K = (6, 128, 128, 2)
        ROUTER_H = D // 2
        rh = jax.nn.relu(features @ router_w1 + router_b1)
        expert_logits = jax.nn.softmax(rh @ router_w2 + router_b2, axis=-1)
        top_w, top_i = jax.lax.top_k(expert_logits, TOP_K)
        routing_weights = jax.nn.softmax(top_w, axis=-1)
        h1 = jax.nn.relu(jnp.einsum('bsd,edh->bseh', features, expert_w1) + expert_b1)
        h2 = jax.nn.relu(jnp.einsum('bseh,ehf->bsef', h1, expert_w2) + expert_b2)
        expert_out = jnp.einsum('bsef,efo->bseo', h2, expert_w3) + expert_b3
        sel = jnp.take_along_axis(expert_out, top_i[:, :, :, None], axis=2)
        combined = jnp.sum(sel * routing_weights[..., None], axis=2)
        return combined

    def _L3_gnn_ref(x, adj, W, b):
        import jax, jax.numpy as jnp
        import numpy as np
        N = adj.shape[0]
        adj = adj + jnp.eye(N, dtype=adj.dtype)
        deg = adj.sum(axis=1)
        deg_inv_sqrt = deg ** (-0.5)
        deg_inv_sqrt = jnp.where(jnp.isinf(deg_inv_sqrt), 0.0, deg_inv_sqrt)
        adj_normalized = deg_inv_sqrt[:, None] * adj * deg_inv_sqrt[None, :]
        support = x @ W.T + b
        return adj_normalized @ support

    def _L3_ffn_ref(x, router_w, w1, w2, w3):
        import jax, jax.numpy as jnp
        import numpy as np
        N_EXPERTS = 8
        TOP_K = 2
        B, T, C = x.shape
        flat = x.reshape(-1, C)
        logits = flat @ router_w.T
        probs = jax.nn.softmax(logits, axis=-1)
        topk_probs, topk_idx = jax.lax.top_k(probs, TOP_K)
        topk_probs = topk_probs / (jnp.sum(topk_probs, axis=-1, keepdims=True) + 1e-09)
        onehot = jax.nn.one_hot(topk_idx, N_EXPERTS, dtype=flat.dtype)
        gates = jnp.einsum('nk,nke->ne', topk_probs, onehot)
        h1 = jnp.einsum('nc,ehc->neh', flat, w1)
        h3 = jnp.einsum('nc,ehc->neh', flat, w3)
        h = jax.nn.silu(h1) * h3
        y = jnp.einsum('neh,ech->nec', h, w2)
        out = jnp.einsum('ne,nec->nc', gates, y)
        return out.reshape(B, T, C)
    x = x + _L0_gnn_ref(_layernorm(x, axis=-1), adj, L0_gnn_W1, L0_gnn_W2, L0_gnn_b)
    x = x + _L0_ffn_ref(_layernorm(x, axis=-1)[None], L0_ffn_Wg, L0_ffn_bg, L0_ffn_W1, L0_ffn_b1, L0_ffn_W2, L0_ffn_b2)[0]
    x = x + _L1_gnn_ref(_layernorm(x, axis=-1), adj, L1_gnn_W, L1_gnn_a)
    x = x + _L1_ffn_ref(_layernorm(x, axis=-1)[None], L1_ffn_hl_w, L1_ffn_hl_b, L1_ffn_wq, L1_ffn_wk, L1_ffn_wv, L1_ffn_gate_w, L1_ffn_gate_b, L1_ffn_ln_g, L1_ffn_ln_b, L1_ffn_fc1_w, L1_ffn_fc1_b, L1_ffn_fc2_w, L1_ffn_fc2_b, L1_ffn_fnorm_g, L1_ffn_fnorm_b, L1_ffn_fgate_w)[0]
    x = x + _L2_gnn_ref(_layernorm(x, axis=-1), adj, L2_gnn_H_v)
    x = x + _L2_ffn_ref(_layernorm(x, axis=-1)[None], L2_ffn_router_w1, L2_ffn_router_b1, L2_ffn_router_w2, L2_ffn_router_b2, L2_ffn_expert_w1, L2_ffn_expert_b1, L2_ffn_expert_w2, L2_ffn_expert_b2, L2_ffn_expert_w3, L2_ffn_expert_b3)[0]
    x = x + _L3_gnn_ref(_layernorm(x, axis=-1), adj, L3_gnn_W, L3_gnn_b)
    x = x + _L3_ffn_ref(_layernorm(x, axis=-1)[None], L3_ffn_router_w, L3_ffn_w1, L3_ffn_w2, L3_ffn_w3)[0]
    return x

_drawn_inputs = setup_inputs


def setup_inputs(seed=0):
    import zlib

    import numpy as np

    out = dict(_drawn_inputs(seed))
    spreads = {'L0_ffn_bg': (0.0, 0.1),
     'L0_ffn_b1': (0.0, 0.338),
     'L0_ffn_b2': (0.0, 0.1),
     'L1_ffn_ln_g': (1.0, 0.2),
     'L1_ffn_ln_b': (0.0, 0.272),
     'L1_ffn_fnorm_g': (1.0, 0.2),
     'L1_ffn_fnorm_b': (0.0, 0.285),
     'L2_ffn_router_b1': (0.0, 0.375),
     'L2_ffn_router_b2': (0.0, 0.303),
     'L2_ffn_expert_b1': (0.0, 0.694),
     'L2_ffn_expert_b2': (0.0, 0.414),
     'L2_ffn_expert_b3': (0.0, 0.1)}
    factors = {'L1_ffn_wq': 7.6,
     'L1_ffn_wk': 7.799,
     'L1_ffn_wv': 2.683,
     'L1_ffn_gate_w': 8.0,
     'L1_ffn_gate_b': 24.506,
     'L1_ffn_fc1_w': 4.601,
     'L1_ffn_fc1_b': 8.0,
     'L1_ffn_fc2_w': 4.124,
     'L1_ffn_fc2_b': 3.297}
    for name, (base, spread) in spreads.items():
        noise = np.random.default_rng([zlib.crc32(name.encode()), seed]).standard_normal(out[name].shape)
        drawn = base * np.exp(spread * noise) if base else spread * noise
        out[name] = jnp.asarray(drawn.astype(out[name].dtype))
    for name, factor in factors.items():
        out[name] = (out[name] * factor).astype(out[name].dtype)
    return out
```

```python
import concourse.bass as bass
from concourse import mybir
from contextlib import ExitStack

FP32 = mybir.dt.float32
FP16 = mybir.dt.float16
ALU = mybir.AluOpType
ACT = mybir.ActivationFunctionType
AX = mybir.AxisListType
ds = bass.ds

P = 128
N = 4096
T = N // P
GT = 4
GW = GT * P
G = T // GT
D = 128
NODE_K = 16
BIG = 1.0e30
EPS_LN = 1e-5


def over(ap, n):
    return ap.unsqueeze(2).broadcast_to([ap.shape[0], ap.shape[1], n])


def rows(ap, n):
    return ap.unsqueeze(1).broadcast_to([ap.shape[0], n, ap.shape[1]])


class Core:

    def __init__(self, nc, ctx):
        self.nc, self.ctx, self.n, self.sems = nc, ctx, 0, []
        self.x = self.keep("x_nat", [P, T, D])
        self.xn = self.keep("x_normed", [P, T, D])
        self.xT = self.keep("x_normedT", [P, N])
        self.ident = self.keep("ident", [P, P])
        self.ident16 = self.keep("ident16", [P, P], FP16)
        self.deg = self.keep("deg", [P, T])
        self.banks = ctx.enter_context(nc.psum_tensor("banks", [P, 8, GW], FP32))
        self.psum = [self.banks[:, i, :] for i in range(8)]

    def keep(self, name, shape, dt=FP32):
        return self.ctx.enter_context(self.nc.sbuf_tensor(name, shape, dt))

    def sem(self, name):
        self.n += 1
        s = self.layer.enter_context(self.nc.semaphore(f"{name}_{self.n}"))
        self.sems.append(s)
        return s

    def begin_layer(self):
        self.layer, self.sems = ExitStack(), []

    def end_layer(self):
        with self.nc.Block() as block:
            @block.gpsimd
            def _(pool):
                for s in self.sems:
                    pool.sem_clear(s)
        self.layer.close()


def load_inputs(core, x):
    nc = core.nc
    loaded, zeroed = core.sem("x_loaded"), core.sem("ident_zeroed")
    with nc.Block() as block:
        @block.sync
        def _(sp):
            sp.dma_start(core.x[:, :, :], x.rearrange("(t p) d -> p t d", p=P)).then_inc(loaded, 16)
            sp.wait_ge(loaded, 16)

        @block.gpsimd
        def _(pool):
            for m in (core.ident, core.ident16):
                nc.gpsimd.memset(m[:, :], 0.0).then_inc(zeroed, 1)
            pool.wait_ge(zeroed, 2)
            for m in (core.ident, core.ident16):
                nc.gpsimd.affine_select(out=m[:, :], in_=m[:, :], compare_op=ALU.not_equal, fill=1.0,
                                        base=0, pattern=[[-1, P]], channel_multiplier=1)


def store_output(core, out):
    nc = core.nc
    stored = core.sem("out_stored")
    with nc.Block() as block:
        @block.sync
        def _(sp):
            sp.dma_start(out.rearrange("(t p) d -> p t d", p=P), core.x[:, :, :]).then_inc(stored, 16)
            sp.wait_ge(stored, 16)


def norm_stage(core, loads, tag, proj=None):
    nc = core.nc
    x, xn, xT = core.x, core.xn, core.xT
    with ExitStack() as own:
        def sb(name, shape):
            return own.enter_context(nc.sbuf_tensor(f"{tag}_{name}", shape, FP32))
        mean, var, rstd = sb("mean", [P, T]), sb("var", [P, T]), sb("rstd", [P, T])
        sq = sb("sq", [P, T, D])
        centred, squared = core.sem(tag + "centred"), core.sem(tag + "squared")
        var_ready, std_ready = core.sem(tag + "var_ready"), core.sem(tag + "std_ready")
        normed, turned, copied = core.sem(tag + "normed"), core.sem(tag + "turned"), core.sem(tag + "copied")
        loaded = core.sem(tag + "w_loaded")
        projected, dma_in = core.sem(tag + "projected"), core.sem(tag + "dma_in")
        w = proj[0].shape[1] if proj else 0

        with nc.Block() as block:
            @block.sync
            def _(sp):
                for dst, src in loads:
                    sp.dma_start(dst, src).then_inc(loaded, 16)
                if loads:
                    sp.wait_ge(loaded, 16 * len(loads))

            @block.vector
            def _(dve):
                nc.vector.tensor_reduce(mean[:, :], x[:, :, :], AX.X, ALU.add)
                dve.drain()
                nc.vector.tensor_scalar(mean[:, :], mean[:, :], 1.0 / D, None, ALU.mult)
                dve.drain()
                for h in range(2):
                    a = slice(h * T // 2, (h + 1) * T // 2)
                    nc.vector.tensor_tensor(xn[:, a, :], x[:, a, :], over(mean[:, a], D),
                                            ALU.subtract).then_inc(centred, 1)
                for h in range(2):
                    a = slice(h * T // 2, (h + 1) * T // 2)
                    dve.wait_ge(squared, h + 1)
                    nc.vector.tensor_reduce(var[:, a], sq[:, a, :], AX.X, ALU.add)
                dve.drain()
                nc.vector.tensor_scalar(var[:, :], var[:, :], 1.0 / D, EPS_LN, ALU.mult,
                                        ALU.add).then_inc(var_ready, 1)
                dve.wait_ge(std_ready, 1)
                nc.vector.reciprocal(rstd[:, :], rstd[:, :])
                dve.drain()
                for g in range(G):
                    a = slice(g * GT, (g + 1) * GT)
                    nc.vector.tensor_tensor(xn[:, a, :], xn[:, a, :], over(rstd[:, a], D),
                                            ALU.mult).then_inc(normed, 1)
                if proj:
                    dve.wait_ge(projected, 1)
                    bank = core.psum[6][:, 0:T * w].rearrange("p (t w) -> p t w", w=w)
                    if proj[1] is None:
                        nc.vector.tensor_copy(proj[2], bank)
                    else:
                        dve.wait_ge(loaded, 16 * len(loads))
                        nc.vector.tensor_tensor(proj[2], bank, rows(proj[1], T), ALU.add)

            @block.scalar
            def _(act):
                for h in range(2):
                    a = slice(h * T // 2, (h + 1) * T // 2)
                    act.wait_ge(centred, h + 1)
                    nc.scalar.activation(sq[:, a, :], xn[:, a, :], ACT.Square).then_inc(squared, 1)
                act.wait_ge(var_ready, 1)
                nc.scalar.activation(rstd[:, :], var[:, :], ACT.Sqrt).then_inc(std_ready, 1)
                for g in range(G):
                    act.wait_ge(turned, g + 1)
                    nc.scalar.activation(xT[:, g * GW:(g + 1) * GW], core.psum[g % 4][:, :],
                                         ACT.Copy).then_inc(copied, 1)

            @block.tensor
            def _(pe):
                for g in range(G):
                    pe.wait_ge(normed, g + 1)
                    if g >= 4:
                        pe.wait_ge(copied, g - 3)
                    for r in range(GT):
                        last = nc.tensor.transpose(core.psum[g % 4][:, r * P:(r + 1) * P],
                                                   xn[:, g * GT + r, :], core.ident[:, :])
                    last.then_inc(turned, 1)
                if proj:
                    pe.wait_ge(copied, G)
                    pe.wait_ge(loaded, 16 * len(loads))
                    for t in range(T):
                        last = nc.tensor.matmul(core.psum[6][:, t * w:(t + 1) * w],
                                                xT[:, t * P:(t + 1) * P], proj[0],
                                                start=True, stop=True)
                    last.then_inc(projected, 1)


def top2(nc, dve, sb, score, e, second):
    hot1, hot2, cand, rest = (sb(n, [P, T, e]) for n in ("hot1", "hot2", "cand", "rest"))
    order = sb("order", [P, e])
    best, pick = sb("best", [P, T]), sb("pick", [P, T])
    for j in range(e):
        nc.vector.memset(order[:, j:j + 1], float(e - j))
    dve.drain()
    for hot, src, top in ((hot1, score, best), (hot2, rest, second)):
        nc.vector.tensor_reduce(top[:, :], src[:, :, :], AX.X, ALU.max)
        dve.drain()
        nc.vector.tensor_tensor(cand[:, :, :], src[:, :, :], over(top[:, :], e), ALU.is_equal)
        dve.drain()
        nc.vector.tensor_tensor(cand[:, :, :], cand[:, :, :], rows(order[:, :], T), ALU.mult)
        dve.drain()
        nc.vector.tensor_reduce(pick[:, :], cand[:, :, :], AX.X, ALU.max)
        dve.drain()
        nc.vector.tensor_tensor(hot[:, :, :], cand[:, :, :], over(pick[:, :], e), ALU.is_equal)
        dve.drain()
        if hot is hot1:
            nc.vector.scalar_tensor_tensor(rest[:, :, :], hot1[:, :, :], -BIG, score[:, :, :],
                                           ALU.mult, ALU.add)
            dve.drain()
    return hot1, hot2, best


def gates_onehot(core, score, e, gates, tag):
    nc = core.nc
    with ExitStack() as own:
        def sb(name, shape):
            return own.enter_context(nc.sbuf_tensor(f"{tag}_{name}", shape, FP32))
        second = sb("second", [P, T])
        with nc.Block() as block:
            @block.vector
            def _(dve):
                hot1, hot2, _best = top2(nc, dve, sb, score, e, second)
                nc.vector.tensor_tensor(gates[:, :, :], hot1[:, :, :], hot2[:, :, :], ALU.add)


def gates_softmax(core, score, e, gates, renorm, tag):
    nc = core.nc
    with ExitStack() as own:
        def sb(name, shape):
            return own.enter_context(nc.sbuf_tensor(f"{tag}_{name}", shape, FP32))
        top, den, second = sb("top", [P, T]), sb("den", [P, T]), sb("second", [P, T])
        prob = sb("prob", [P, T, e])
        shifted, exped = core.sem(tag + "shifted"), core.sem(tag + "exped")
        with nc.Block() as block:
            @block.vector
            def _(dve):
                nc.vector.tensor_reduce(top[:, :], score[:, :, :], AX.X, ALU.max)
                dve.drain()
                nc.vector.tensor_tensor(prob[:, :, :], score[:, :, :], over(top[:, :], e),
                                        ALU.subtract).then_inc(shifted, 1)
                dve.wait_ge(exped, 1)
                nc.vector.tensor_reduce(den[:, :], prob[:, :, :], AX.X, ALU.add)
                dve.drain()
                nc.vector.reciprocal(den[:, :], den[:, :])
                dve.drain()
                nc.vector.tensor_tensor(prob[:, :, :], prob[:, :, :], over(den[:, :], e), ALU.mult)
                dve.drain()
                hot1, hot2, best = top2(nc, dve, sb, prob, e, second)
                if renorm:
                    nc.vector.scalar_tensor_tensor(den[:, :], best[:, :], 1e-9, second[:, :],
                                                   ALU.add, ALU.add)
                else:
                    nc.vector.tensor_tensor(second[:, :], second[:, :], best[:, :],
                                            ALU.subtract).then_inc(shifted, 1)
                    dve.wait_ge(exped, 2)
                    nc.vector.memset(best[:, :], 1.0)
                    nc.vector.tensor_scalar(den[:, :], second[:, :], 1.0, None, ALU.add)
                dve.drain()
                nc.vector.reciprocal(den[:, :], den[:, :])
                dve.drain()
                nc.vector.tensor_tensor(best[:, :], best[:, :], den[:, :], ALU.mult)
                nc.vector.tensor_tensor(second[:, :], second[:, :], den[:, :], ALU.mult)
                dve.drain()
                nc.vector.tensor_tensor(hot1[:, :, :], hot1[:, :, :], over(best[:, :], e), ALU.mult)
                nc.vector.tensor_tensor(hot2[:, :, :], hot2[:, :, :], over(second[:, :], e), ALU.mult)
                dve.drain()
                nc.vector.tensor_tensor(gates[:, :, :], hot1[:, :, :], hot2[:, :, :], ALU.add)

            @block.scalar
            def _(act):
                act.wait_ge(shifted, 1)
                nc.scalar.activation(prob[:, :, :], prob[:, :, :], ACT.Exp).then_inc(exped, 1)
                if not renorm:
                    act.wait_ge(shifted, 2)
                    nc.scalar.activation(second[:, :], second[:, :], ACT.Exp).then_inc(exped, 1)

def add_expert(core, dve, bank, gates, g, ex, bias, yb, taken, x):
    nc = core.nc
    if bias is not None:
        nc.vector.tensor_tensor(yb[:, ex % 2, :, :], bank[:, :].rearrange("p (r d) -> p r d", d=D),
                                rows(bias, GT), ALU.add).then_inc(taken, 1)
        dve.drain()
    for r in range(GT):
        src = yb[:, ex % 2, r, :] if bias is not None else bank[:, r * P:(r + 1) * P]
        row = x[:, ds(g * GT + r, 1), :]
        last = nc.vector.scalar_tensor_tensor(
            row, src.unsqueeze(1), gates[:, ds(g * GT + r, 1), ex:ex + 1].rearrange("p a b -> p (a b)"),
            row, ALU.mult, ALU.add)
    if bias is None:
        last.then_inc(taken, 1)
        dve.drain()


def experts_gelu(core, e, w1, b1, w2, b2, gates, tag):
    nc, x = core.nc, core.x
    C, RING = 2, 4
    U = e * C
    with ExitStack() as own:
        def sb(name, shape):
            return own.enter_context(nc.sbuf_tensor(f"{tag}_{name}", shape, FP32))
        hid = sb("hid", [P, 2, C, GW])
        yb = sb("yb", [P, 2, GT, D])
        sums = core.sem(tag + "hidden_sums")
        hidden = core.sem(tag + "hidden_ready")
        down_done = core.sem(tag + "down_done")
        taken = core.sem(tag + "y_taken")
        with nc.Block() as block:
            @block.tensor
            def _(pe):
                pe.sem_inc(down_done, 2)
                with pe.Fori(0, G) as g:
                    for s in range(e + 1):
                        if s < e:
                            for c in range(C):
                                n = s * C + c
                                pe.wait_ge(hidden, g * U + (n + 1))
                                nc.tensor.matmul(core.psum[n % RING][:, :], w1[:, s, c * P:(c + 1) * P],
                                                 core.xT[:, ds(g * GW, GW)], start=True,
                                                 stop=True).then_inc(sums, 1)
                        if s >= 1:
                            ex = s - 1
                            pe.wait_ge(hidden, g * U + ((ex + 1) * C + RING))
                            pe.wait_ge(taken, g * e + (ex + 1))
                            for r in range(GT):
                                for c in range(C):
                                    last = nc.tensor.matmul(core.psum[6 + ex % 2][:, r * P:(r + 1) * P],
                                                            hid[:, ex % 2, c, r * P:(r + 1) * P],
                                                            w2[:, ex, c, :], start=(c == 0), stop=(c == C - 1))
                            last.then_inc(down_done, 1)

            @block.scalar
            def _(act):
                act.sem_inc(hidden, RING)
                with act.Fori(0, G) as g:
                    for ex in range(e):
                        act.wait_ge(down_done, g * e + (ex + 1))
                        for c in range(C):
                            n = ex * C + c
                            act.wait_ge(sums, g * U + (n + 1))
                            nc.scalar.activation(hid[:, ex % 2, c, :], core.psum[n % RING][:, :], ACT.Gelu,
                                                 bias=b1[:, ex, c:c + 1]).then_inc(hidden, 1)

            @block.vector
            def _(dve):
                dve.sem_inc(taken, 2)
                with dve.Fori(0, G) as g:
                    for ex in range(e):
                        dve.wait_ge(down_done, g * e + (ex + 3))
                        add_expert(core, dve, core.psum[6 + ex % 2], gates, g, ex, b2[:, ex, :], yb, taken, x)
                    dve.drain()


def experts_deep(core, e, w1, b1, w2, b2, w3, b3, gates, tag):
    nc, x = core.nc, core.x
    RING = 4
    U = 2 * e
    order = []
    for s in range(e + 1):
        if s < e:
            order.append((s, 0))
        if s >= 1:
            order.append((s - 1, 1))
    turn = {k: n for n, k in enumerate(order)}
    with ExitStack() as own:
        def sb(name, shape):
            return own.enter_context(nc.sbuf_tensor(f"{tag}_{name}", shape, FP32))
        hid = sb("hid", [P, 2, 2, GW])
        yb = sb("yb", [P, 2, GT, D])
        sums = core.sem(tag + "hidden_sums")
        hidden = core.sem(tag + "hidden_ready")
        down_done = core.sem(tag + "down_done")
        taken = core.sem(tag + "y_taken")
        with nc.Block() as block:
            @block.tensor
            def _(pe):
                pe.sem_inc(down_done, 2)
                with pe.Fori(0, G) as g:
                    def fill(ex, level, rhs):
                        n = turn[ex, level]
                        pe.wait_ge(hidden, g * U + (n + 1))
                        nc.tensor.matmul(core.psum[n % RING][:, :], (w1, w2)[level][:, ex, :], rhs,
                                         start=True, stop=True).then_inc(sums, 1)

                    for s in range(e + 2):
                        if s < e:
                            fill(s, 0, core.xT[:, ds(g * GW, GW)])
                        if 1 <= s <= e:
                            pe.wait_ge(hidden, g * U + (turn[s - 1, 0] + 1 + RING))
                            fill(s - 1, 1, hid[:, (s - 1) % 2, 0, :])
                        if s >= 2:
                            ex = s - 2
                            pe.wait_ge(hidden, g * U + (turn[ex, 1] + 1 + RING))
                            pe.wait_ge(taken, g * e + (ex + 1))
                            for r in range(GT):
                                last = nc.tensor.matmul(core.psum[6 + ex % 2][:, r * P:(r + 1) * P],
                                                        hid[:, ex % 2, 1, r * P:(r + 1) * P],
                                                        w3[:, ex, :], start=True, stop=True)
                            last.then_inc(down_done, 1)

            @block.scalar
            def _(act):
                act.sem_inc(hidden, RING)
                with act.Fori(0, G) as g:
                    for n, (ex, level) in enumerate(order):
                        act.wait_ge(sums, g * U + (n + 1))
                        if level == 1:
                            act.wait_ge(down_done, g * e + (ex + 1))
                        nc.scalar.activation(hid[:, ex % 2, level, :], core.psum[n % RING][:, :], ACT.Relu,
                                             bias=(b1, b2)[level][:, ex:ex + 1]).then_inc(hidden, 1)

            @block.vector
            def _(dve):
                dve.sem_inc(taken, 2)
                with dve.Fori(0, G) as g:
                    for ex in range(e):
                        dve.wait_ge(down_done, g * e + (ex + 3))
                        add_expert(core, dve, core.psum[6 + ex % 2], gates, g, ex, b3[:, ex, :], yb, taken, x)
                    dve.drain()


def experts_swiglu(core, e, chunks, w1, w3, w2, gates, tag):
    nc, x = core.nc, core.x
    C = len(chunks)
    RING = C
    U = e * C
    with ExitStack() as own:
        def sb(name, shape):
            return own.enter_context(nc.sbuf_tensor(f"{tag}_{name}", shape, FP32))
        sil = sb("sil", [P, C, GW])
        hid = sb("hid", [P, 2, C, GW])
        sums = core.sem(tag + "hidden_sums")
        silued = core.sem(tag + "silu_ready")
        hidden = core.sem(tag + "hidden_ready")
        down_done = core.sem(tag + "down_done")
        taken = core.sem(tag + "y_taken")
        with nc.Block() as block:
            @block.tensor
            def _(pe):
                pe.sem_inc(down_done, 2)
                with pe.Fori(0, G) as g:
                    for s in range(e + 1):
                        if s < e:
                            for c, (lo, m) in enumerate(chunks):
                                n = s * C + c
                                pe.wait_ge(silued, g * U + (n + 1))
                                nc.tensor.matmul(core.psum[c][0:m, :], w1[:, s, lo:lo + m],
                                                 core.xT[:, ds(g * GW, GW)], start=True, stop=True)
                                pe.wait_ge(hidden, g * U + (n + 1))
                                nc.tensor.matmul(core.psum[C + c][0:m, :], w3[:, s, lo:lo + m],
                                                 core.xT[:, ds(g * GW, GW)], start=True,
                                                 stop=True).then_inc(sums, 1)
                        if s >= 1:
                            ex = s - 1
                            pe.wait_ge(hidden, g * U + ((ex + 1) * C + RING))
                            pe.wait_ge(taken, g * e + (ex + 1))
                            for r in range(GT):
                                for c, (lo, m) in enumerate(chunks):
                                    last = nc.tensor.matmul(core.psum[6 + ex % 2][:, r * P:(r + 1) * P],
                                                            hid[0:m, ex % 2, c, r * P:(r + 1) * P],
                                                            w2[0:m, ex, c, :], start=(c == 0), stop=(c == C - 1))
                            last.then_inc(down_done, 1)

            @block.scalar
            def _(act):
                act.sem_inc(silued, RING)
                with act.Fori(0, G) as g:
                    for n in range(U):
                        c, m = n % C, chunks[n % C][1]
                        act.wait_ge(sums, g * U + (n + 1))
                        act.wait_ge(hidden, g * U + (n + 1))
                        nc.scalar.activation(sil[0:m, c, :], core.psum[c][0:m, :],
                                             ACT.Silu).then_inc(silued, 1)

            @block.vector
            def _(dve):
                dve.sem_inc(taken, 2)
                dve.sem_inc(hidden, RING)
                with dve.Fori(0, G) as g:
                    for s in range(e + 1):
                        if s < e:
                            dve.wait_ge(down_done, g * e + (s + 1))
                            for c, (lo, m) in enumerate(chunks):
                                dve.wait_ge(silued, g * U + (s * C + c + 1 + RING))
                                nc.vector.tensor_tensor(hid[0:m, s % 2, c, :], sil[0:m, c, :],
                                                        core.psum[C + c][0:m, :], ALU.mult).then_inc(hidden, 1)
                        if s >= 1:
                            ex = s - 1
                            dve.wait_ge(down_done, g * e + (ex + 3))
                            add_expert(core, dve, core.psum[6 + ex % 2], gates, g, ex, None, None, taken, x)


def typed_features_stage(core, w1, w2, b, R, skip, tag):
    nc = core.nc
    K = NODE_K
    KB = GW // D
    NB = K // KB
    with ExitStack() as own:
        def sb(name, shape):
            return own.enter_context(nc.sbuf_tensor(f"{tag}_{name}", shape, FP32))
        xg = sb("xg", [P, GW])
        nodeT = sb("nodeT", [K, GW])
        node = sb("node", [P, GT, K])
        prod = sb("prod", [P, K, D])
        gathered = core.sem(tag + "xg_ready")
        group_done = core.sem(tag + "group_done")
        small = core.sem(tag + "small_ready")
        nodeT_in = core.sem(tag + "nodeT_in")
        node_in = core.sem(tag + "node_in")
        skipped = core.sem(tag + "skip_sums")
        skip_in = core.sem(tag + "skip_in")
        hw_full = core.sem(tag + "hw_full")
        hw_read = core.sem(tag + "hw_read")
        ones = core.sem(tag + "ones")
        with nc.Block() as block:
            @block.gpsimd
            def _(pool):
                nc.gpsimd.memset(R[:, :, D:D + 1], 1.0).then_inc(ones, 1)
                with pool.Fori(0, G) as g:
                    pool.wait_ge(group_done, g + 1)
                    nc.gpsimd.tensor_copy(xg[:, :], core.xT[:, ds(g * GW, GW)]).then_inc(gathered, 1)
                pool.wait_ge(ones, 1)

            @block.tensor
            def _(pe):
                pe.sem_inc(group_done, 1)
                with pe.Fori(0, G) as g:
                    pe.wait_ge(gathered, g + 1)
                    pe.wait_ge(skip_in, g + 1)
                    pe.wait_ge(node_in, g + 1)
                    nc.tensor.matmul(core.psum[4][0:K, :], w1, xg[:, :], start=True, stop=True)
                    for r in range(GT):
                        last = nc.tensor.matmul(core.psum[5][:, r * K:(r + 1) * K], xg[:, r * P:(r + 1) * P],
                                                w1, start=True, stop=True)
                    last.then_inc(small, 1)
                    for r in range(GT):
                        for q in range(NB):
                            pe.wait_ge(hw_read, g * (GT * NB) + (r * NB + q + 1))
                            nc.tensor.matmul(core.psum[q][:, :], xg[:, r * P:(r + 1) * P],
                                             w2[:, q * GW:(q + 1) * GW], start=True,
                                             stop=True).then_inc(hw_full, 1)
                        if r == 0:
                            pe.wait_ge(nodeT_in, g + 1)
                            for rr in range(GT):
                                last = nc.tensor.matmul(core.psum[6][:, rr * P:(rr + 1) * P],
                                                        nodeT[:, rr * P:(rr + 1) * P], b, start=True, stop=True)
                            last.then_inc(skipped, 1)
                    pe.drain().then_inc(group_done, 1)

            @block.scalar
            def _(act):
                act.sem_inc(skip_in, 1)
                with act.Fori(0, G) as g:
                    act.wait_ge(small, g + 1)
                    nc.scalar.activation(nodeT[:, :], core.psum[4][0:K, :], ACT.Copy).then_inc(nodeT_in, 1)
                    act.wait_ge(skipped, g + 1)
                    nc.scalar.activation(skip[:, ds(g * GT, GT), :],
                                         core.psum[6][:, :].rearrange("p (r d) -> p r d", d=D),
                                         ACT.Copy).then_inc(skip_in, 1)

            @block.vector
            def _(dve):
                dve.sem_inc(node_in, 1)
                dve.sem_inc(hw_read, NB)
                with dve.Fori(0, G) as g:
                    dve.drain()
                    dve.wait_ge(small, g + 1)
                    nc.vector.tensor_copy(node[:, :, :], core.psum[5][:, 0:GT * K].rearrange(
                        "p (r k) -> p r k", k=K)).then_inc(node_in, 1)
                    dve.drain()
                    for r in range(GT):
                        for q in range(NB):
                            dve.wait_ge(hw_full, g * (GT * NB) + (r * NB + q + 1))
                            nc.vector.tensor_tensor(
                                prod[:, q * KB:(q + 1) * KB, :],
                                core.psum[q][:, :].rearrange("p (k d) -> p k d", d=D),
                                over(node[:, r, q * KB:(q + 1) * KB], D), ALU.mult).then_inc(hw_read, 1)
                        dve.drain()
                        nc.vector.tensor_reduce(R[:, ds(g * GT + r, 1), 0:D].rearrange("p a d -> p (a d)"),
                                                prod[:, :, :].rearrange("p k d -> p d k"), AX.X, ALU.add)
                        dve.drain()


def adj_product_stage(core, adjT, R, width, finish, tag):
    nc = core.nc
    B = 4
    with ExitStack() as own:
        at = own.enter_context(nc.sbuf_tensor(f"{tag}_at", [P, B, T * P], FP32))
        landed = [core.sem(f"{tag}at_landed{i}") for i in range(B)]
        used = [core.sem(f"{tag}at_used{i}") for i in range(B)]
        out_read = core.sem(tag + "out_read")
        src = adjT.rearrange("t p j i -> p t (j i)")
        with nc.Block() as block:
            @block.sync
            def _(sp):
                with sp.Fori(0, T // B) as it:
                    for q in range(B):
                        sp.wait_ge(used[q], it + 1)
                        sp.dma_start(at[:, q:q + 1, :],
                                     src[:, ds(it * B + q, 1), :]).then_inc(landed[q], 16)

            @block.tensor
            def _(pe):
                for q in range(B):
                    pe.sem_inc(used[q], 1)
                with pe.Fori(0, T // B) as it:
                    for q in range(B):
                        pe.wait_ge(landed[q], it * 16 + 16)
                        pe.wait_ge(out_read, it * B + (q + 1))
                        for j in range(T):
                            last = nc.tensor.matmul(core.psum[q % 2][:, 0:width],
                                                    at[:, q, j * P:(j + 1) * P], R[:, j, 0:width],
                                                    start=(j == 0), stop=(j == T - 1))
                        last.then_inc(used[q], 1)

            @block.vector
            def _(dve):
                dve.sem_inc(out_read, 2)
                with dve.Fori(0, T // B) as it:
                    for q in range(B):
                        dve.wait_ge(used[q], it + 2)
                        finish(dve, it * B + q, core.psum[q % 2], out_read)

def first_graph_layer(core, w):
    nc = core.nc
    with ExitStack() as own:
        R = own.enter_context(nc.sbuf_tensor("l0_R", [P, T, D + 1], FP32))
        skip = own.enter_context(nc.sbuf_tensor("l0_skip", [P, T, D], FP32))
        with ExitStack() as weights:
            w1 = weights.enter_context(nc.sbuf_tensor("l0_w1", [D, NODE_K], FP32))
            w2 = weights.enter_context(nc.sbuf_tensor("l0_w2", [D, NODE_K, D], FP32))
            b = weights.enter_context(nc.sbuf_tensor("l0_b", [NODE_K, D], FP32))
            norm_stage(core, [(w1[:, :], w["L0_gnn_W1"]),
                              (w2[:, :, :], w["L0_gnn_W2"].rearrange("k c f -> c k f")),
                              (b[:, :], w["L0_gnn_b"])], "l0g")
            typed_features_stage(core, w1[:, :], w2[:, :, :].rearrange("c k f -> c (k f)"), b[:, :], R, skip, "l0t")
        tmp = own.enter_context(nc.sbuf_tensor("l0_sum", [P, 1, D], FP32))

        def finish(dve, t, bank, out_read):
            nc.vector.tensor_tensor(tmp[:, :, :], bank[:, 0:D].unsqueeze(1), skip[:, ds(t, 1), :], ALU.add)
            nc.vector.tensor_scalar(core.deg[:, ds(t, 1)], bank[:, D:D + 1], 1.0, None,
                                    ALU.add).then_inc(out_read, 1)
            dve.drain()
            row = core.x[:, ds(t, 1), :]
            nc.vector.scalar_tensor_tensor(row, tmp[:, :, :], 0.0, row, ALU.max, ALU.add)
            dve.drain()

        adj_product_stage(core, w["adjT"], R, D + 1, finish, "l0a")


def first_expert_layer(core, w):
    nc = core.nc
    E, H = 8, 256
    with ExitStack() as own:
        def sb(name, shape):
            return own.enter_context(nc.sbuf_tensor("l0f_" + name, shape, FP32))
        wg, bg = sb("wg", [D, E]), sb("bg", [P, E])
        w1, b1 = sb("w1", [D, E, H]), sb("b1", [P, E, 2])
        w2, b2 = sb("w2", [P, E, 2, D]), sb("b2", [P, E, D])
        score, gates = sb("score", [P, T, E]), sb("gates", [P, T, E])
        norm_stage(core, [(wg[:, :], w["L0_ffn_Wg"]), (bg[:, :], w["L0_ffn_bg"].partition_broadcast(P)),
                          (w1[:, :, :], w["L0_ffn_W1"].rearrange("e d h -> d e h")),
                          (b1[:, :, :], w["L0_ffn_b1"]),
                          (w2[:, :, :, :], w["L0_ffn_W2"].rearrange("e (c h) d -> h e c d", h=P)),
                          (b2[:, :, :].rearrange("p e d -> p (e d)"),
                           w["L0_ffn_b2"].rearrange("e d -> (e d)").partition_broadcast(P))],
                   "l0n", (wg[:, :], bg[:, :], score[:, :, :]))
        gates_onehot(core, score, E, gates, "l0gate")
        experts_gelu(core, E, w1, b1, w2, b2, gates, "l0e")


def third_expert_layer(core, w):
    nc = core.nc
    E, RH = 6, 64
    with ExitStack() as own:
        def sb(name, shape):
            return own.enter_context(nc.sbuf_tensor("l2f_" + name, shape, FP32))
        rw1, rb1, rw2, rb2 = sb("rw1", [D, RH]), sb("rb1", [RH, 1]), sb("rw2", [RH, E]), sb("rb2", [P, E])
        w1, w2, w3 = sb("w1", [D, E, D]), sb("w2", [D, E, D]), sb("w3", [D, E, D])
        b1, b2, b3 = sb("b1", [P, E]), sb("b2", [P, E]), sb("b3", [P, E, D])
        score, gates = sb("score", [P, T, E]), sb("gates", [P, T, E])
        rh = sb("rh", [RH, N])
        norm_stage(core, [(rw1[:, :], w["L2_ffn_router_w1"]), (rb1[:, :], w["L2_ffn_router_b1"].unsqueeze(1)),
                          (rw2[:, :], w["L2_ffn_router_w2"]), (rb2[:, :], w["L2_ffn_router_b2"].partition_broadcast(P)),
                          (w1[:, :, :], w["L2_ffn_expert_w1"].rearrange("e d h -> d e h")),
                          (w2[:, :, :], w["L2_ffn_expert_w2"].rearrange("e d h -> d e h")),
                          (w3[:, :, :], w["L2_ffn_expert_w3"].rearrange("e d h -> d e h")),
                          (b1[:, :], w["L2_ffn_expert_b1"]), (b2[:, :], w["L2_ffn_expert_b2"]),
                          (b3[:, :, :].rearrange("p e d -> p (e d)"),
                           w["L2_ffn_expert_b3"].rearrange("e d -> (e d)").partition_broadcast(P))], "l2n")
        sums, hidden, scored = core.sem("router_sums"), core.sem("router_hidden"), core.sem("router_scores")
        with nc.Block() as block:
            @block.tensor
            def _(pe):
                for g in range(G):
                    if g >= 4:
                        pe.wait_ge(hidden, g - 3)
                    nc.tensor.matmul(core.psum[g % 4][0:RH, :], rw1[:, :], core.xT[:, g * GW:(g + 1) * GW],
                                     start=True, stop=True).then_inc(sums, 1)
                pe.wait_ge(hidden, G)
                for t in range(T):
                    last = nc.tensor.matmul(core.psum[6][:, t * E:(t + 1) * E], rh[:, t * P:(t + 1) * P],
                                            rw2[:, :], start=True, stop=True)
                last.then_inc(scored, 1)

            @block.scalar
            def _(act):
                for g in range(G):
                    act.wait_ge(sums, g + 1)
                    nc.scalar.activation(rh[:, g * GW:(g + 1) * GW], core.psum[g % 4][0:RH, :], ACT.Relu,
                                         bias=rb1[:, 0:1]).then_inc(hidden, 1)

            @block.vector
            def _(dve):
                dve.wait_ge(scored, 1)
                nc.vector.tensor_tensor(score[:, :, :], core.psum[6][:, 0:T * E].rearrange("p (t e) -> p t e", e=E),
                                        rows(rb2[:, :], T), ALU.add)
        gates_softmax(core, score, E, gates, False, "l2gate")
        experts_deep(core, E, w1, b1, w2, b2, w3, b3, gates, "l2e")


def fourth_expert_layer(core, w):
    nc = core.nc
    E, H = 8, 341
    chunks = [(lo, min(P, H - lo)) for lo in range(0, H, P)]
    with ExitStack() as own:
        def sb(name, shape):
            return own.enter_context(nc.sbuf_tensor("l3f_" + name, shape, FP32))
        rw = sb("rw", [D, E])
        w1, w3 = sb("w1", [D, E, H]), sb("w3", [D, E, H])
        w2 = sb("w2", [P, E, len(chunks), D])
        score, gates = sb("score", [P, T, E]), sb("gates", [P, T, E])
        norm_stage(core, [(rw[:, :], w["L3_ffn_router_w"]),
                          (w1[:, :, :], w["L3_ffn_w1"]), (w3[:, :, :], w["L3_ffn_w3"])] +
                   [(w2[0:m, :, c, :], w["L3_ffn_w2"][lo:lo + m, :, :]) for c, (lo, m) in enumerate(chunks)],
                   "l3n", (rw[:, :], None, score[:, :, :]))
        gates_softmax(core, score, E, gates, True, "l3gate")
        experts_swiglu(core, E, chunks, w1, w3, w2, gates, "l3e")


def fourth_graph_layer(core, w):
    nc = core.nc
    with ExitStack() as own:
        def sb(name, shape):
            return own.enter_context(nc.sbuf_tensor("l3g_" + name, shape, FP32))
        R, w_, b = sb("R", [P, T, D]), sb("w", [D, D]), sb("b", [P, D])
        dinv, live, tmp = sb("dinv", [P, T]), sb("live", [P, T]), sb("tmp", [P, 1, D])
        norm_stage(core, [(w_[:, :], w["L3_gnn_W"]), (b[:, :], w["L3_gnn_b"].partition_broadcast(P))], "l3g")
        safe, rooted = core.sem("deg_safe"), core.sem("deg_rooted")
        made, taken = core.sem("support_made"), core.sem("support_taken")
        with nc.Block() as block:
            @block.tensor
            def _(pe):
                for g in range(G):
                    if g >= 4:
                        pe.wait_ge(taken, g - 3)
                    for r in range(GT):
                        t = g * GT + r
                        last = nc.tensor.matmul(core.psum[g % 4][:, r * P:(r + 1) * P],
                                                core.xT[:, t * P:(t + 1) * P], w_[:, :], start=True, stop=True)
                    last.then_inc(made, 1)

            @block.vector
            def _(dve):
                nc.vector.tensor_scalar(live[:, :], core.deg[:, :], 0.0, None, ALU.not_equal)
                dve.drain()
                nc.vector.scalar_tensor_tensor(dinv[:, :], live[:, :], -1.0, core.deg[:, :], ALU.mult, ALU.add)
                dve.drain()
                nc.vector.tensor_scalar(dinv[:, :], dinv[:, :], 1.0, None, ALU.add).then_inc(safe, 1)
                dve.wait_ge(rooted, 1)
                nc.vector.reciprocal(dinv[:, :], dinv[:, :])
                dve.drain()
                nc.vector.tensor_tensor(dinv[:, :], dinv[:, :], live[:, :], ALU.mult)
                dve.drain()
                for g in range(G):
                    a = slice(g * GT, (g + 1) * GT)
                    dve.wait_ge(made, g + 1)
                    nc.vector.tensor_tensor(R[:, a, :], core.psum[g % 4][:, :].rearrange("p (r d) -> p r d", d=D),
                                            rows(b[:, :], GT), ALU.add).then_inc(taken, 1)
                    dve.drain()
                    nc.vector.tensor_tensor(R[:, a, :], R[:, a, :], over(dinv[:, a], D), ALU.mult)

            @block.scalar
            def _(act):
                act.wait_ge(safe, 1)
                nc.scalar.activation(dinv[:, :], dinv[:, :], ACT.Sqrt).then_inc(rooted, 1)

        def finish(dve, t, bank, out_read):
            nc.vector.tensor_tensor(tmp[:, :, :], bank[:, 0:D].unsqueeze(1), R[:, ds(t, 1), :],
                                    ALU.add).then_inc(out_read, 1)
            dve.drain()
            row = core.x[:, ds(t, 1), :]
            nc.vector.scalar_tensor_tensor(row, tmp[:, :, :], dinv[:, ds(t, 1)], row, ALU.mult, ALU.add)
            dve.drain()

        adj_product_stage(core, w["adjT"], R, D, finish, "l3a")

def row_attention_stage(core, kind, adj, row, own, R, tag):
    nc = core.nc
    leaky = kind == "leaky"
    AB, LB, NB, LAG, BANKS = 4, 2, T // GT, 2, 4
    with ExitStack() as mine:
        def sb(name, shape):
            return mine.enter_context(nc.sbuf_tensor(f"{tag}_{name}", shape, FP32))
        A, L, PT = sb("A", [P, AB, N]), sb("L", [P, LB, N]), sb("PT", [P, NB, GW])
        top, c1, c2 = sb("top", [P, AB]), sb("c1", [P, AB]), sb("c2", [P, AB])
        den = sb("den", [P, 2])
        landed = [core.sem(f"{tag}landed{i}") for i in range(AB)]
        a_used = [core.sem(f"{tag}a_used{i}") for i in range(AB)]
        masked = core.sem(tag + "masked")
        b_done = core.sem(tag + "b_done")
        l_ready = core.sem(tag + "l_ready")
        l_free = core.sem(tag + "l_free")
        turned = core.sem(tag + "turned")
        copied = core.sem(tag + "copied")
        used = core.sem(tag + "used")
        out_full = core.sem(tag + "out_full")
        out_read = core.sem(tag + "out_read")
        src = adj.rearrange("(t p) j -> p t j", p=P)
        with nc.Block() as block:
            @block.sync
            def _(sp):
                with sp.Fori(0, T // AB) as it:
                    for q in range(AB):
                        sp.wait_ge(a_used[q], it + 1)
                        sp.dma_start(A[:, q:q + 1, :], src[:, ds(it * AB + q, 1), :]).then_inc(landed[q], 16)

            @block.vector
            def _(dve):
                for q in range(AB):
                    dve.sem_inc(a_used[q], 1)
                dve.sem_inc(out_read, 2)

                def stage_a(it, q):
                    t, l = it * AB + q, q % LB
                    a = A[:, q, :]
                    dve.wait_ge(landed[q], it * 16 + 16)
                    if leaky:
                        diag = A[:, q:q + 1, ds(t * P, P)]
                        nc.vector.tensor_tensor(diag, diag, core.ident[:, :].unsqueeze(1), ALU.max)
                        dve.drain()
                        nc.vector.tensor_scalar(a, a, 0.0, -BIG, ALU.is_le, ALU.mult)
                        dve.drain()
                        nc.vector.tensor_tensor_reduce(a, a, row[:, :], 1.0, -3.0 * BIG, ALU.add, ALU.max,
                                                       top[:, q:q + 1])
                        dve.drain()
                        nc.vector.tensor_tensor(top[:, q:q + 1], top[:, q:q + 1], own[:, ds(t, 1)], ALU.add)
                        dve.drain()
                        nc.vector.scalar_tensor_tensor(c1[:, q:q + 1], top[:, q:q + 1], 0.2, top[:, q:q + 1],
                                                       ALU.mult, ALU.max)
                        dve.drain()
                        nc.vector.scalar_tensor_tensor(c2[:, q:q + 1], own[:, ds(t, 1)], 0.2, c1[:, q:q + 1],
                                                       ALU.mult, ALU.subtract)
                        dve.drain()
                        nc.vector.tensor_tensor(c1[:, q:q + 1], own[:, ds(t, 1)], c1[:, q:q + 1],
                                                ALU.subtract).then_inc(masked, 1)
                    else:
                        dve.wait_ge(l_free, t + 1)
                        nc.vector.tensor_scalar(L[:, l, :], a, 0.0, -BIG, ALU.is_equal, ALU.mult)
                        dve.drain()
                        nc.vector.tensor_tensor(a, a, row[:, :], ALU.mult)
                        dve.drain()
                        nc.vector.tensor_tensor_reduce(L[:, l, :], a, L[:, l, :], 1.0, -3.0 * BIG, ALU.add,
                                                       ALU.max, top[:, q:q + 1])
                        dve.drain()
                        nc.vector.tensor_scalar(c1[:, q:q + 1], top[:, q:q + 1], -0.1 * BIG, -1.0, ALU.max,
                                                ALU.mult).then_inc(masked, 1)
                        dve.sem_inc(a_used[q], 1)

                def stage_c(it, q):
                    t, l = it * AB + q, q % LB
                    dve.wait_ge(b_done, t + 1)
                    nc.vector.scalar_tensor_tensor(L[:, l, :], A[:, q, :], c1[:, q:q + 1], L[:, l, :],
                                                   ALU.add, ALU.max).then_inc(l_ready, 1)
                    dve.drain().then_inc(a_used[q], 1)

                def stage_o(t, parity):
                    bank, d = core.psum[6 + parity], den[:, parity:parity + 1]
                    dve.wait_ge(out_full, t + 1)
                    if leaky:
                        nc.vector.reciprocal(d, bank[:, D:D + 1])
                    else:
                        nc.vector.tensor_scalar(d, bank[:, D:D + 1], 0.0, None, ALU.is_le)
                        dve.drain()
                        nc.vector.tensor_tensor(d, d, bank[:, D:D + 1], ALU.add)
                        dve.drain()
                        nc.vector.reciprocal(d, d)
                    dve.drain()
                    xt = core.x[:, ds(t, 1), :]
                    nc.vector.scalar_tensor_tensor(xt, bank[:, 0:D].unsqueeze(1), d, xt, ALU.mult,
                                                   ALU.add).then_inc(out_read, 1)
                    dve.drain()

                def tiles(it, first, last):
                    for q in range(AB):
                        t = it * AB + q
                        if not (last and q == AB - 1):
                            stage_a(it if q < AB - 1 else it + 1, (q + 1) % AB)
                        if leaky:
                            stage_c(it, q)
                        if not (first and q < 2):
                            stage_o(t - 2, q % 2)

                stage_a(0, 0)
                tiles(0, True, False)
                with dve.Fori(1, T // AB - 1) as it:
                    tiles(it, False, False)
                tiles(T // AB - 1, False, True)
                for t in (T - 2, T - 1):
                    stage_o(t, t % 2)

            @block.scalar
            def _(act):
                act.sem_inc(copied, BANKS)

                def stage_b(it, q):
                    t, l = it * AB + q, q % LB
                    act.wait_ge(masked, t + 1)
                    if leaky:
                        act.wait_ge(l_free, t + 1)
                        nc.scalar.activation(L[:, l, :], A[:, q, :], ACT.Identity, bias=c2[:, q:q + 1],
                                             scale=0.2).then_inc(b_done, 1)
                    else:
                        nc.scalar.activation(L[:, l, :], L[:, l, :], ACT.Exp,
                                             bias=c1[:, q:q + 1]).then_inc(b_done, 1)

                def tiles(it, last):
                    for q in range(AB):
                        if not (last and q == AB - 1):
                            stage_b(it if q < AB - 1 else it + 1, (q + 1) % AB)
                        for b in range(NB):
                            n = (it * AB + q) * NB + b
                            act.wait_ge(turned, n + 1)
                            act.wait_ge(used, n + 1)
                            nc.scalar.activation(PT[:, b, :], core.psum[b % BANKS][:, :],
                                                 ACT.Exp if leaky else ACT.Copy).then_inc(copied, 1)

                stage_b(0, 0)
                with act.Fori(0, T // AB - 1) as it:
                    tiles(it, False)
                tiles(T // AB - 1, True)

            @block.tensor
            def _(pe):
                pe.sem_inc(l_free, LB)
                pe.sem_inc(used, NB)
                with pe.Fori(0, T // AB) as it:
                    steps = [(q, b) for q in range(AB) for b in range(NB)]
                    for s in range(len(steps) + LAG):
                        if s < len(steps):
                            q, b = steps[s]
                            t = it * AB + q
                            if b == 0:
                                pe.wait_ge(l_ready if leaky else b_done, t + 1)
                            pe.wait_ge(copied, t * NB + (b + 1))
                            for r in range(GT):
                                j = b * GT + r
                                last = nc.tensor.transpose(core.psum[b % BANKS][:, r * P:(r + 1) * P],
                                                           L[:, q % LB, j * P:(j + 1) * P], core.ident[:, :])
                            last.then_inc(turned, 1)
                            if b == NB - 1:
                                pe.wait_ge(turned, t * NB + NB)
                                pe.sem_inc(l_free, 1)
                        if s >= LAG:
                            q, b = steps[s - LAG]
                            t = it * AB + q
                            if b == 0:
                                pe.wait_ge(out_read, t + 1)
                            pe.wait_ge(copied, t * NB + (b + 1 + BANKS))
                            for r in range(GT):
                                j = b * GT + r
                                last = nc.tensor.matmul(core.psum[6 + q % 2][:, 0:D + 1],
                                                        PT[:, b, r * P:(r + 1) * P], R[:, j, :],
                                                        start=(j == 0), stop=(j == T - 1))
                            last.then_inc(used, 1)
                            if b == NB - 1:
                                pe.wait_ge(used, t * NB + 2 * NB)
                                pe.sem_inc(out_full, 1)


def replicate(nc, dve, rep, col):
    nc.vector.memset(rep, 1.0)
    dve.drain()
    nc.vector.tensor_scalar(rep, rep, col, None, ALU.mult)


def second_graph_layer(core, w):
    nc = core.nc
    with ExitStack() as mine:
        def sb(name, shape):
            return mine.enter_context(nc.sbuf_tensor("l1g_" + name, shape, FP32))
        R, own = sb("R", [P, T, D + 1]), sb("own", [P, T])
        with ExitStack() as inner:
            def sbi(name, shape):
                return inner.enter_context(nc.sbuf_tensor("l1g_" + name, shape, FP32))
            w_, a, rep, WhT = sbi("w", [D, D]), sbi("a", [D, 2]), sbi("rep", [D, P]), sbi("WhT", [P, 2, GW])
            norm_stage(core, [(w_[:, :], w["L1_gnn_W"]), (a[:, :], w["L1_gnn_a"])], "l1g")
            made, taken, whT_in = core.sem("wh_made"), core.sem("wh_taken"), core.sem("whT_in")
            dst_made, dst_in, rep_ready = core.sem("dst_made"), core.sem("dst_in"), core.sem("rep_ready")
            with nc.Block() as block:
                @block.gpsimd
                def _(pool):
                    nc.gpsimd.memset(R[:, :, D:D + 1], 1.0)

                @block.tensor
                def _(pe):
                    pe.wait_ge(rep_ready, 1)
                    for g in range(G):
                        cols = core.xT[:, g * GW:(g + 1) * GW]
                        if g >= 2:
                            pe.wait_ge(taken, g - 1)
                            pe.wait_ge(whT_in, g - 1)
                            pe.wait_ge(dst_in, g - 1)
                        for r in range(GT):
                            nc.tensor.matmul(core.psum[g % 2][:, r * P:(r + 1) * P],
                                             core.xT[:, (g * GT + r) * P:(g * GT + r + 1) * P], w_[:, :],
                                             start=True, stop=True)
                        nc.tensor.matmul(core.psum[2 + g % 2][:, :], w_[:, :], cols, start=True,
                                         stop=True).then_inc(made, 1)
                        pe.wait_ge(whT_in, g + 1)
                        for r in range(GT):
                            nc.tensor.matmul(core.psum[6][:, g * GT + r:g * GT + r + 1],
                                             WhT[:, g % 2, r * P:(r + 1) * P], a[:, 0:1], start=True, stop=True)
                        nc.tensor.matmul(core.psum[4 + g % 2][:, :], rep[:, :], WhT[:, g % 2, :], start=True,
                                         stop=True).then_inc(dst_made, 1)

                @block.scalar
                def _(act):
                    for g in range(G):
                        act.wait_ge(made, g + 1)
                        if g >= 2:
                            act.wait_ge(dst_made, g - 1)
                        nc.scalar.activation(WhT[:, g % 2, :], core.psum[2 + g % 2][:, :],
                                             ACT.Copy).then_inc(whT_in, 1)
                        act.wait_ge(dst_made, g + 1)
                        nc.scalar.activation(core.xT[:, g * GW:(g + 1) * GW], core.psum[4 + g % 2][:, :],
                                             ACT.Copy).then_inc(dst_in, 1)

                @block.vector
                def _(dve):
                    replicate(nc, dve, rep[:, :], a[:, 1:2])
                    dve.drain().then_inc(rep_ready, 1)
                    for g in range(G):
                        dve.wait_ge(made, g + 1)
                        nc.vector.tensor_copy(R[:, g * GT:(g + 1) * GT, 0:D],
                                              core.psum[g % 2][:, :].rearrange("p (r d) -> p r d", d=D)).then_inc(taken, 1)
                    dve.wait_ge(dst_made, G)
                    nc.vector.tensor_copy(own[:, :], core.psum[6][:, 0:T])
        row_attention_stage(core, "leaky", w["adj"], core.xT, own, R, "l1a")


def third_graph_layer(core, w):
    nc = core.nc
    with ExitStack() as mine:
        R = mine.enter_context(nc.sbuf_tensor("l2g_R", [P, T, D + 1], FP32))
        with ExitStack() as inner:
            hv = inner.enter_context(nc.sbuf_tensor("l2g_hv", [D, 1], FP32))
            rep = inner.enter_context(nc.sbuf_tensor("l2g_rep", [D, P], FP32))
            norm_stage(core, [(hv[:, :], w["L2_gnn_H_v"])], "l2g")
            made, row_in, rep_ready = core.sem("row_made"), core.sem("row_in"), core.sem("rep_ready")
            with nc.Block() as block:
                @block.gpsimd
                def _(pool):
                    nc.gpsimd.memset(R[:, :, D:D + 1], 1.0)

                @block.tensor
                def _(pe):
                    pe.wait_ge(rep_ready, 1)
                    for g in range(G):
                        if g >= 4:
                            pe.wait_ge(row_in, g - 3)
                        nc.tensor.matmul(core.psum[g % 4][:, :], rep[:, :], core.xT[:, g * GW:(g + 1) * GW],
                                         start=True, stop=True).then_inc(made, 1)

                @block.scalar
                def _(act):
                    for g in range(G):
                        act.wait_ge(made, g + 1)
                        nc.scalar.activation(core.xT[:, g * GW:(g + 1) * GW], core.psum[g % 4][:, :],
                                             ACT.Copy).then_inc(row_in, 1)

                @block.vector
                def _(dve):
                    replicate(nc, dve, rep[:, :], hv[:, 0:1])
                    dve.drain().then_inc(rep_ready, 1)
                    nc.vector.tensor_copy(R[:, :, 0:D], core.xn[:, :, :])
        row_attention_stage(core, "scaled", w["adj"], core.xT, None, R, "l2a")

HEADS, QS, HD = 4, 4, 32
ROOT = float(HD) ** 0.5
STACK = 3 * HD
EPS_HEAD = 1e-8
MASKED, MASK_UNIT = -60000.0, 64.0


def norm_rows(nc, dve, src, out, sq, mean, var, width, eps, var_ready, std_ready, turn):
    nc.vector.tensor_reduce(mean, src, AX.X, ALU.add)
    dve.drain()
    nc.vector.tensor_scalar(mean, mean, 1.0 / width, None, ALU.mult)
    dve.drain()
    nc.vector.tensor_tensor(out, src, over(mean, width), ALU.subtract)
    dve.drain()
    nc.vector.tensor_tensor(sq, out, out, ALU.mult)
    dve.drain()
    nc.vector.tensor_reduce(var, sq, AX.X, ALU.add)
    dve.drain()
    nc.vector.tensor_scalar(var, var, 1.0 / width, eps, ALU.mult, ALU.add).then_inc(var_ready, 1)
    dve.wait_ge(std_ready, turn)
    nc.vector.reciprocal(var, var)
    dve.drain()
    nc.vector.tensor_tensor(out, out, over(var, width), ALU.mult)
    dve.drain()


def softmax_rows(nc, dve, src, stat, shifted, exped, turn):
    nc.vector.tensor_reduce(stat, src, AX.X, ALU.max)
    dve.drain()
    nc.vector.tensor_tensor(src, src, over(stat, 4), ALU.subtract).then_inc(shifted, 1)
    dve.wait_ge(exped, turn)
    nc.vector.tensor_reduce(stat, src, AX.X, ALU.add)
    dve.drain()
    nc.vector.reciprocal(stat, stat)
    dve.drain()
    nc.vector.tensor_tensor(src, src, over(stat, 4), ALU.mult)
    dve.drain()


class HeadTiles:

    def __init__(self, core, own):
        nc = core.nc

        def sb(name, shape, dt=FP32):
            return own.enter_context(nc.sbuf_tensor("l1f_" + name, shape, dt))
        self.hlw, self.hlb = sb("hlw", [D, HEADS, HD]), sb("hlb", [HD, HEADS])
        self.wq, self.wk, self.wv = sb("wq", [HD, HEADS, QS, HD]), sb("wk", [HD, HEADS, HD]), sb("wv", [HD, HEADS, HD])
        self.gw, self.gb = sb("gw", [P, HEADS, QS]), sb("gb", [P, HEADS, QS])
        self.lng, self.lnb = sb("lng", [P, HD]), sb("lnb", [P, HD])
        self.hlw_n, self.hlb_n = sb("hlw_n", [D, HD]), sb("hlb_n", [HD, 1])
        self.wq_n, self.wk_n, self.wvi_n = sb("wq_n", [HD, QS, 3, HD]), sb("wk_n", [HD, 3, HD]), sb("wvi_n", [HD, 2 * HD])
        self.sxT = sb("sxT", [HD, 2, GW])
        self.qT = sb("qT", [STACK + 3, QS, N], FP16)
        self.kT = sb("kT", [STACK + 3, N], FP16)
        self.V = sb("V", [P, T, HD + 1])
        self.sx = sb("sx", [P, T, HD])
        self.PT = sb("PT", [P, 4, 2, GW])
        self.pm, self.nm, self.nd = sb("pm", [P, GT, G]), sb("nm", [P, GT]), sb("nd", [P, GT])
        self.m3 = sb("m3", [P, 2, GT, 3], FP16)
        self.rec = sb("rec", [P, GT])
        self.at = core.xn
        self.atT = sb("atT", [P, 2, GW])
        self.gs, self.stat = sb("gs", [P, T, QS]), sb("stat", [P, T])
        self.mean, self.var = sb("mean", [P, T]), sb("var", [P, T])
        self.hn, self.tmp = sb("hn", [P, T, HD]), sb("tmp", [P, T, HD])
        self.fx = sb("fx", [P, T, D])
        self.tri, self.triT = sb("tri", [P, P], FP16), sb("triT", [P, P], FP16)
        self.unit = sb("unit", [P, P], FP16)


def attention_constants(core, h):
    nc = core.nc
    filled = core.sem("mask_filled")
    with nc.Block() as block:
        @block.gpsimd
        def _(pool):
            nc.gpsimd.memset(h.tri[:, :], 0.0).then_inc(filled, 1)
            nc.gpsimd.memset(h.triT[:, :], 0.0).then_inc(filled, 1)
            nc.gpsimd.memset(h.unit[:, :], 0.0).then_inc(filled, 1)
            nc.gpsimd.memset(h.V[:, :, HD:HD + 1], 1.0).then_inc(filled, 1)
            pool.wait_ge(filled, 4)
            nc.gpsimd.memset(h.kT[STACK:STACK + 3, :], 1.0).then_inc(filled, 1)
            pool.wait_ge(filled, 5)
            nc.gpsimd.affine_select(out=h.tri[:, :], in_=h.tri[:, :], compare_op=ALU.is_ge, fill=MASKED,
                                    base=0, pattern=[[-1, P]], channel_multiplier=1)
            nc.gpsimd.affine_select(out=h.triT[:, :], in_=h.triT[:, :], compare_op=ALU.is_ge, fill=MASKED,
                                    base=0, pattern=[[1, P]], channel_multiplier=-1)
            nc.gpsimd.affine_select(out=h.unit[:, :], in_=h.unit[:, :], compare_op=ALU.not_equal, fill=MASK_UNIT,
                                    base=0, pattern=[[-1, P]], channel_multiplier=1)


class Schedule:

    def __init__(self):
        self.events = []
        blocks = {sg: [("M", sg, r, c) for r in range(GT) for c in range(sg + 1)] for sg in range(G)}
        self.events += blocks[0] + [("T", 0)] + blocks[1]
        for sg in range(G):
            pairs = 2 * sg + 2
            ahead = list(blocks.get(sg + 2, []))
            rest = ahead[:]
            for p in range(pairs):
                self.events.append(("E", sg, p))
                if p == 1 and sg + 1 < G:
                    self.events.append(("T", sg + 1))
                if p >= 1:
                    k = -(-len(rest) // (pairs - p))
                    self.events += rest[:k]
                    rest = rest[k:]
        self.closing, group = {}, -1
        for at, ev in enumerate(self.events):
            if ev[0] == "E" and ev[1] != group:
                if group >= 0:
                    self.closing[at - 1] = group
                group = ev[1]
        self.closing[len(self.events) - 1] = group
        self.m_blocks = sum(1 for ev in self.events if ev[0] == "M")
        self.pairs = sum(1 for ev in self.events if ev[0] == "E")


def heads_stage(core, h):
    nc = core.nc
    sch = Schedule()
    NM, NE = sch.m_blocks, sch.pairs
    MB = (4, 5, 6)
    U = G * (QS + 1)
    s = {n: core.sem("l1h_" + n) for n in
         ("w_ready", "sx_sums", "sx_in", "qk_sums", "qk_high", "qk_split", "v_sums", "v_in", "m_full", "m_read",
          "m3_ready", "mt_full", "mt_read", "s_full", "exped", "pv_done", "po_full", "po_read", "at_ready",
          "at_turned", "at_copied", "gate_sums", "shifted", "gs_exp", "var_ready", "std_ready", "proj_done")}

    with nc.Block() as block:
        @block.tensor
        def _(pe):
            pe.sem_inc(s["pv_done"], 4)
            with pe.Fori(0, HEADS) as n:
                pe.wait_ge(s["w_ready"], n + 1)
                for g in range(G):
                    if g >= 2:
                        pe.wait_ge(s["sx_in"], n * G + (g - 1))
                    nc.tensor.matmul(core.psum[4 + g % 2][0:HD, :], h.hlw_n[:, :], core.xT[:, g * GW:(g + 1) * GW],
                                     start=True, stop=True).then_inc(s["sx_sums"], 1)
                    pe.wait_ge(s["sx_in"], n * G + (g + 1))
                    for e in range(QS + 1):
                        u = g * (QS + 1) + e
                        if u >= 4:
                            pe.wait_ge(s["qk_split"], n * U + (u - 3))
                        lhsT = (h.wq_n[:, e, :, :] if e < QS else h.wk_n[:, :, :]).rearrange("d k o -> d (k o)")
                        nc.tensor.matmul(core.psum[u % 4][0:STACK, :], lhsT, h.sxT[:, g % 2, :],
                                         start=True, stop=True).then_inc(s["qk_sums"], 1)
                    if g >= 2:
                        pe.wait_ge(s["v_in"], n * G + (g - 1))
                    for r in range(GT):
                        last = nc.tensor.matmul(core.psum[6 + g % 2][:, r * 2 * HD:(r + 1) * 2 * HD],
                                                h.sxT[:, g % 2, r * P:(r + 1) * P], h.wvi_n[:, :],
                                                start=True, stop=True)
                    last.then_inc(s["v_sums"], 1)

                with pe.Fori(0, QS) as e:
                    it = n * QS + e
                    pe.wait_ge(s["qk_split"], n * U + U)
                    pe.wait_ge(s["v_in"], n * G + G)
                    turn, users, mcount, tcount, ecount, pending = 0, [], 0, 0, 0, []

                    def ring_wait():
                        nonlocal turn
                        if turn < len(MB):
                            pe.wait_ge(s["m_read"], it * NM + 1)
                            pe.wait_ge(s["mt_read"], it * G + 1)
                        else:
                            kind, count = users[turn - len(MB)]
                            if kind == "M":
                                pe.wait_ge(s["m_read"], it * NM + (count + 1))
                            else:
                                pe.wait_ge(s["mt_read"], it * G + (count + 1))
                        bank = core.psum[MB[turn % len(MB)]]
                        turn += 1
                        return bank

                    def attend(sg, p, k):
                        slot = k % 4
                        pe.wait_ge(s["exped"], it * NE + (k + 3))
                        if p == 0:
                            pe.wait_ge(s["po_read"], it * G + (sg + 1))
                        for jj in range(2):
                            j = 2 * p + jj
                            for r in range(max(0, j - GT * sg), GT):
                                last = nc.tensor.matmul(
                                    core.psum[7][:, r * (HD + 1):(r + 1) * (HD + 1)],
                                    h.PT[:, slot, jj, r * P:(r + 1) * P], h.V[:, j, :],
                                    start=(j == 0 and r == 0), stop=(j == GT * sg + r), skip_group_check=True)
                        last.then_inc(s["pv_done"], 1)
                        if p == 2 * sg + 1:
                            pe.wait_ge(s["pv_done"], it * NE + (k + 5))
                            pe.sem_inc(s["po_full"], 1)

                    for ev in sch.events:
                        if ev[0] == "M":
                            _, sg, r, c = ev
                            bank = ring_wait()
                            width = GW if c < sg else (r + 1) * P
                            last = nc.tensor.matmul(
                                bank[:, 0:width],
                                h.qT[0:STACK, ds(e, 1), (sg * GT + r) * P:(sg * GT + r + 1) * P].rearrange("k a q -> k (a q)"),
                                h.kT[0:STACK, c * GW:c * GW + width], start=True, stop=(c < sg))
                            if c == sg:
                                last = nc.tensor.matmul(bank[:, r * P:(r + 1) * P], h.unit[:, :], h.tri[:, :],
                                                        start=False, stop=True)
                            last.then_inc(s["m_full"], 1)
                            mcount += 1
                            users.append(("M", mcount))
                        elif ev[0] == "T":
                            sg = ev[1]
                            bank = ring_wait()
                            pe.wait_ge(s["m3_ready"], it * G + (sg + 1))
                            for r in range(GT):
                                last = nc.tensor.matmul(bank[STACK:STACK + 3, r * P:(r + 1) * P],
                                                        h.m3[:, sg % 2, r, :], core.ident16[:, :],
                                                        start=True, stop=True)
                            last.then_inc(s["mt_full"], 1)
                            tcount += 1
                            users.append(("T", tcount))
                        else:
                            _, sg, p = ev
                            k = ecount
                            ecount += 1
                            if p == 0:
                                pe.wait_ge(s["mt_read"], it * G + (sg + 2))
                            pe.wait_ge(s["exped"], it * NE + (k + 1))
                            for jj in range(2):
                                j = 2 * p + jj
                                lo = max(0, j - GT * sg) * P
                                bank = core.psum[2 * (k % 2) + jj]
                                diag = j >= GT * sg
                                last = nc.tensor.matmul(
                                    bank[:, lo:GW], h.kT[:, j * P:(j + 1) * P],
                                    h.qT[:, ds(e, 1), sg * GW + lo:(sg + 1) * GW].rearrange("k a q -> k (a q)"),
                                    start=True, stop=not diag)
                                if diag:
                                    last = nc.tensor.matmul(bank[:, lo:lo + P], h.unit[:, :], h.triT[:, :],
                                                            start=False, stop=True)
                            last.then_inc(s["s_full"], 1)
                            pending.append((sg, p, k))
                            if len(pending) > 1:
                                attend(*pending.pop(0))
                            if p == 2 * sg + 1:
                                attend(*pending.pop(0))

                pe.wait_ge(s["at_ready"], n + 1)
                for g in range(G + 1):
                    if g < G:
                        if g >= 4:
                            pe.wait_ge(s["at_copied"], n * G + (g - 3))
                        for r in range(GT):
                            last = nc.tensor.transpose(core.psum[g % 4][:, r * P:(r + 1) * P],
                                                       h.at[:, g * GT + r, :], core.ident[:, :])
                        last.then_inc(s["at_turned"], 1)
                    if g >= 1:
                        pe.wait_ge(s["at_copied"], n * G + g)
                        for r in range(GT):
                            t = (g - 1) * GT + r
                            last = nc.tensor.matmul(core.psum[6][:, t * QS:(t + 1) * QS],
                                                    h.atT[:, (g - 1) % 2, r * P:(r + 1) * P],
                                                    h.gw[:, ds(n, 1), :].rearrange("p a e -> p (a e)"),
                                                    start=True, stop=True)
                        last.then_inc(s["gate_sums"], 1)

        @block.scalar
        def _(act):
            act.sem_inc(s["exped"], 2)
            act.sem_inc(s["mt_read"], 1)
            with act.Fori(0, HEADS) as n:
                act.wait_ge(s["w_ready"], n + 1)
                for g in range(G):
                    act.wait_ge(s["sx_sums"], n * G + (g + 1))
                    if g >= 2:
                        act.wait_ge(s["v_sums"], n * G + (g - 1))
                    nc.scalar.activation(h.sxT[:, g % 2, :], core.psum[4 + g % 2][0:HD, :], ACT.Identity,
                                         bias=h.hlb_n[:, :]).then_inc(s["sx_in"], 1)
                    for e in range(QS + 1):
                        u = g * (QS + 1) + e
                        dst = h.qT[0:STACK, e, g * GW:(g + 1) * GW] if e < QS else h.kT[0:STACK, g * GW:(g + 1) * GW]
                        act.wait_ge(s["qk_sums"], n * U + (u + 1))
                        nc.scalar.activation(dst, core.psum[u % 4][0:STACK, :], ACT.Copy).then_inc(s["qk_high"], 1)
                with act.Fori(0, QS) as e:
                    it = n * QS + e
                    k, tcount = 0, 0
                    for ev in sch.events:
                        if ev[0] == "T":
                            sg = ev[1]
                            turn = sum(1 for x in sch.events[:sch.events.index(ev)] if x[0] in "MT")
                            act.wait_ge(s["mt_full"], it * G + (sg + 1))
                            nc.scalar.activation(
                                h.qT[STACK:STACK + 3, ds(e, 1), sg * GW:(sg + 1) * GW],
                                core.psum[MB[turn % len(MB)]][STACK:STACK + 3, :].unsqueeze(1),
                                ACT.Copy).then_inc(s["mt_read"], 1)
                        elif ev[0] == "E":
                            _, sg, p = ev
                            act.wait_ge(s["s_full"], it * NE + (k + 1))
                            act.wait_ge(s["pv_done"], it * NE + (k + 1))
                            b = 2 * (k % 2)
                            if 2 * p + 1 < GT * sg:
                                last = nc.scalar.activation(h.PT[:, k % 4, :, :], core.banks[:, b:b + 2, :], ACT.Exp,
                                                            scale=ROOT)
                            else:
                                for jj in range(2):
                                    lo = max(0, 2 * p + jj - GT * sg) * P
                                    last = nc.scalar.activation(h.PT[:, k % 4, jj, lo:GW], core.psum[b + jj][:, lo:GW],
                                                                ACT.Exp, scale=ROOT)
                            last.then_inc(s["exped"], 1)
                            k += 1
                for g in range(G):
                    act.wait_ge(s["at_turned"], n * G + (g + 1))
                    if g >= 2:
                        act.wait_ge(s["gate_sums"], n * G + (g - 1))
                    nc.scalar.activation(h.atT[:, g % 2, :], core.psum[g % 4][:, :], ACT.Copy).then_inc(s["at_copied"], 1)
                act.wait_ge(s["shifted"], n + 1)
                nc.scalar.activation(h.gs[:, :, :], h.gs[:, :, :], ACT.Exp).then_inc(s["gs_exp"], 1)
                act.wait_ge(s["var_ready"], n + 1)
                nc.scalar.activation(h.var[:, :], h.var[:, :], ACT.Sqrt).then_inc(s["std_ready"], 1)

        @block.vector
        def _(dve):
            dve.sem_inc(s["m_read"], 1)
            dve.sem_inc(s["po_read"], 1)
            with dve.Fori(0, HEADS) as n:
                one = ds(n, 1)
                nc.vector.tensor_copy(h.hlw_n[:, :].unsqueeze(1), h.hlw[:, one, :])
                nc.vector.tensor_copy(h.hlb_n[:, :], h.hlb[:, one])
                for k in range(3):
                    nc.vector.tensor_copy(h.wq_n[:, :, k, :], h.wq[:, one, :, :].rearrange("d a e o -> d (a e) o"))
                    nc.vector.tensor_copy(h.wk_n[:, k:k + 1, :], h.wk[:, one, :])
                nc.vector.tensor_copy(h.wvi_n[:, 0:HD].unsqueeze(1), h.wv[:, one, :])
                nc.vector.tensor_copy(h.wvi_n[:, HD:2 * HD], core.ident[0:HD, 0:HD])
                dve.drain().then_inc(s["w_ready"], 1)
                for g in range(G):
                    for e in range(QS + 1):
                        u = g * (QS + 1) + e
                        lo = 2 * HD if e < QS else HD
                        dst = h.qT[lo:lo + HD, e, g * GW:(g + 1) * GW] if e < QS else h.kT[lo:lo + HD, g * GW:(g + 1) * GW]
                        dve.wait_ge(s["qk_high"], n * U + (u + 1))
                        nc.vector.tensor_tensor(dst, core.psum[u % 4][lo:lo + HD, :], dst,
                                                ALU.subtract).then_inc(s["qk_split"], 1)
                    dve.wait_ge(s["v_sums"], n * G + (g + 1))
                    both = core.psum[6 + g % 2][:, 0:GT * 2 * HD].rearrange("p (r w) -> p r w", w=2 * HD)
                    nc.vector.tensor_copy(h.V[:, g * GT:(g + 1) * GT, 0:HD], both[:, :, 0:HD])
                    nc.vector.tensor_copy(h.sx[:, g * GT:(g + 1) * GT, :], both[:, :, HD:2 * HD]).then_inc(s["v_in"], 1)

                with dve.Fori(0, QS) as e:
                    it = n * QS + e
                    turn, mcount = 0, 0
                    for at, ev in enumerate(sch.events):
                        if ev[0] == "T":
                            turn += 1
                        elif ev[0] == "M":
                            _, sg, r, c = ev
                            width = GW if c < sg else (r + 1) * P
                            dve.wait_ge(s["m_full"], it * NM + (mcount + 1))
                            nc.vector.tensor_reduce(h.pm[:, r, c:c + 1], core.psum[MB[turn % len(MB)]][:, 0:width],
                                                    AX.X, ALU.max).then_inc(s["m_read"], 1)
                            turn += 1
                            mcount += 1
                            if r == GT - 1 and c == sg:
                                m3 = h.m3[:, sg % 2, :, :]
                                dve.drain()
                                nc.vector.tensor_reduce(h.nm[:, :], h.pm[:, :, 0:sg + 1], AX.X, ALU.max, negate=True)
                                dve.drain()
                                nc.vector.tensor_copy(m3[:, :, 0], h.nm[:, :])
                                dve.drain()
                                nc.vector.tensor_tensor(h.nd[:, :], h.nm[:, :], m3[:, :, 0], ALU.subtract)
                                dve.drain()
                                nc.vector.tensor_copy(m3[:, :, 1], h.nd[:, :])
                                dve.drain()
                                nc.vector.tensor_tensor(m3[:, :, 2], h.nd[:, :], m3[:, :, 1], ALU.subtract)
                                dve.drain().then_inc(s["m3_ready"], 1)
                        if at in sch.closing:
                            sg = sch.closing[at]
                            po = core.psum[7][:, 0:GT * (HD + 1)].rearrange("p (r w) -> p r w", w=HD + 1)
                            dve.wait_ge(s["po_full"], it * G + (sg + 1))
                            nc.vector.reciprocal(h.rec[:, :], po[:, :, HD])
                            dve.drain()
                            out = h.at[:, sg * GT:(sg + 1) * GT, ds(e * HD, HD)]
                            nc.vector.tensor_tensor(out, po[:, :, 0:HD], over(h.rec[:, :], HD),
                                                    ALU.mult).then_inc(s["po_read"], 1)
                            dve.drain()

                nc.vector.tensor_scalar(h.tmp[:, :, :], h.sx[:, :, :], 0.0, None, ALU.not_equal)
                dve.drain()
                for e in range(QS):
                    a = h.at[:, :, e * HD:(e + 1) * HD]
                    last = nc.vector.tensor_tensor(a, a, h.tmp[:, :, :], ALU.mult)
                dve.drain().then_inc(s["at_ready"], 1)
                dve.wait_ge(s["gate_sums"], n * G + G)
                nc.vector.tensor_tensor(h.gs[:, :, :], core.psum[6][:, 0:T * QS].rearrange("p (t e) -> p t e", e=QS),
                                        h.gb[:, one, :].broadcast_to([P, T, QS]), ALU.add)
                dve.drain()
                softmax_rows(nc, dve, h.gs[:, :, :], h.stat[:, :], s["shifted"], s["gs_exp"], n + 1)
                nc.vector.tensor_copy(h.hn[:, :, :], h.sx[:, :, :])
                for e in range(QS):
                    nc.vector.tensor_tensor(h.tmp[:, :, :], h.at[:, :, e * HD:(e + 1) * HD],
                                            over(h.gs[:, :, e], HD), ALU.mult)
                    dve.drain()
                    nc.vector.tensor_tensor(h.hn[:, :, :], h.hn[:, :, :], h.tmp[:, :, :], ALU.add)
                    dve.drain()
                norm_rows(nc, dve, h.hn[:, :, :], h.hn[:, :, :], h.tmp[:, :, :], h.mean[:, :], h.var[:, :], HD,
                          EPS_HEAD, s["var_ready"], s["std_ready"], n + 1)
                nc.vector.tensor_tensor(h.hn[:, :, :], h.hn[:, :, :], rows(h.lng[:, :], T), ALU.mult)
                dve.drain()
                nc.vector.tensor_tensor(h.fx[:, :, ds(n * HD, HD)], h.hn[:, :, :], rows(h.lnb[:, :], T), ALU.add)
                dve.drain()


def head_mix_stage(core, h, bd1, bd2, b1, b2, ng, nb, fg, own):
    nc = core.nc

    def sb(name, shape):
        return own.enter_context(nc.sbuf_tensor("l1m_" + name, shape, FP32))
    fxT, h1, hx, sq = sb("fxT", [P, 2, GW]), sb("h1", [P, 2, GW]), core.xn, sb("sq", [P, T, D])
    mean, var = sb("mean", [P, T * HEADS]), sb("var", [P, T * HEADS])
    hg, stat = sb("hg", [P, T, HEADS]), sb("stat", [P, T])
    s = {n: core.sem("l1m_" + n) for n in
         ("turned", "fxT_in", "h1_sums", "h1_in", "h1_ready", "h2_sums", "h2_read", "var_ready", "std_ready",
          "out_ready", "out_turned", "out_copied", "fg_sums", "shifted", "exped")}
    blocks = lambda ap: ap.rearrange("p t (n d) -> p (t n) d", d=HD)
    with nc.Block() as block:
        @block.tensor
        def _(pe):
            for g in range(G):
                if g >= 2:
                    pe.wait_ge(s["fxT_in"], g - 1)
                for r in range(GT):
                    last = nc.tensor.transpose(core.psum[g % 2][:, r * P:(r + 1) * P], h.fx[:, g * GT + r, :],
                                               core.ident[:, :])
                last.then_inc(s["turned"], 1)
                pe.wait_ge(s["fxT_in"], g + 1)
                if g >= 2:
                    pe.wait_ge(s["h1_in"], g - 1)
                nc.tensor.matmul(core.psum[2 + g % 2][:, :], bd1[:, :], fxT[:, g % 2, :], start=True,
                                 stop=True).then_inc(s["h1_sums"], 1)
                pe.wait_ge(s["h1_ready"], g + 1)
                if g >= 2:
                    pe.wait_ge(s["h2_read"], g - 1)
                for r in range(GT):
                    last = nc.tensor.matmul(core.psum[4 + g % 2][:, r * P:(r + 1) * P],
                                            h1[:, g % 2, r * P:(r + 1) * P], bd2[:, :], start=True, stop=True)
                last.then_inc(s["h2_sums"], 1)
            pe.wait_ge(s["out_ready"], 1)
            for g in range(G):
                if g >= 2:
                    pe.wait_ge(s["out_copied"], g - 1)
                for r in range(GT):
                    last = nc.tensor.transpose(core.psum[g % 2][:, r * P:(r + 1) * P], hx[:, g * GT + r, :],
                                               core.ident[:, :])
                last.then_inc(s["out_turned"], 1)
                pe.wait_ge(s["out_copied"], g + 1)
                for r in range(GT):
                    t = g * GT + r
                    last = nc.tensor.matmul(core.psum[6][:, t * HEADS:(t + 1) * HEADS],
                                            fxT[:, g % 2, r * P:(r + 1) * P], fg[:, :], start=True, stop=True)
                last.then_inc(s["fg_sums"], 1)

        @block.scalar
        def _(act):
            for g in range(G):
                act.wait_ge(s["turned"], g + 1)
                if g >= 2:
                    act.wait_ge(s["h1_ready"], g - 1)
                nc.scalar.activation(fxT[:, g % 2, :], core.psum[g % 2][:, :], ACT.Copy).then_inc(s["fxT_in"], 1)
                act.wait_ge(s["h1_sums"], g + 1)
                if g >= 2:
                    act.wait_ge(s["h2_sums"], g - 1)
                nc.scalar.activation(h1[:, g % 2, :], core.psum[2 + g % 2][:, :], ACT.Relu,
                                     bias=b1[:, 0:1]).then_inc(s["h1_in"], 1)
            act.wait_ge(s["var_ready"], 1)
            nc.scalar.activation(var[:, :], var[:, :], ACT.Sqrt).then_inc(s["std_ready"], 1)
            for g in range(G):
                act.wait_ge(s["out_turned"], g + 1)
                if g >= 2:
                    act.wait_ge(s["fg_sums"], g - 1)
                nc.scalar.activation(fxT[:, g % 2, :], core.psum[g % 2][:, :], ACT.Copy).then_inc(s["out_copied"], 1)
            act.wait_ge(s["shifted"], 1)
            nc.scalar.activation(hg[:, :, :], hg[:, :, :], ACT.Exp).then_inc(s["exped"], 1)

        @block.vector
        def _(dve):
            for g in range(G):
                a = slice(g * GT, (g + 1) * GT)
                dve.wait_ge(s["h1_in"], g + 1)
                nc.vector.scalar_tensor_tensor(h1[:, g % 2, :], fxT[:, g % 2, :], 0.0, h1[:, g % 2, :],
                                               ALU.not_equal, ALU.mult).then_inc(s["h1_ready"], 1)
                dve.wait_ge(s["h2_sums"], g + 1)
                nc.vector.tensor_tensor(
                    blocks(hx[:, a, :]), core.psum[4 + g % 2][:, :].rearrange("p (n d) -> p n d", d=HD),
                    rows(b2[:, :], GT * HEADS), ALU.add).then_inc(s["h2_read"], 1)
                dve.drain()
                nc.vector.scalar_tensor_tensor(hx[:, a, :], h.fx[:, a, :], 0.0, hx[:, a, :], ALU.not_equal, ALU.mult)
                dve.drain()
                nc.vector.tensor_tensor(hx[:, a, :], hx[:, a, :], h.fx[:, a, :], ALU.add)
            dve.drain()
            norm_rows(nc, dve, blocks(hx[:, :, :]), blocks(hx[:, :, :]), blocks(sq[:, :, :]), mean[:, :], var[:, :],
                      HD, EPS_HEAD, s["var_ready"], s["std_ready"], 1)
            nc.vector.tensor_tensor(blocks(hx[:, :, :]), blocks(hx[:, :, :]), rows(ng[:, :], T * HEADS), ALU.mult)
            dve.drain()
            nc.vector.tensor_tensor(blocks(hx[:, :, :]), blocks(hx[:, :, :]), rows(nb[:, :], T * HEADS), ALU.add)
            dve.drain().then_inc(s["out_ready"], 1)
            dve.wait_ge(s["fg_sums"], G)
            nc.vector.tensor_copy(hg[:, :, :], core.psum[6][:, 0:T * HEADS].rearrange("p (t e) -> p t e", e=HEADS))
            dve.drain()
            softmax_rows(nc, dve, hg[:, :, :], stat[:, :], s["shifted"], s["exped"], 1)
            nc.vector.tensor_tensor(blocks(hx[:, :, :]), blocks(hx[:, :, :]),
                                    over(hg[:, :, :].rearrange("p t n -> p (t n)"), HD), ALU.mult)
            dve.drain()
            nc.vector.tensor_tensor(core.x[:, :, :], core.x[:, :, :], hx[:, :, :], ALU.add)


def second_expert_layer(core, w):
    nc = core.nc
    with ExitStack() as own:
        def sb(name, shape):
            return own.enter_context(nc.sbuf_tensor("l1w_" + name, shape, FP32))
        h = HeadTiles(core, own)
        bd1, bd2, b1, b2 = sb("bd1", [P, P]), sb("bd2", [P, P]), sb("b1", [P, 1]), sb("b2", [P, HD])
        ng, nb, fg = sb("ng", [P, HD]), sb("nb", [P, HD]), sb("fg", [D, HEADS])
        with nc.Block() as block:
            @block.gpsimd
            def _(pool):
                nc.gpsimd.memset(bd1[:, :], 0.0)
                nc.gpsimd.memset(bd2[:, :], 0.0)
        attention_constants(core, h)
        loads = [(h.hlw[:, :, :], w["L1_ffn_hl_w"]), (h.hlb[:, :], w["L1_ffn_hl_b"]), (h.wq[:, :, :, :], w["L1_ffn_wq"]),
                 (h.wk[:, :, :], w["L1_ffn_wk"]), (h.wv[:, :, :], w["L1_ffn_wv"]), (h.gw[:, :, :], w["L1_ffn_gate_w"]),
                 (h.gb[:, :, :].rearrange("p n e -> p (n e)"),
                  w["L1_ffn_gate_b"].rearrange("n e -> (n e)").partition_broadcast(P)),
                 (h.lng[:, :], w["L1_ffn_ln_g"].partition_broadcast(P)),
                 (h.lnb[:, :], w["L1_ffn_ln_b"].partition_broadcast(P)),
                 (b2[:, :], w["L1_ffn_fc2_b"].partition_broadcast(P)),
                 (ng[:, :], w["L1_ffn_fnorm_g"].partition_broadcast(P)),
                 (nb[:, :], w["L1_ffn_fnorm_b"].partition_broadcast(P)), (fg[:, :], w["L1_ffn_fgate_w"])]
        for n in range(HEADS):
            a = slice(n * HD, (n + 1) * HD)
            loads += [(bd1[a, a], w["L1_ffn_fc1_w"]), (bd2[a, a], w["L1_ffn_fc2_w"]),
                      (b1[a, :], w["L1_ffn_fc1_b"].unsqueeze(1))]
        norm_stage(core, loads, "l1n")
        heads_stage(core, h)
        with ExitStack() as mix:
            head_mix_stage(core, h, bd1, bd2, b1, b2, ng, nb, fg, mix)


LAYERS = [first_graph_layer, first_expert_layer, second_graph_layer, second_expert_layer, third_graph_layer,
          third_expert_layer, fourth_graph_layer, fourth_expert_layer]
USED = ["x", "L0_gnn_W1", "L0_gnn_W2", "L0_gnn_b", "adjT", "L0_ffn_Wg", "L0_ffn_bg", "L0_ffn_W1", "L0_ffn_b1",
        "L0_ffn_W2", "L0_ffn_b2", "L1_gnn_W", "L1_gnn_a", "adj", "L1_ffn_hl_w", "L1_ffn_hl_b", "L1_ffn_wq",
        "L1_ffn_wk", "L1_ffn_wv", "L1_ffn_gate_w", "L1_ffn_gate_b", "L1_ffn_ln_g", "L1_ffn_ln_b",
        "L1_ffn_fc2_b", "L1_ffn_fnorm_g", "L1_ffn_fnorm_b", "L1_ffn_fgate_w", "L1_ffn_fc1_w", "L1_ffn_fc2_w",
        "L1_ffn_fc1_b", "L2_gnn_H_v", "L2_ffn_router_w1", "L2_ffn_router_b1", "L2_ffn_router_w2",
        "L2_ffn_router_b2", "L2_ffn_expert_w1", "L2_ffn_expert_w2", "L2_ffn_expert_w3", "L2_ffn_expert_b1",
        "L2_ffn_expert_b2", "L2_ffn_expert_b3", "L3_gnn_W", "L3_gnn_b", "L3_ffn_router_w", "L3_ffn_w1",
        "L3_ffn_w3", "L3_ffn_w2"]


def build(nc, w, out):
    with ExitStack() as ctx:
        core = Core(nc, ctx)
        core.begin_layer()
        load_inputs(core, w["x"])
        core.end_layer()
        for layer in LAYERS:
            core.begin_layer()
            layer(core, w)
            core.end_layer()
        core.begin_layer()
        store_output(core, out)
        core.end_layer()


def kernel(**inputs):
    import numpy as np
    import concourse.bacc as bacc
    from concourse.bass_utils import run_bass_kernel_spmd as run

    t = {name: np.asarray(a) for name, a in inputs.items()}
    tiles = N // P
    t["adjT"] = t["adj"].reshape(tiles, P, tiles, P).transpose(0, 3, 2, 1)
    t["L0_ffn_b1"] = t["L0_ffn_b1"].reshape(8, 2, P).transpose(2, 0, 1)
    t["L2_ffn_expert_b1"] = t["L2_ffn_expert_b1"].T
    t["L2_ffn_expert_b2"] = t["L2_ffn_expert_b2"].T
    t["L1_gnn_a"] = t["L1_gnn_a"].reshape(2, P).T
    t["L3_gnn_W"] = t["L3_gnn_W"].T
    t["L3_ffn_router_w"] = t["L3_ffn_router_w"].T
    for name in ("L3_ffn_w1", "L3_ffn_w3"):
        t[name] = t[name].transpose(2, 0, 1)
    t["L3_ffn_w2"] = t["L3_ffn_w2"].transpose(2, 0, 1)
    t["L1_ffn_hl_w"] = t["L1_ffn_hl_w"].transpose(2, 0, 1)
    t["L1_ffn_hl_b"] = t["L1_ffn_hl_b"].T
    t["L1_ffn_wq"] = t["L1_ffn_wq"].transpose(3, 0, 1, 2)
    t["L1_ffn_wk"] = t["L1_ffn_wk"].transpose(2, 0, 1)
    t["L1_ffn_wv"] = t["L1_ffn_wv"].transpose(2, 0, 1)
    t["L1_ffn_gate_w"] = t["L1_ffn_gate_w"].transpose(2, 0, 1)
    t["L1_ffn_fc1_w"] = t["L1_ffn_fc1_w"].T
    t["L1_ffn_fc2_w"] = t["L1_ffn_fc2_w"].T
    t["L1_ffn_fgate_w"] = t["L1_ffn_fgate_w"].T
    nc = bacc.Bacc("TRN2", target_bir_lowering=False, num_devices=1)
    arrays, w = {}, {}
    for name in USED:
        a = np.ascontiguousarray(t[name])
        arrays[f"{name}_dram"] = a
        w[name] = nc.dram_tensor(f"{name}_dram", a.shape, mybir.dt.from_np(a.dtype), kind="ExternalInput").ap()
    out = nc.dram_tensor("out_dram", (N, D), FP32, kind="ExternalOutput").ap()
    build(nc, w, out)
    return run(nc, [arrays], core_ids=[0]).results[0]["out_dram"]
```

```python
import concourse.bass as bass
from concourse import mybir
from contextlib import ExitStack

FP32 = mybir.dt.float32
FP16 = mybir.dt.float16
BF16 = mybir.dt.bfloat16
ALU = mybir.AluOpType
ACT = mybir.ActivationFunctionType
AX = mybir.AxisListType
ds = bass.ds

P = 128
N = 4096
T = N // P
GT = 4
GW = GT * P
G = T // GT
D = 128
NODE_K = 16
BIG = 1.0e30
EPS_LN = 1e-5


def over(ap, n):
    return ap.unsqueeze(2).broadcast_to([ap.shape[0], ap.shape[1], n])


def rows(ap, n):
    return ap.unsqueeze(1).broadcast_to([ap.shape[0], n, ap.shape[1]])


class Core:

    def __init__(self, nc, ctx):
        self.nc, self.ctx, self.n, self.sems = nc, ctx, 0, []
        self.x = self.keep("x_nat", [P, T, D])
        self.xn = self.keep("x_normed", [P, T, D])
        self.xT = self.keep("x_normedT", [P, N])
        self.ident = self.keep("ident", [P, P])
        self.ident16 = self.keep("ident16", [P, P], FP16)
        self.deg = self.keep("deg", [P, T])
        self.banks = ctx.enter_context(nc.psum_tensor("banks", [P, 8, GW], FP32))
        self.psum = [self.banks[:, i, :] for i in range(8)]

    def keep(self, name, shape, dt=FP32):
        return self.ctx.enter_context(self.nc.sbuf_tensor(name, shape, dt))

    def sem(self, name):
        self.n += 1
        s = self.layer.enter_context(self.nc.semaphore(f"{name}_{self.n}"))
        self.sems.append(s)
        return s

    def begin_layer(self):
        self.layer, self.sems = ExitStack(), []

    def end_layer(self):
        with self.nc.Block() as block:
            @block.gpsimd
            def _(pool):
                for s in self.sems:
                    pool.sem_clear(s)
        self.layer.close()


def load_inputs(core, x):
    nc = core.nc
    loaded, zeroed = core.sem("x_loaded"), core.sem("ident_zeroed")
    with nc.Block() as block:
        @block.sync
        def _(sp):
            sp.dma_start(core.x[:, :, :], x.rearrange("(t p) d -> p t d", p=P)).then_inc(loaded, 16)
            sp.wait_ge(loaded, 16)

        @block.gpsimd
        def _(pool):
            for m in (core.ident, core.ident16):
                nc.gpsimd.memset(m[:, :], 0.0).then_inc(zeroed, 1)
            pool.wait_ge(zeroed, 2)
            for m in (core.ident, core.ident16):
                nc.gpsimd.affine_select(out=m[:, :], in_=m[:, :], compare_op=ALU.not_equal, fill=1.0,
                                        base=0, pattern=[[-1, P]], channel_multiplier=1)


def store_output(core, out):
    nc = core.nc
    stored = core.sem("out_stored")
    with nc.Block() as block:
        @block.sync
        def _(sp):
            sp.dma_start(out.rearrange("(t p) d -> p t d", p=P), core.x[:, :, :]).then_inc(stored, 16)
            sp.wait_ge(stored, 16)


def norm_stage(core, loads, tag, proj=None):
    nc = core.nc
    x, xn, xT = core.x, core.xn, core.xT
    with ExitStack() as own:
        def sb(name, shape):
            return own.enter_context(nc.sbuf_tensor(f"{tag}_{name}", shape, FP32))
        mean, var, rstd = sb("mean", [P, T]), sb("var", [P, T]), sb("rstd", [P, T])
        sq = xT[:, :].rearrange("p (t d) -> p t d", d=D)
        centred, squared = core.sem(tag + "centred"), core.sem(tag + "squared")
        var_ready, std_ready = core.sem(tag + "var_ready"), core.sem(tag + "std_ready")
        normed, turned, copied = core.sem(tag + "normed"), core.sem(tag + "turned"), core.sem(tag + "copied")
        loaded = core.sem(tag + "w_loaded")
        projected, dma_in = core.sem(tag + "projected"), core.sem(tag + "dma_in")
        w = proj[0].shape[1] if proj else 0

        with nc.Block() as block:
            @block.sync
            def _(sp):
                for dst, src in loads:
                    sp.dma_start(dst, src).then_inc(loaded, 16)
                if loads:
                    sp.wait_ge(loaded, 16 * len(loads))

            @block.vector
            def _(dve):
                nc.vector.tensor_reduce(mean[:, :], x[:, :, :], AX.X, ALU.add)
                dve.drain()
                nc.vector.tensor_scalar(mean[:, :], mean[:, :], 1.0 / D, None, ALU.mult)
                dve.drain()
                for h in range(2):
                    a = slice(h * T // 2, (h + 1) * T // 2)
                    nc.vector.tensor_tensor(xn[:, a, :], x[:, a, :], over(mean[:, a], D),
                                            ALU.subtract).then_inc(centred, 1)
                for h in range(2):
                    a = slice(h * T // 2, (h + 1) * T // 2)
                    dve.wait_ge(squared, h + 1)
                    nc.vector.tensor_reduce(var[:, a], sq[:, a, :], AX.X, ALU.add)
                dve.drain()
                nc.vector.tensor_scalar(var[:, :], var[:, :], 1.0 / D, EPS_LN, ALU.mult,
                                        ALU.add).then_inc(var_ready, 1)
                dve.wait_ge(std_ready, 1)
                nc.vector.reciprocal(rstd[:, :], rstd[:, :])
                dve.drain()
                for g in range(G):
                    a = slice(g * GT, (g + 1) * GT)
                    nc.vector.tensor_tensor(xn[:, a, :], xn[:, a, :], over(rstd[:, a], D),
                                            ALU.mult).then_inc(normed, 1)
                if proj:
                    dve.wait_ge(projected, 1)
                    bank = core.psum[6][:, 0:T * w].rearrange("p (t w) -> p t w", w=w)
                    if proj[1] is None:
                        nc.vector.tensor_copy(proj[2], bank)
                    else:
                        dve.wait_ge(loaded, 16 * len(loads))
                        nc.vector.tensor_tensor(proj[2], bank, rows(proj[1], T), ALU.add)

            @block.scalar
            def _(act):
                for h in range(2):
                    a = slice(h * T // 2, (h + 1) * T // 2)
                    act.wait_ge(centred, h + 1)
                    nc.scalar.activation(sq[:, a, :], xn[:, a, :], ACT.Square).then_inc(squared, 1)
                act.wait_ge(var_ready, 1)
                nc.scalar.activation(rstd[:, :], var[:, :], ACT.Sqrt).then_inc(std_ready, 1)
                for g in range(G):
                    act.wait_ge(turned, g + 1)
                    nc.scalar.activation(xT[:, g * GW:(g + 1) * GW], core.psum[g % 4][:, :],
                                         ACT.Copy).then_inc(copied, 1)

            @block.tensor
            def _(pe):
                for g in range(G):
                    pe.wait_ge(normed, g + 1)
                    if g >= 4:
                        pe.wait_ge(copied, g - 3)
                    for r in range(GT):
                        last = nc.tensor.transpose(core.psum[g % 4][:, r * P:(r + 1) * P],
                                                   xn[:, g * GT + r, :], core.ident[:, :])
                    last.then_inc(turned, 1)
                if proj:
                    pe.wait_ge(copied, G)
                    pe.wait_ge(loaded, 16 * len(loads))
                    for t in range(T):
                        last = nc.tensor.matmul(core.psum[6][:, t * w:(t + 1) * w],
                                                xT[:, t * P:(t + 1) * P], proj[0],
                                                start=True, stop=True)
                    last.then_inc(projected, 1)


def top2(nc, dve, sb, score, e, second):
    hot1, hot2, cand, rest = (sb(n, [P, T, e]) for n in ("hot1", "hot2", "cand", "rest"))
    order = sb("order", [P, e])
    best, pick = sb("best", [P, T]), sb("pick", [P, T])
    for j in range(e):
        nc.vector.memset(order[:, j:j + 1], float(e - j))
    dve.drain()
    for hot, src, top in ((hot1, score, best), (hot2, rest, second)):
        nc.vector.tensor_reduce(top[:, :], src[:, :, :], AX.X, ALU.max)
        dve.drain()
        nc.vector.tensor_tensor(cand[:, :, :], src[:, :, :], over(top[:, :], e), ALU.is_equal)
        dve.drain()
        nc.vector.tensor_tensor(cand[:, :, :], cand[:, :, :], rows(order[:, :], T), ALU.mult)
        dve.drain()
        nc.vector.tensor_reduce(pick[:, :], cand[:, :, :], AX.X, ALU.max)
        dve.drain()
        nc.vector.tensor_tensor(hot[:, :, :], cand[:, :, :], over(pick[:, :], e), ALU.is_equal)
        dve.drain()
        if hot is hot1:
            nc.vector.scalar_tensor_tensor(rest[:, :, :], hot1[:, :, :], -BIG, score[:, :, :],
                                           ALU.mult, ALU.add)
            dve.drain()
    return hot1, hot2, best


WEIGHT_UNIT = 16.0


def split_high(nc, act, splits, highs):
    for src, dst, unit in splits:
        if unit != 1.0:
            nc.scalar.activation(src, src, ACT.Copy, scale=unit)
            act.drain()
        nc.scalar.activation(dst[:, 0, :], src, ACT.Copy).then_inc(highs, 1)


def split_low(nc, pool, splits, highs):
    for i, (src, dst, _unit) in enumerate(splits):
        pool.wait_ge(highs, i + 1)
        nc.gpsimd.tensor_tensor(dst[:, 1, :], src, dst[:, 0, :], ALU.subtract)


def split_product(nc, out, a, b, a_cols, b_cols):
    for i, (ka, kb) in enumerate(((0, 0), (0, 1), (1, 0))):
        last = nc.tensor.matmul(out, a[:, ka, a_cols], b[:, kb, b_cols], start=(i == 0), stop=(i == 2))
    return last


def gates_onehot(core, score, e, gates, splits, tag):
    nc = core.nc
    with ExitStack() as own:
        def sb(name, shape):
            return own.enter_context(nc.sbuf_tensor(f"{tag}_{name}", shape, FP32))
        second = sb("second", [P, T])
        highs = core.sem(tag + "highs")
        with nc.Block() as block:
            @block.scalar
            def _(act):
                split_high(nc, act, splits, highs)

            @block.gpsimd
            def _(pool):
                split_low(nc, pool, splits, highs)

            @block.vector
            def _(dve):
                hot1, hot2, _best = top2(nc, dve, sb, score, e, second)
                nc.vector.tensor_tensor(gates[:, :, :], hot1[:, :, :], hot2[:, :, :], ALU.add)


def gates_softmax(core, score, e, gates, renorm, splits, tag):
    nc = core.nc
    with ExitStack() as own:
        def sb(name, shape):
            return own.enter_context(nc.sbuf_tensor(f"{tag}_{name}", shape, FP32))
        top, den, second = sb("top", [P, T]), sb("den", [P, T]), sb("second", [P, T])
        prob = sb("prob", [P, T, e])
        shifted, exped = core.sem(tag + "shifted"), core.sem(tag + "exped")
        highs = core.sem(tag + "highs")
        with nc.Block() as block:
            @block.gpsimd
            def _(pool):
                split_low(nc, pool, splits, highs)

            @block.vector
            def _(dve):
                nc.vector.tensor_reduce(top[:, :], score[:, :, :], AX.X, ALU.max)
                dve.drain()
                nc.vector.tensor_tensor(prob[:, :, :], score[:, :, :], over(top[:, :], e),
                                        ALU.subtract).then_inc(shifted, 1)
                dve.wait_ge(exped, 1)
                nc.vector.tensor_reduce(den[:, :], prob[:, :, :], AX.X, ALU.add)
                dve.drain()
                nc.vector.reciprocal(den[:, :], den[:, :])
                dve.drain()
                nc.vector.tensor_tensor(prob[:, :, :], prob[:, :, :], over(den[:, :], e), ALU.mult)
                dve.drain()
                hot1, hot2, best = top2(nc, dve, sb, prob, e, second)
                if renorm:
                    nc.vector.scalar_tensor_tensor(den[:, :], best[:, :], 1e-9, second[:, :],
                                                   ALU.add, ALU.add)
                else:
                    nc.vector.tensor_tensor(second[:, :], second[:, :], best[:, :],
                                            ALU.subtract).then_inc(shifted, 1)
                    dve.wait_ge(exped, 2)
                    nc.vector.memset(best[:, :], 1.0)
                    nc.vector.tensor_scalar(den[:, :], second[:, :], 1.0, None, ALU.add)
                dve.drain()
                nc.vector.reciprocal(den[:, :], den[:, :])
                dve.drain()
                nc.vector.tensor_tensor(best[:, :], best[:, :], den[:, :], ALU.mult)
                nc.vector.tensor_tensor(second[:, :], second[:, :], den[:, :], ALU.mult)
                dve.drain()
                nc.vector.tensor_tensor(hot1[:, :, :], hot1[:, :, :], over(best[:, :], e), ALU.mult)
                nc.vector.tensor_tensor(hot2[:, :, :], hot2[:, :, :], over(second[:, :], e), ALU.mult)
                dve.drain()
                nc.vector.tensor_tensor(gates[:, :, :], hot1[:, :, :], hot2[:, :, :], ALU.add)

            @block.scalar
            def _(act):
                act.wait_ge(shifted, 1)
                nc.scalar.activation(prob[:, :, :], prob[:, :, :], ACT.Exp).then_inc(exped, 1)
                split_high(nc, act, splits, highs)
                if not renorm:
                    act.wait_ge(shifted, 2)
                    nc.scalar.activation(second[:, :], second[:, :], ACT.Exp).then_inc(exped, 1)

def add_expert(core, dve, bank, gates, g, ex, bias, yb, taken, x):
    nc = core.nc
    if bias is not None:
        nc.vector.tensor_tensor(yb[:, ex % 2, :, :], bank[:, :].rearrange("p (r d) -> p r d", d=D),
                                rows(bias, GT), ALU.add).then_inc(taken, 1)
        dve.drain()
    for r in range(GT):
        src = yb[:, ex % 2, r, :] if bias is not None else bank[:, r * P:(r + 1) * P]
        row = x[:, ds(g * GT + r, 1), :]
        last = nc.vector.scalar_tensor_tensor(
            row, src.unsqueeze(1), gates[:, ds(g * GT + r, 1), ex:ex + 1].rearrange("p a b -> p (a b)"),
            row, ALU.mult, ALU.add)
    if bias is None:
        last.then_inc(taken, 1)
        dve.drain()


def experts_gelu(core, e, xs, w1, b1, w2, b2, gates, tag):
    nc, x = core.nc, core.x
    C, RING = 2, 4
    U = e * C
    with ExitStack() as own:
        def sb(name, shape):
            return own.enter_context(nc.sbuf_tensor(f"{tag}_{name}", shape, FP32))
        hid = sb("hid", [P, 2, C, GW])
        yb = sb("yb", [P, 2, GT, D])
        sums = core.sem(tag + "hidden_sums")
        hidden = core.sem(tag + "hidden_ready")
        down_done = core.sem(tag + "down_done")
        taken = core.sem(tag + "y_taken")
        with nc.Block() as block:
            @block.tensor
            def _(pe):
                pe.sem_inc(down_done, 2)
                with pe.Fori(0, G) as g:
                    for s in range(e + 1):
                        if s < e:
                            for c in range(C):
                                n = s * C + c
                                pe.wait_ge(hidden, g * U + (n + 1))
                                split_product(nc, core.psum[n % RING][:, :], w1, xs, slice(n * P, (n + 1) * P),
                                              ds(g * GW, GW)).then_inc(sums, 1)
                        if s >= 1:
                            ex = s - 1
                            pe.wait_ge(hidden, g * U + ((ex + 1) * C + RING))
                            pe.wait_ge(taken, g * e + (ex + 1))
                            for r in range(GT):
                                for c in range(C):
                                    last = nc.tensor.matmul(core.psum[6 + ex % 2][:, r * P:(r + 1) * P],
                                                            hid[:, ex % 2, c, r * P:(r + 1) * P],
                                                            w2[:, ex, c, :], start=(c == 0), stop=(c == C - 1))
                            last.then_inc(down_done, 1)

            @block.scalar
            def _(act):
                act.sem_inc(hidden, RING)
                with act.Fori(0, G) as g:
                    for ex in range(e):
                        act.wait_ge(down_done, g * e + (ex + 1))
                        for c in range(C):
                            n = ex * C + c
                            act.wait_ge(sums, g * U + (n + 1))
                            nc.scalar.activation(hid[:, ex % 2, c, :], core.psum[n % RING][:, :], ACT.Gelu,
                                                 scale=1.0 / WEIGHT_UNIT, bias=b1[:, ex, c:c + 1]).then_inc(hidden, 1)

            @block.vector
            def _(dve):
                dve.sem_inc(taken, 2)
                with dve.Fori(0, G) as g:
                    for ex in range(e):
                        dve.wait_ge(down_done, g * e + (ex + 3))
                        add_expert(core, dve, core.psum[6 + ex % 2], gates, g, ex, b2[:, ex, :], yb, taken, x)
                    dve.drain()


def experts_deep(core, e, xs, w1, b1, w2, b2, w3, b3, gates, tag):
    nc, x = core.nc, core.x
    RING = 4
    U = 2 * e
    order = []
    for s in range(e + 1):
        if s < e:
            order.append((s, 0))
        if s >= 1:
            order.append((s - 1, 1))
    turn = {k: n for n, k in enumerate(order)}
    with ExitStack() as own:
        def sb(name, shape):
            return own.enter_context(nc.sbuf_tensor(f"{tag}_{name}", shape, FP32))
        hid = sb("hid", [P, 2, 2, GW])
        yb = sb("yb", [P, 2, GT, D])
        sums = core.sem(tag + "hidden_sums")
        hidden = core.sem(tag + "hidden_ready")
        down_done = core.sem(tag + "down_done")
        taken = core.sem(tag + "y_taken")
        with nc.Block() as block:
            @block.tensor
            def _(pe):
                pe.sem_inc(down_done, 2)
                with pe.Fori(0, G) as g:
                    def fill(ex, level):
                        n = turn[ex, level]
                        pe.wait_ge(hidden, g * U + (n + 1))
                        if level == 0:
                            split_product(nc, core.psum[n % RING][:, :], w1, xs, slice(ex * P, (ex + 1) * P),
                                          ds(g * GW, GW)).then_inc(sums, 1)
                        else:
                            nc.tensor.matmul(core.psum[n % RING][:, :], w2[:, ex, :], hid[:, ex % 2, 0, :],
                                             start=True, stop=True).then_inc(sums, 1)

                    for s in range(e + 2):
                        if s < e:
                            fill(s, 0)
                        if 1 <= s <= e:
                            pe.wait_ge(hidden, g * U + (turn[s - 1, 0] + 1 + RING))
                            fill(s - 1, 1)
                        if s >= 2:
                            ex = s - 2
                            pe.wait_ge(hidden, g * U + (turn[ex, 1] + 1 + RING))
                            pe.wait_ge(taken, g * e + (ex + 1))
                            for r in range(GT):
                                last = nc.tensor.matmul(core.psum[6 + ex % 2][:, r * P:(r + 1) * P],
                                                        hid[:, ex % 2, 1, r * P:(r + 1) * P],
                                                        w3[:, ex, :], start=True, stop=True)
                            last.then_inc(down_done, 1)

            @block.scalar
            def _(act):
                act.sem_inc(hidden, RING)
                with act.Fori(0, G) as g:
                    for n, (ex, level) in enumerate(order):
                        act.wait_ge(sums, g * U + (n + 1))
                        if level == 1:
                            act.wait_ge(down_done, g * e + (ex + 1))
                        nc.scalar.activation(hid[:, ex % 2, level, :], core.psum[n % RING][:, :], ACT.Relu,
                                             scale=(1.0 / WEIGHT_UNIT, 1.0)[level], bias=(b1, b2)[level][:, ex:ex + 1]).then_inc(hidden, 1)

            @block.vector
            def _(dve):
                dve.sem_inc(taken, 2)
                with dve.Fori(0, G) as g:
                    for ex in range(e):
                        dve.wait_ge(down_done, g * e + (ex + 3))
                        add_expert(core, dve, core.psum[6 + ex % 2], gates, g, ex, b3[:, ex, :], yb, taken, x)
                    dve.drain()


def experts_swiglu(core, e, chunks, xs, w1, w3, w2, gates, tag):
    nc, x = core.nc, core.x
    C, H = len(chunks), sum(m for _lo, m in chunks)
    RING = C
    U = e * C
    with ExitStack() as own:
        def sb(name, shape):
            return own.enter_context(nc.sbuf_tensor(f"{tag}_{name}", shape, FP32))
        sil = sb("sil", [P, C, GW])
        hid = sb("hid", [P, 2, C, GW])
        sums = core.sem(tag + "hidden_sums")
        silued = core.sem(tag + "silu_ready")
        hidden = core.sem(tag + "hidden_ready")
        down_done = core.sem(tag + "down_done")
        taken = core.sem(tag + "y_taken")
        with nc.Block() as block:
            @block.tensor
            def _(pe):
                pe.sem_inc(down_done, 2)
                with pe.Fori(0, G) as g:
                    for s in range(e + 1):
                        if s < e:
                            for c, (lo, m) in enumerate(chunks):
                                n = s * C + c
                                pe.wait_ge(silued, g * U + (n + 1))
                                cols = slice(s * H + lo, s * H + lo + m)
                                split_product(nc, core.psum[c][0:m, :], w1, xs, cols, ds(g * GW, GW))
                                pe.wait_ge(hidden, g * U + (n + 1))
                                split_product(nc, core.psum[C + c][0:m, :], w3, xs, cols,
                                              ds(g * GW, GW)).then_inc(sums, 1)
                        if s >= 1:
                            ex = s - 1
                            pe.wait_ge(hidden, g * U + ((ex + 1) * C + RING))
                            pe.wait_ge(taken, g * e + (ex + 1))
                            for r in range(GT):
                                for c, (lo, m) in enumerate(chunks):
                                    last = nc.tensor.matmul(core.psum[6 + ex % 2][:, r * P:(r + 1) * P],
                                                            hid[0:m, ex % 2, c, r * P:(r + 1) * P],
                                                            w2[0:m, ex, c, :], start=(c == 0), stop=(c == C - 1))
                            last.then_inc(down_done, 1)

            @block.scalar
            def _(act):
                act.sem_inc(silued, RING)
                with act.Fori(0, G) as g:
                    for n in range(U):
                        c, m = n % C, chunks[n % C][1]
                        act.wait_ge(sums, g * U + (n + 1))
                        act.wait_ge(hidden, g * U + (n + 1))
                        nc.scalar.activation(sil[0:m, c, :], core.psum[c][0:m, :],
                                             ACT.Silu, scale=1.0 / WEIGHT_UNIT).then_inc(silued, 1)

            @block.vector
            def _(dve):
                dve.sem_inc(taken, 2)
                dve.sem_inc(hidden, RING)
                with dve.Fori(0, G) as g:
                    for s in range(e + 1):
                        if s < e:
                            dve.wait_ge(down_done, g * e + (s + 1))
                            for c, (lo, m) in enumerate(chunks):
                                dve.wait_ge(silued, g * U + (s * C + c + 1 + RING))
                                nc.vector.scalar_tensor_tensor(
                                    hid[0:m, s % 2, c, :], core.psum[C + c][0:m, :], 1.0 / WEIGHT_UNIT,
                                    sil[0:m, c, :], ALU.mult, ALU.mult).then_inc(hidden, 1)
                        if s >= 1:
                            ex = s - 1
                            dve.wait_ge(down_done, g * e + (ex + 3))
                            add_expert(core, dve, core.psum[6 + ex % 2], gates, g, ex, None, None, taken, x)


def typed_features_stage(core, w1, w2, b, R, skip, tag):
    nc = core.nc
    K = NODE_K
    KB = GW // D
    NB = K // KB
    with ExitStack() as own:
        def sb(name, shape):
            return own.enter_context(nc.sbuf_tensor(f"{tag}_{name}", shape, FP32))
        xg = sb("xg", [P, GW])
        nodeT = sb("nodeT", [K, GW])
        node = sb("node", [P, GT, K])
        prod = sb("prod", [P, K, D])
        gathered = core.sem(tag + "xg_ready")
        group_done = core.sem(tag + "group_done")
        small = core.sem(tag + "small_ready")
        nodeT_in = core.sem(tag + "nodeT_in")
        node_in = core.sem(tag + "node_in")
        skipped = core.sem(tag + "skip_sums")
        skip_in = core.sem(tag + "skip_in")
        hw_full = core.sem(tag + "hw_full")
        hw_read = core.sem(tag + "hw_read")
        ones = core.sem(tag + "ones")
        with nc.Block() as block:
            @block.gpsimd
            def _(pool):
                nc.gpsimd.memset(R[:, :, D:D + 1], 1.0).then_inc(ones, 1)
                with pool.Fori(0, G) as g:
                    pool.wait_ge(group_done, g + 1)
                    nc.gpsimd.tensor_copy(xg[:, :], core.xT[:, ds(g * GW, GW)]).then_inc(gathered, 1)
                pool.wait_ge(ones, 1)

            @block.tensor
            def _(pe):
                pe.sem_inc(group_done, 1)
                with pe.Fori(0, G) as g:
                    pe.wait_ge(gathered, g + 1)
                    pe.wait_ge(skip_in, g + 1)
                    pe.wait_ge(node_in, g + 1)
                    nc.tensor.matmul(core.psum[4][0:K, :], w1, xg[:, :], start=True, stop=True)
                    for r in range(GT):
                        last = nc.tensor.matmul(core.psum[5][:, r * K:(r + 1) * K], xg[:, r * P:(r + 1) * P],
                                                w1, start=True, stop=True)
                    last.then_inc(small, 1)
                    for r in range(GT):
                        for q in range(NB):
                            pe.wait_ge(hw_read, g * (GT * NB) + (r * NB + q + 1))
                            nc.tensor.matmul(core.psum[q][:, :], xg[:, r * P:(r + 1) * P],
                                             w2[:, q * GW:(q + 1) * GW], start=True,
                                             stop=True).then_inc(hw_full, 1)
                        if r == 0:
                            pe.wait_ge(nodeT_in, g + 1)
                            for rr in range(GT):
                                last = nc.tensor.matmul(core.psum[6][:, rr * P:(rr + 1) * P],
                                                        nodeT[:, rr * P:(rr + 1) * P], b, start=True, stop=True)
                            last.then_inc(skipped, 1)
                    pe.drain().then_inc(group_done, 1)

            @block.scalar
            def _(act):
                act.sem_inc(skip_in, 1)
                with act.Fori(0, G) as g:
                    act.wait_ge(small, g + 1)
                    nc.scalar.activation(nodeT[:, :], core.psum[4][0:K, :], ACT.Copy).then_inc(nodeT_in, 1)
                    act.wait_ge(skipped, g + 1)
                    nc.scalar.activation(skip[:, ds(g * GT, GT), :],
                                         core.psum[6][:, :].rearrange("p (r d) -> p r d", d=D),
                                         ACT.Copy).then_inc(skip_in, 1)

            @block.vector
            def _(dve):
                dve.sem_inc(node_in, 1)
                dve.sem_inc(hw_read, NB)
                with dve.Fori(0, G) as g:
                    dve.drain()
                    dve.wait_ge(small, g + 1)
                    nc.vector.tensor_copy(node[:, :, :], core.psum[5][:, 0:GT * K].rearrange(
                        "p (r k) -> p r k", k=K)).then_inc(node_in, 1)
                    dve.drain()
                    for r in range(GT):
                        for q in range(NB):
                            dve.wait_ge(hw_full, g * (GT * NB) + (r * NB + q + 1))
                            nc.vector.tensor_tensor(
                                prod[:, q * KB:(q + 1) * KB, :],
                                core.psum[q][:, :].rearrange("p (k d) -> p k d", d=D),
                                over(node[:, r, q * KB:(q + 1) * KB], D), ALU.mult).then_inc(hw_read, 1)
                        dve.drain()
                        nc.vector.tensor_reduce(R[:, ds(g * GT + r, 1), 0:D].rearrange("p a d -> p (a d)"),
                                                prod[:, :, :].rearrange("p k d -> p d k"), AX.X, ALU.add)
                        dve.drain()


def adj_product_stage(core, adjT, R, width, finish, tag):
    nc = core.nc
    B = 4
    with ExitStack() as own:
        at = own.enter_context(nc.sbuf_tensor(f"{tag}_at", [P, B, T * P], FP32))
        landed = [core.sem(f"{tag}at_landed{i}") for i in range(B)]
        used = [core.sem(f"{tag}at_used{i}") for i in range(B)]
        out_read = core.sem(tag + "out_read")
        src = adjT.rearrange("t p j i -> p t (j i)")
        with nc.Block() as block:
            @block.sync
            def _(sp):
                with sp.Fori(0, T // B) as it:
                    for q in range(B):
                        sp.wait_ge(used[q], it + 1)
                        sp.dma_start(at[:, q:q + 1, :],
                                     src[:, ds(it * B + q, 1), :]).then_inc(landed[q], 16)

            @block.tensor
            def _(pe):
                for q in range(B):
                    pe.sem_inc(used[q], 1)
                with pe.Fori(0, T // B) as it:
                    for q in range(B):
                        pe.wait_ge(landed[q], it * 16 + 16)
                        pe.wait_ge(out_read, it * B + (q + 1))
                        for j in range(T):
                            last = nc.tensor.matmul(core.psum[q % 2][:, 0:width],
                                                    at[:, q, j * P:(j + 1) * P], R[:, j, 0:width],
                                                    start=(j == 0), stop=(j == T - 1))
                        last.then_inc(used[q], 1)

            @block.vector
            def _(dve):
                dve.sem_inc(out_read, 2)
                with dve.Fori(0, T // B) as it:
                    for q in range(B):
                        dve.wait_ge(used[q], it + 2)
                        finish(dve, it * B + q, core.psum[q % 2], out_read)

def first_graph_layer(core, w):
    nc = core.nc
    with ExitStack() as own:
        R = own.enter_context(nc.sbuf_tensor("l0_R", [P, T, D + 1], FP32))
        skip = own.enter_context(nc.sbuf_tensor("l0_skip", [P, T, D], FP32))
        with ExitStack() as weights:
            w1 = weights.enter_context(nc.sbuf_tensor("l0_w1", [D, NODE_K], FP32))
            w2 = weights.enter_context(nc.sbuf_tensor("l0_w2", [D, NODE_K, D], FP32))
            b = weights.enter_context(nc.sbuf_tensor("l0_b", [NODE_K, D], FP32))
            norm_stage(core, [(w1[:, :], w["L0_gnn_W1"]),
                              (w2[:, :, :], w["L0_gnn_W2"].rearrange("k c f -> c k f")),
                              (b[:, :], w["L0_gnn_b"])], "l0g")
            typed_features_stage(core, w1[:, :], w2[:, :, :].rearrange("c k f -> c (k f)"), b[:, :], R, skip, "l0t")
        tmp = own.enter_context(nc.sbuf_tensor("l0_sum", [P, 1, D], FP32))

        def finish(dve, t, bank, out_read):
            nc.vector.tensor_tensor(tmp[:, :, :], bank[:, 0:D].unsqueeze(1), skip[:, ds(t, 1), :], ALU.add)
            nc.vector.tensor_scalar(core.deg[:, ds(t, 1)], bank[:, D:D + 1], 1.0, None,
                                    ALU.add).then_inc(out_read, 1)
            dve.drain()
            row = core.x[:, ds(t, 1), :]
            nc.vector.scalar_tensor_tensor(row, tmp[:, :, :], 0.0, row, ALU.max, ALU.add)
            dve.drain()

        adj_product_stage(core, w["adjT"], R, D + 1, finish, "l0a")


def first_expert_layer(core, w):
    nc = core.nc
    E, H = 8, 256
    with ExitStack() as own:
        def sb(name, shape):
            return own.enter_context(nc.sbuf_tensor("l0f_" + name, shape, FP32))

        def halves(name, n):
            return own.enter_context(nc.sbuf_tensor("l0f_" + name, [D, 2, n], FP16))
        wg, bg = sb("wg", [D, E]), sb("bg", [P, E])
        w1, b1 = sb("w1", [D, E, H]), sb("b1", [P, E, 2])
        w2, b2 = sb("w2", [P, E, 2, D]), sb("b2", [P, E, D])
        score, gates = sb("score", [P, T, E]), sb("gates", [P, T, E])
        norm_stage(core, [(wg[:, :], w["L0_ffn_Wg"]), (bg[:, :], w["L0_ffn_bg"].partition_broadcast(P)),
                          (w1[:, :, :], w["L0_ffn_W1"].rearrange("e d h -> d e h")),
                          (b1[:, :, :], w["L0_ffn_b1"]),
                          (w2[:, :, :, :], w["L0_ffn_W2"].rearrange("e (c h) d -> h e c d", h=P)),
                          (b2[:, :, :].rearrange("p e d -> p (e d)"),
                           w["L0_ffn_b2"].rearrange("e d -> (e d)").partition_broadcast(P))],
                   "l0n", (wg[:, :], bg[:, :], score[:, :, :]))
        xs, w1s = halves("xs", N), halves("w1s", E * H)
        splits = [(core.xT[:, :], xs, 1.0), (w1[:, :, :].rearrange("d e h -> d (e h)"), w1s, WEIGHT_UNIT)]
        gates_onehot(core, score, E, gates, splits, "l0gate")
        experts_gelu(core, E, xs, w1s, b1, w2, b2, gates, "l0e")


def third_expert_layer(core, w):
    nc = core.nc
    E, RH = 6, 64
    with ExitStack() as own:
        def sb(name, shape):
            return own.enter_context(nc.sbuf_tensor("l2f_" + name, shape, FP32))

        def halves(name, n):
            return own.enter_context(nc.sbuf_tensor("l2f_" + name, [D, 2, n], FP16))
        rw1, rb1, rw2, rb2 = sb("rw1", [D, RH]), sb("rb1", [RH, 1]), sb("rw2", [RH, E]), sb("rb2", [P, E])
        w1, w2, w3 = sb("w1", [D, E, D]), sb("w2", [D, E, D]), sb("w3", [D, E, D])
        b1, b2, b3 = sb("b1", [P, E]), sb("b2", [P, E]), sb("b3", [P, E, D])
        score, gates = sb("score", [P, T, E]), sb("gates", [P, T, E])
        rh = sb("rh", [RH, N])
        norm_stage(core, [(rw1[:, :], w["L2_ffn_router_w1"]), (rb1[:, :], w["L2_ffn_router_b1"].unsqueeze(1)),
                          (rw2[:, :], w["L2_ffn_router_w2"]), (rb2[:, :], w["L2_ffn_router_b2"].partition_broadcast(P)),
                          (w1[:, :, :], w["L2_ffn_expert_w1"].rearrange("e d h -> d e h")),
                          (w2[:, :, :], w["L2_ffn_expert_w2"].rearrange("e d h -> d e h")),
                          (w3[:, :, :], w["L2_ffn_expert_w3"].rearrange("e d h -> d e h")),
                          (b1[:, :], w["L2_ffn_expert_b1"]), (b2[:, :], w["L2_ffn_expert_b2"]),
                          (b3[:, :, :].rearrange("p e d -> p (e d)"),
                           w["L2_ffn_expert_b3"].rearrange("e d -> (e d)").partition_broadcast(P))], "l2n")
        sums, hidden, scored = core.sem("router_sums"), core.sem("router_hidden"), core.sem("router_scores")
        with nc.Block() as block:
            @block.tensor
            def _(pe):
                for g in range(G):
                    if g >= 4:
                        pe.wait_ge(hidden, g - 3)
                    nc.tensor.matmul(core.psum[g % 4][0:RH, :], rw1[:, :], core.xT[:, g * GW:(g + 1) * GW],
                                     start=True, stop=True).then_inc(sums, 1)
                pe.wait_ge(hidden, G)
                for t in range(T):
                    last = nc.tensor.matmul(core.psum[6][:, t * E:(t + 1) * E], rh[:, t * P:(t + 1) * P],
                                            rw2[:, :], start=True, stop=True)
                last.then_inc(scored, 1)

            @block.scalar
            def _(act):
                for g in range(G):
                    act.wait_ge(sums, g + 1)
                    nc.scalar.activation(rh[:, g * GW:(g + 1) * GW], core.psum[g % 4][0:RH, :], ACT.Relu,
                                         bias=rb1[:, 0:1]).then_inc(hidden, 1)

            @block.vector
            def _(dve):
                dve.wait_ge(scored, 1)
                nc.vector.tensor_tensor(score[:, :, :], core.psum[6][:, 0:T * E].rearrange("p (t e) -> p t e", e=E),
                                        rows(rb2[:, :], T), ALU.add)
        xs, w1s = halves("xs", N), halves("w1s", E * D)
        splits = [(core.xT[:, :], xs, 1.0), (w1[:, :, :].rearrange("d e h -> d (e h)"), w1s, WEIGHT_UNIT)]
        gates_softmax(core, score, E, gates, False, splits, "l2gate")
        experts_deep(core, E, xs, w1s, b1, w2, b2, w3, b3, gates, "l2e")


def fourth_expert_layer(core, w):
    nc = core.nc
    E, H = 8, 341
    chunks = [(lo, min(P, H - lo)) for lo in range(0, H, P)]
    with ExitStack() as own:
        def sb(name, shape):
            return own.enter_context(nc.sbuf_tensor("l3f_" + name, shape, FP32))

        def halves(name, n):
            return own.enter_context(nc.sbuf_tensor("l3f_" + name, [D, 2, n], FP16))
        rw = sb("rw", [D, E])
        w1, w3 = sb("w1", [D, E, H]), sb("w3", [D, E, H])
        w2 = sb("w2", [P, E, len(chunks), D])
        score, gates = sb("score", [P, T, E]), sb("gates", [P, T, E])
        norm_stage(core, [(rw[:, :], w["L3_ffn_router_w"]),
                          (w1[:, :, :], w["L3_ffn_w1"]), (w3[:, :, :], w["L3_ffn_w3"])] +
                   [(w2[0:m, :, c, :], w["L3_ffn_w2"][lo:lo + m, :, :]) for c, (lo, m) in enumerate(chunks)],
                   "l3n", (rw[:, :], None, score[:, :, :]))
        xs, w1s, w3s = halves("xs", N), halves("w1s", E * H), halves("w3s", E * H)
        splits = [(core.xT[:, :], xs, 1.0), (w1[:, :, :].rearrange("d e h -> d (e h)"), w1s, WEIGHT_UNIT),
                  (w3[:, :, :].rearrange("d e h -> d (e h)"), w3s, WEIGHT_UNIT)]
        gates_softmax(core, score, E, gates, True, splits, "l3gate")
        experts_swiglu(core, E, chunks, xs, w1s, w3s, w2, gates, "l3e")


def fourth_graph_layer(core, w):
    nc = core.nc
    with ExitStack() as own:
        def sb(name, shape):
            return own.enter_context(nc.sbuf_tensor("l3g_" + name, shape, FP32))
        R, w_, b = sb("R", [P, T, D]), sb("w", [D, D]), sb("b", [P, D])
        dinv, live, tmp = sb("dinv", [P, T]), sb("live", [P, T]), sb("tmp", [P, 1, D])
        norm_stage(core, [(w_[:, :], w["L3_gnn_W"]), (b[:, :], w["L3_gnn_b"].partition_broadcast(P))], "l3g")
        safe, rooted = core.sem("deg_safe"), core.sem("deg_rooted")
        made, taken = core.sem("support_made"), core.sem("support_taken")
        with nc.Block() as block:
            @block.tensor
            def _(pe):
                for g in range(G):
                    if g >= 4:
                        pe.wait_ge(taken, g - 3)
                    for r in range(GT):
                        t = g * GT + r
                        last = nc.tensor.matmul(core.psum[g % 4][:, r * P:(r + 1) * P],
                                                core.xT[:, t * P:(t + 1) * P], w_[:, :], start=True, stop=True)
                    last.then_inc(made, 1)

            @block.vector
            def _(dve):
                nc.vector.tensor_scalar(live[:, :], core.deg[:, :], 0.0, None, ALU.not_equal)
                dve.drain()
                nc.vector.scalar_tensor_tensor(dinv[:, :], live[:, :], -1.0, core.deg[:, :], ALU.mult, ALU.add)
                dve.drain()
                nc.vector.tensor_scalar(dinv[:, :], dinv[:, :], 1.0, None, ALU.add).then_inc(safe, 1)
                dve.wait_ge(rooted, 1)
                nc.vector.reciprocal(dinv[:, :], dinv[:, :])
                dve.drain()
                nc.vector.tensor_tensor(dinv[:, :], dinv[:, :], live[:, :], ALU.mult)
                dve.drain()
                for g in range(G):
                    a = slice(g * GT, (g + 1) * GT)
                    dve.wait_ge(made, g + 1)
                    nc.vector.tensor_tensor(R[:, a, :], core.psum[g % 4][:, :].rearrange("p (r d) -> p r d", d=D),
                                            rows(b[:, :], GT), ALU.add).then_inc(taken, 1)
                    dve.drain()
                    nc.vector.tensor_tensor(R[:, a, :], R[:, a, :], over(dinv[:, a], D), ALU.mult)

            @block.scalar
            def _(act):
                act.wait_ge(safe, 1)
                nc.scalar.activation(dinv[:, :], dinv[:, :], ACT.Sqrt).then_inc(rooted, 1)

        def finish(dve, t, bank, out_read):
            nc.vector.tensor_tensor(tmp[:, :, :], bank[:, 0:D].unsqueeze(1), R[:, ds(t, 1), :],
                                    ALU.add).then_inc(out_read, 1)
            dve.drain()
            row = core.x[:, ds(t, 1), :]
            nc.vector.scalar_tensor_tensor(row, tmp[:, :, :], dinv[:, ds(t, 1)], row, ALU.mult, ALU.add)
            dve.drain()

        adj_product_stage(core, w["adjT"], R, D, finish, "l3a")

def row_attention_stage(core, kind, adj, row, own, R, tag):
    nc = core.nc
    leaky = kind == "leaky"
    AB, LB, NB, LAG, BANKS = 4, 2, T // GT, 2, 4
    HALF = N // 2
    with ExitStack() as mine:
        def sb(name, shape):
            return mine.enter_context(nc.sbuf_tensor(f"{tag}_{name}", shape, FP32))
        A, L, PT = sb("A", [P, AB, N]), sb("L", [P, LB, N]), sb("PT", [P, NB, GW])
        top, c1, c2, c3 = (sb(name, [P, AB]) for name in ("top", "c1", "c2", "c3"))
        den = sb("den", [P, 2])
        if not leaky:
            mask = mine.enter_context(nc.sbuf_tensor(tag + "_mask", [P, 2, N], BF16))
        landed = [core.sem(f"{tag}landed{i}") for i in range(AB)]
        a_used = [core.sem(f"{tag}a_used{i}") for i in range(AB)]
        mask_made = core.sem(tag + "mask_made")
        rows_scaled = core.sem(tag + "rows_scaled")
        masked = core.sem(tag + "masked")
        b_done = core.sem(tag + "b_done")
        raised = core.sem(tag + "raised")
        pool_used = core.sem(tag + "pool_used")
        l_ready = core.sem(tag + "l_ready")
        l_free = core.sem(tag + "l_free")
        turned = core.sem(tag + "turned")
        copied = core.sem(tag + "copied")
        used = core.sem(tag + "used")
        out_full = core.sem(tag + "out_full")
        out_read = core.sem(tag + "out_read")
        src = adj.rearrange("(t p) j -> p t j", p=P)
        with nc.Block() as block:
            @block.sync
            def _(sp):
                with sp.Fori(0, T // AB) as it:
                    for q in range(AB):
                        sp.wait_ge(a_used[q], it * 2 + 2)
                        sp.dma_start(A[:, q:q + 1, :], src[:, ds(it * AB + q, 1), :]).then_inc(landed[q], 16)

            @block.vector
            def _(dve):
                for q in range(AB):
                    dve.sem_inc(a_used[q], 2)
                dve.sem_inc(out_read, 2)

                def stage_a(it, q):
                    t, l = it * AB + q, q % LB
                    a = A[:, q, :]
                    if leaky:
                        dve.wait_ge(landed[q], it * 16 + 16)
                        diag = A[:, q:q + 1, ds(t * P, P)]
                        nc.vector.tensor_tensor(diag, diag, core.ident[:, :].unsqueeze(1), ALU.max)
                        dve.drain()
                        nc.vector.tensor_scalar(a, a, 0.0, -BIG, ALU.is_le, ALU.mult)
                        dve.drain()
                        nc.vector.tensor_tensor_reduce(a, a, row[:, :], 1.0, -3.0 * BIG, ALU.add, ALU.max,
                                                       top[:, q:q + 1])
                        dve.drain()
                        nc.vector.tensor_tensor(top[:, q:q + 1], top[:, q:q + 1], own[:, ds(t, 1)], ALU.add)
                        dve.drain()
                        nc.vector.scalar_tensor_tensor(c1[:, q:q + 1], top[:, q:q + 1], 0.2, top[:, q:q + 1],
                                                       ALU.mult, ALU.max)
                        dve.drain()
                        nc.vector.scalar_tensor_tensor(c2[:, q:q + 1], own[:, ds(t, 1)], 0.2, c1[:, q:q + 1],
                                                       ALU.mult, ALU.subtract)
                        nc.vector.tensor_scalar(c3[:, q:q + 1], own[:, ds(t, 1)], 0.8, None, ALU.mult)
                        dve.drain()
                        nc.vector.tensor_tensor(c1[:, q:q + 1], own[:, ds(t, 1)], c1[:, q:q + 1],
                                                ALU.subtract).then_inc(masked, 1)
                    else:
                        dve.wait_ge(rows_scaled, t + 1)
                        dve.wait_ge(l_free, t + 1)
                        nc.vector.memset(top[:, q:q + 1], 0.0)
                        dve.drain()
                        nc.vector.tensor_tensor_reduce(L[:, l, :], a, mask[:, q % 2, :], 1.0, -3.0 * BIG, ALU.add,
                                                       ALU.max, top[:, q:q + 1])
                        dve.drain()
                        nc.vector.tensor_scalar(c1[:, q:q + 1], top[:, q:q + 1], -0.1 * BIG, -1.0, ALU.max,
                                                ALU.mult).then_inc(masked, 1)
                        dve.sem_inc(a_used[q], 2)

                def make_mask(it, q):
                    dve.wait_ge(landed[q], it * 16 + 16)
                    nc.vector.tensor_scalar(mask[:, q % 2, :], A[:, q, :], 0.0, -BIG, ALU.is_equal, ALU.mult)
                    dve.drain().then_inc(mask_made, 1)

                def stage_c(it, q):
                    t, l = it * AB + q, q % LB
                    dve.wait_ge(b_done, t + 1)
                    nc.vector.scalar_tensor_tensor(L[:, l, 0:HALF], A[:, q, 0:HALF], c1[:, q:q + 1], L[:, l, 0:HALF],
                                                   ALU.add, ALU.max).then_inc(l_ready, 1)
                    dve.drain().then_inc(a_used[q], 1)

                def stage_o(t, parity):
                    bank, d = core.psum[6 + parity], den[:, parity:parity + 1]
                    dve.wait_ge(out_full, t + 1)
                    if leaky:
                        nc.vector.reciprocal(d, bank[:, D:D + 1])
                    else:
                        nc.vector.tensor_scalar(d, bank[:, D:D + 1], 0.0, None, ALU.is_le)
                        dve.drain()
                        nc.vector.tensor_tensor(d, d, bank[:, D:D + 1], ALU.add)
                        dve.drain()
                        nc.vector.reciprocal(d, d)
                    dve.drain()
                    xt = core.x[:, ds(t, 1), :]
                    nc.vector.scalar_tensor_tensor(xt, bank[:, 0:D].unsqueeze(1), d, xt, ALU.mult,
                                                   ALU.add).then_inc(out_read, 1)
                    dve.drain()

                def tiles(it, first, last):
                    for q in range(AB):
                        t = it * AB + q
                        out = not (first and q < 2)
                        if out and not leaky:
                            stage_o(t - 2, q % 2)
                        if not leaky and not (last and q >= AB - 2):
                            make_mask(it if q < AB - 2 else it + 1, (q + 2) % AB)
                        if not (last and q == AB - 1):
                            stage_a(it if q < AB - 1 else it + 1, (q + 1) % AB)
                        if leaky:
                            stage_c(it, q)
                            if out:
                                stage_o(t - 2, q % 2)

                if not leaky:
                    make_mask(0, 0)
                    make_mask(0, 1)
                stage_a(0, 0)
                tiles(0, True, False)
                with dve.Fori(1, T // AB - 1) as it:
                    tiles(it, False, False)
                tiles(T // AB - 1, False, True)
                for t in (T - 2, T - 1):
                    stage_o(t, t % 2)

            @block.gpsimd
            def _(pool):
                if leaky:
                    with pool.Fori(0, T // AB) as it:
                        for q in range(AB):
                            pool.wait_ge(b_done, it * AB + (q + 1))
                            pool.wait_ge(raised, it * AB + (q + 1))
                            half = L[:, q % LB, HALF:N]
                            nc.gpsimd.tensor_tensor(half, A[:, q, HALF:N], half, ALU.add).then_inc(pool_used, 1)
                            pool.drain().then_inc(a_used[q], 1)
                else:
                    with pool.Fori(0, T // AB) as it:
                        for q in range(AB):
                            pool.wait_ge(mask_made, it * AB + (q + 1))
                            nc.gpsimd.tensor_tensor(A[:, q, :], A[:, q, :], row[:, :],
                                                    ALU.mult).then_inc(rows_scaled, 1)

            @block.scalar
            def _(act):
                act.sem_inc(copied, BANKS)

                PIECES = 1 if leaky else 4

                def stage_b(it, q, piece=None):
                    t, l = it * AB + q, q % LB
                    if leaky:
                        act.wait_ge(masked, t + 1)
                        act.wait_ge(l_free, t + 1)
                        nc.scalar.activation(L[:, l, :], A[:, q, :], ACT.Identity, bias=c2[:, q:q + 1],
                                             scale=0.2).then_inc(b_done, 1)
                    else:
                        act.wait_ge(masked, t + 1)
                        part = L[:, l, piece * N // PIECES:(piece + 1) * N // PIECES]
                        last = nc.scalar.activation(part, part, ACT.Exp, bias=c1[:, q:q + 1])
                        if piece == PIECES - 1:
                            last.then_inc(b_done, 1)

                def raise_half(it, q):
                    act.wait_ge(b_done, it * AB + (q + 1))
                    nc.scalar.activation(A[:, q, HALF:N], A[:, q, HALF:N], ACT.Relu, scale=0.8,
                                         bias=c3[:, q:q + 1]).then_inc(raised, 1)

                def tiles(it, last):
                    for q in range(AB):
                        coming = (it if q < AB - 1 else it + 1, (q + 1) % AB)
                        ahead = not (last and q == AB - 1)
                        if leaky and ahead:
                            stage_b(*coming)
                        for b in range(NB):
                            n = (it * AB + q) * NB + b
                            act.wait_ge(turned, n + 1)
                            act.wait_ge(used, n + 1)
                            nc.scalar.activation(PT[:, b, :], core.psum[b % BANKS][:, :],
                                                 ACT.Exp if leaky else ACT.Copy).then_inc(copied, 1)
                            if leaky and ahead and b == NB // 2 - 1:
                                raise_half(*coming)
                            piece = b - (NB - 1 - PIECES)
                            if not leaky and ahead and 0 <= piece < PIECES:
                                stage_b(*coming, piece)

                for piece in range(PIECES):
                    stage_b(0, 0, piece)
                if leaky:
                    raise_half(0, 0)
                with act.Fori(0, T // AB - 1) as it:
                    tiles(it, False)
                tiles(T // AB - 1, True)

            @block.tensor
            def _(pe):
                pe.sem_inc(l_free, LB)
                pe.sem_inc(used, NB)
                with pe.Fori(0, T // AB) as it:
                    steps = [(q, b) for q in range(AB) for b in range(NB)]
                    for s in range(len(steps) + LAG):
                        if s < len(steps):
                            q, b = steps[s]
                            t = it * AB + q
                            if b == 0:
                                pe.wait_ge(l_ready if leaky else b_done, t + 1)
                                if leaky:
                                    pe.wait_ge(pool_used, t + 1)
                            pe.wait_ge(copied, t * NB + (b + 1))
                            for r in range(GT):
                                j = b * GT + r
                                last = nc.tensor.transpose(core.psum[b % BANKS][:, r * P:(r + 1) * P],
                                                           L[:, q % LB, j * P:(j + 1) * P], core.ident[:, :])
                            last.then_inc(turned, 1)
                            if b == NB - 1:
                                pe.wait_ge(turned, t * NB + NB)
                                pe.sem_inc(l_free, 1)
                        if s >= LAG:
                            q, b = steps[s - LAG]
                            t = it * AB + q
                            if b == 0:
                                pe.wait_ge(out_read, t + 1)
                            pe.wait_ge(copied, t * NB + (b + 1 + BANKS))
                            for r in range(GT):
                                j = b * GT + r
                                last = nc.tensor.matmul(core.psum[6 + q % 2][:, 0:D + 1],
                                                        PT[:, b, r * P:(r + 1) * P], R[:, j, :],
                                                        start=(j == 0), stop=(j == T - 1))
                            last.then_inc(used, 1)
                            if b == NB - 1:
                                pe.wait_ge(used, t * NB + 2 * NB)
                                pe.sem_inc(out_full, 1)


def replicate(nc, dve, rep, col):
    nc.vector.memset(rep, 1.0)
    dve.drain()
    nc.vector.tensor_scalar(rep, rep, col, None, ALU.mult)


def second_graph_layer(core, w):
    nc = core.nc
    with ExitStack() as mine:
        def sb(name, shape):
            return mine.enter_context(nc.sbuf_tensor("l1g_" + name, shape, FP32))
        R, own = sb("R", [P, T, D + 1]), sb("own", [P, T])
        with ExitStack() as inner:
            def sbi(name, shape):
                return inner.enter_context(nc.sbuf_tensor("l1g_" + name, shape, FP32))
            w_, a, rep, WhT = sbi("w", [D, D]), sbi("a", [D, 2]), sbi("rep", [D, P]), sbi("WhT", [P, 2, GW])
            norm_stage(core, [(w_[:, :], w["L1_gnn_W"]), (a[:, :], w["L1_gnn_a"])], "l1g")
            made, taken, whT_in = core.sem("wh_made"), core.sem("wh_taken"), core.sem("whT_in")
            dst_made, dst_in, rep_ready = core.sem("dst_made"), core.sem("dst_in"), core.sem("rep_ready")
            with nc.Block() as block:
                @block.gpsimd
                def _(pool):
                    nc.gpsimd.memset(R[:, :, D:D + 1], 1.0)

                @block.tensor
                def _(pe):
                    pe.wait_ge(rep_ready, 1)
                    for g in range(G):
                        cols = core.xT[:, g * GW:(g + 1) * GW]
                        if g >= 2:
                            pe.wait_ge(taken, g - 1)
                            pe.wait_ge(whT_in, g - 1)
                            pe.wait_ge(dst_in, g - 1)
                        for r in range(GT):
                            nc.tensor.matmul(core.psum[g % 2][:, r * P:(r + 1) * P],
                                             core.xT[:, (g * GT + r) * P:(g * GT + r + 1) * P], w_[:, :],
                                             start=True, stop=True)
                        nc.tensor.matmul(core.psum[2 + g % 2][:, :], w_[:, :], cols, start=True,
                                         stop=True).then_inc(made, 1)
                        pe.wait_ge(whT_in, g + 1)
                        for r in range(GT):
                            nc.tensor.matmul(core.psum[6][:, g * GT + r:g * GT + r + 1],
                                             WhT[:, g % 2, r * P:(r + 1) * P], a[:, 0:1], start=True, stop=True)
                        nc.tensor.matmul(core.psum[4 + g % 2][:, :], rep[:, :], WhT[:, g % 2, :], start=True,
                                         stop=True).then_inc(dst_made, 1)

                @block.scalar
                def _(act):
                    for g in range(G):
                        act.wait_ge(made, g + 1)
                        if g >= 2:
                            act.wait_ge(dst_made, g - 1)
                        nc.scalar.activation(WhT[:, g % 2, :], core.psum[2 + g % 2][:, :],
                                             ACT.Copy).then_inc(whT_in, 1)
                        act.wait_ge(dst_made, g + 1)
                        nc.scalar.activation(core.xT[:, g * GW:(g + 1) * GW], core.psum[4 + g % 2][:, :],
                                             ACT.Copy).then_inc(dst_in, 1)

                @block.vector
                def _(dve):
                    replicate(nc, dve, rep[:, :], a[:, 1:2])
                    dve.drain().then_inc(rep_ready, 1)
                    for g in range(G):
                        dve.wait_ge(made, g + 1)
                        nc.vector.tensor_copy(R[:, g * GT:(g + 1) * GT, 0:D],
                                              core.psum[g % 2][:, :].rearrange("p (r d) -> p r d", d=D)).then_inc(taken, 1)
                    dve.wait_ge(dst_made, G)
                    nc.vector.tensor_copy(own[:, :], core.psum[6][:, 0:T])
        row_attention_stage(core, "leaky", w["adj"], core.xT, own, R, "l1a")


def third_graph_layer(core, w):
    nc = core.nc
    with ExitStack() as mine:
        R = mine.enter_context(nc.sbuf_tensor("l2g_R", [P, T, D + 1], FP32))
        with ExitStack() as inner:
            hv = inner.enter_context(nc.sbuf_tensor("l2g_hv", [D, 1], FP32))
            rep = inner.enter_context(nc.sbuf_tensor("l2g_rep", [D, P], FP32))
            norm_stage(core, [(hv[:, :], w["L2_gnn_H_v"])], "l2g")
            made, row_in, rep_ready = core.sem("row_made"), core.sem("row_in"), core.sem("rep_ready")
            with nc.Block() as block:
                @block.gpsimd
                def _(pool):
                    nc.gpsimd.memset(R[:, :, D:D + 1], 1.0)

                @block.tensor
                def _(pe):
                    pe.wait_ge(rep_ready, 1)
                    for g in range(G):
                        if g >= 4:
                            pe.wait_ge(row_in, g - 3)
                        nc.tensor.matmul(core.psum[g % 4][:, :], rep[:, :], core.xT[:, g * GW:(g + 1) * GW],
                                         start=True, stop=True).then_inc(made, 1)

                @block.scalar
                def _(act):
                    for g in range(G):
                        act.wait_ge(made, g + 1)
                        nc.scalar.activation(core.xT[:, g * GW:(g + 1) * GW], core.psum[g % 4][:, :],
                                             ACT.Copy).then_inc(row_in, 1)

                @block.vector
                def _(dve):
                    replicate(nc, dve, rep[:, :], hv[:, 0:1])
                    dve.drain().then_inc(rep_ready, 1)
                    nc.vector.tensor_copy(R[:, :, 0:D], core.xn[:, :, :])
        row_attention_stage(core, "scaled", w["adj"], core.xT, None, R, "l2a")

HEADS, QS, HD = 4, 4, 32
ROOT = float(HD) ** 0.5
STACK = 3 * HD
EPS_HEAD = 1e-8
MASKED, MASK_UNIT = -60000.0, 64.0
VW = 3 * HD + 1
SLOTS = 8
FIRST_LEAD, FULL_LEAD = 22, 42
TURN_LAG = 4
PAIRS = QS * G * (G + 1)
DELAY = 6


def norm_rows(nc, dve, src, out, sq, mean, var, width, eps, var_ready, std_ready, turn):
    nc.vector.tensor_reduce(mean, src, AX.X, ALU.add)
    dve.drain()
    nc.vector.tensor_scalar(mean, mean, 1.0 / width, None, ALU.mult)
    dve.drain()
    nc.vector.tensor_tensor(out, src, over(mean, width), ALU.subtract)
    dve.drain()
    nc.vector.tensor_tensor(sq, out, out, ALU.mult)
    dve.drain()
    nc.vector.tensor_reduce(var, sq, AX.X, ALU.add)
    dve.drain()
    nc.vector.tensor_scalar(var, var, 1.0 / width, eps, ALU.mult, ALU.add).then_inc(var_ready, 1)
    dve.wait_ge(std_ready, turn)
    nc.vector.reciprocal(var, var)
    dve.drain()
    nc.vector.tensor_tensor(out, out, over(var, width), ALU.mult)
    dve.drain()


def softmax_rows(nc, dve, src, stat, shifted, exped, turn):
    nc.vector.tensor_reduce(stat, src, AX.X, ALU.max)
    dve.drain()
    nc.vector.tensor_tensor(src, src, over(stat, 4), ALU.subtract).then_inc(shifted, 1)
    dve.wait_ge(exped, turn)
    nc.vector.tensor_reduce(stat, src, AX.X, ALU.add)
    dve.drain()
    nc.vector.reciprocal(stat, stat)
    dve.drain()
    nc.vector.tensor_tensor(src, src, over(stat, 4), ALU.mult)
    dve.drain()


class HeadTiles:

    def __init__(self, core, own):
        nc = core.nc

        def sb(name, shape, dt=FP32):
            return own.enter_context(nc.sbuf_tensor("l1f_" + name, shape, dt))
        self.hlw, self.hlb = sb("hlw", [D, HEADS, HD]), sb("hlb", [STACK, HEADS])
        self.wq, self.wk = sb("wq", [STACK, HEADS, QS, HD]), sb("wk", [STACK, HEADS, HD])
        self.wqs = sb("wqs", [STACK, HEADS, QS, 3, HD], FP16)
        self.wks = sb("wks", [STACK, HEADS, 3, HD], FP16)
        self.wv = sb("wv", [HD, HEADS, HD])
        self.gw, self.gb = sb("gw", [P, HEADS, QS]), sb("gb", [P, HEADS, QS])
        self.lng, self.lnb = sb("lng", [P, HD]), sb("lnb", [P, HD])
        self.hlw_n, self.hlb_n = sb("hlw_n", [D, 3, HD]), sb("hlb_n", [STACK, 1])
        self.wvi_n = sb("wvi_n", [HD, 2 * HD])
        self.sxT = sb("sxT", [HD, 2, GW])
        self.sxs = sb("sxs", [STACK, 2, GW], FP16)
        self.qT = sb("qT", [STACK + 3, QS, N], FP16)
        self.kT = sb("kT", [STACK + 3, N], FP16)
        self.V = sb("V", [P, T, VW], BF16)
        self.v32 = sb("v32", [P, 2, GT, HD])
        self.sx = sb("sx", [P, T, HD])
        self.PT = sb("PT", [P, SLOTS, 2, GW])
        self.Phigh = self.PT[:, :, :, :].rearrange("p s j q -> p (s j q)").bitcast(BF16).rearrange(
            "p (s j q two) -> p s j q two", s=SLOTS, j=2, two=2)[:, :, :, :, 1]
        self.Plow = sb("Plow", [P, SLOTS, 2, GW], FP16)
        self.oT = sb("oT", [VW, 2, GW])
        self.pick = sb("pick", [VW, HD + 1])
        self.pm, self.nm, self.nd = sb("pm", [P, GT, G]), sb("nm", [P, GT]), sb("nd", [P, GT])
        self.m3 = sb("m3", [P, 2, GT, 3], FP16)
        self.rec = sb("rec", [P, GT])
        self.at = core.xn
        self.atT = sb("atT", [P, 2, GW])
        self.gs, self.stat = sb("gs", [P, T, QS]), sb("stat", [P, T])
        self.mean, self.var = sb("mean", [P, T]), sb("var", [P, T])
        self.hn, self.tmp = sb("hn", [P, T, HD]), sb("tmp", [P, T, HD])
        self.fx = sb("fx", [P, T, D])
        self.tri, self.triT = sb("tri", [P, P], FP16), sb("triT", [P, P], FP16)
        self.unit = sb("unit", [P, P], FP16)


def attention_constants(core, h):
    nc = core.nc
    filled = core.sem("mask_filled")
    with nc.Block() as block:
        @block.gpsimd
        def _(pool):
            nc.gpsimd.memset(h.tri[:, :], 0.0).then_inc(filled, 1)
            nc.gpsimd.memset(h.triT[:, :], 0.0).then_inc(filled, 1)
            nc.gpsimd.memset(h.unit[:, :], 0.0).then_inc(filled, 1)
            nc.gpsimd.memset(h.V[:, :, 3 * HD:VW], 1.0).then_inc(filled, 1)
            pool.wait_ge(filled, 4)
            nc.gpsimd.memset(h.kT[STACK:STACK + 3, :], 1.0).then_inc(filled, 1)
            pool.wait_ge(filled, 5)
            nc.gpsimd.affine_select(out=h.tri[:, :], in_=h.tri[:, :], compare_op=ALU.is_ge, fill=MASKED,
                                    base=0, pattern=[[-1, P]], channel_multiplier=1)
            nc.gpsimd.affine_select(out=h.triT[:, :], in_=h.triT[:, :], compare_op=ALU.is_ge, fill=MASKED,
                                    base=0, pattern=[[1, P]], channel_multiplier=-1)
            nc.gpsimd.affine_select(out=h.unit[:, :], in_=h.unit[:, :], compare_op=ALU.not_equal, fill=MASK_UNIT,
                                    base=0, pattern=[[-1, P]], channel_multiplier=1)

        @block.vector
        def _(dve):
            nc.vector.memset(h.pick[:, :], 0.0)
            dve.drain()
            for k in range(3):
                nc.vector.tensor_copy(h.pick[k * HD:(k + 1) * HD, 0:HD], core.ident[0:HD, 0:HD])
            nc.vector.memset(h.pick[3 * HD:VW, HD:HD + 1], 1.0)


class Schedule:

    def __init__(self):
        units = [(e, sg) for e in range(QS) for sg in range(G)]
        blocks = [("M", u, r, c) for u, (e, sg) in enumerate(units) for r in range(GT) for c in range(sg + 1)]
        ends = {}
        for n, x in enumerate(blocks):
            ends[x[1]] = n + 1
        ev, waiting, k, m, turned = [], [], 0, 0, 0
        self.gate = []

        def maxima(upto):
            nonlocal m, turned
            while m < min(upto, len(blocks)):
                ev.append(blocks[m])
                m += 1
                if turned < len(units) and m >= min(ends[turned] + TURN_LAG, len(blocks)):
                    ev.append(("T", turned))
                    turned += 1

        maxima(FIRST_LEAD)
        for u, (e, sg) in enumerate(units):
            for p in range(2 * sg + 2):
                if p == 0:
                    maxima(ends[u])
                    while turned <= u:
                        ev.append(("T", turned))
                        turned += 1
                ev.append(("E", u, p))
                waiting.append(("A", u, p, k))
                k += 1
                goal = 2 * k + min(FULL_LEAD, FIRST_LEAD + k // 2)
                maxima(goal - 1)
                if len(waiting) > DELAY:
                    self._close(ev, waiting.pop(0), units)
                maxima(goal)
        while waiting:
            self._close(ev, waiting.pop(0), units)
        if self.owed is not None:
            self._turn_back(ev, units)
        ev += self.gate
        self.events, self.units, self.pairs = ev, units, k
        self.m_blocks = sum(1 for x in ev if x[0] == "M")
        self.users = [x for x in ev if x[0] in "MTOGH"]
        self.turn = {x: n for n, x in enumerate(self.users)}
        self.rank = {}
        seen = dict.fromkeys("MTOGH", 0)
        for x in self.users:
            seen[x[0]] += 1
            self.rank[x] = seen[x[0]]

        todo = [x for x in ev if x[0] == "A" and not residual_on_pool(x[3])]
        self.dve_events, scored = [], 0
        for x in ev:
            scored += x[0] == "E"
            while todo and (todo[0][3] < scored - 3 or x == todo[0]):
                self.dve_events.append(("R",) + todo.pop(0)[1:])
            self.dve_events.append(x)
        for n in range(len(self.dve_events) - 2, -1, -1):
            here, behind = self.dve_events[n:n + 2]
            if here[0] == "O" and behind[0] == "M":
                self.dve_events[n:n + 2] = [behind, here]

    owed = None

    def _turn_back(self, ev, units):
        ev.append(("O", self.owed))
        if units[self.owed][0] == QS - 1:
            self.gate += [("G", self.owed), ("H", self.owed)]
        self.owed = None

    def _close(self, ev, a, units):
        ev.append(a)
        _, u, p, _k = a
        if self.gate:
            ev.append(self.gate.pop(0))
        if self.owed is not None and (p >= 1):
            self._turn_back(ev, units)
        if p == 2 * units[u][1] + 1:
            self.owed = u


def residual_on_pool(k):
    return k % 2 == 0 if k >= PAIRS - FULL_LEAD // 2 else k % 5 != 4


def pair_parts(sg, p):
    if 2 * p + 1 < GT * sg:
        return [(slice(0, 2), 0)]
    return [(slice(jj, jj + 1), max(0, 2 * p + jj - GT * sg) * P) for jj in range(2)]


def heads_stage(core, h):
    nc = core.nc
    sch = Schedule()
    NM, NE, NU = sch.m_blocks, sch.pairs, len(sch.units)
    NPOOL = sum(1 for k in range(NE) if residual_on_pool(k))
    MB = (4, 5, 6)
    U = G * (QS + 1)
    s = {n: core.sem("l1h_" + n) for n in
         ("w_ready", "sx_sums", "sx_high", "sx_split", "qk_sums", "qk_high", "qk_split", "v_sums", "v_in", "m_full", "m_read",
          "m3_ready", "mt_full", "mt_read", "s_full", "exped", "low_pool", "low_dve", "pv_done", "oT_full", "oT_in",
          "po_full", "po_read", "at_ready", "at_turned", "at_copied", "gate_sums", "gate_read", "shifted", "gs_exp", "var_ready",
          "std_ready", "low_dve_free")}
    ring_bank = lambda x: core.psum[MB[sch.turn[x] % len(MB)]]

    with nc.Block() as block:
        @block.tensor
        def _(pe):
            pe.sem_inc(s["pv_done"], SLOTS)
            pe.sem_inc(s["po_full"], 2)
            with pe.Fori(0, HEADS) as n:
                pe.wait_ge(s["w_ready"], n + 1)

                def project_sx(g):
                    if g >= 2:
                        pe.wait_ge(s["sx_split"], n * G + (g - 1))
                    nc.tensor.matmul(core.psum[5 + g % 2][0:STACK, :], h.hlw_n[:, :, :].rearrange("p e o -> p (e o)"),
                                     core.xT[:, g * GW:(g + 1) * GW], start=True, stop=True).then_inc(s["sx_sums"], 1)

                project_sx(0)
                for g in range(G):
                    if g + 1 < G:
                        project_sx(g + 1)
                    pe.wait_ge(s["sx_split"], n * G + (g + 1))
                    for e in range(QS + 1):
                        u = g * (QS + 1) + e
                        if g >= 1:
                            pe.wait_ge(s["qk_split"], n * U + (u - QS))
                        w = h.wqs[:, ds(n, 1), e, :, :] if e < QS else h.wks[:, ds(n, 1), :, :]
                        nc.tensor.matmul(core.psum[e][0:STACK, :], w.rearrange("r a k o -> r (a k o)"),
                                         h.sxs[:, g % 2, :], start=True, stop=True).then_inc(s["qk_sums"], 1)
                    if g >= 1:
                        pe.wait_ge(s["v_in"], n * G + g)
                    for r in range(GT):
                        last = nc.tensor.matmul(core.psum[7][:, r * 2 * HD:(r + 1) * 2 * HD],
                                                h.sxT[0:HD, g % 2, r * P:(r + 1) * P], h.wvi_n[:, :],
                                                start=True, stop=True)
                    last.then_inc(s["v_sums"], 1)
                pe.wait_ge(s["qk_split"], n * U + U)
                pe.wait_ge(s["v_in"], n * G + G)

                def ring_wait(x):
                    t = sch.turn[x]
                    if t >= len(MB):
                        old = sch.users[t - len(MB)]
                        per, sem = {"M": (NM, s["m_read"]), "T": (NU, s["mt_read"]), "O": (NU, s["po_read"]),
                                    "G": (G, s["at_copied"]), "H": (G, s["gate_read"])}[old[0]]
                        pe.wait_ge(sem, n * per + sch.rank[old])
                    return ring_bank(x)

                for x in sch.events:
                    e, sg = sch.units[x[1]]
                    if x[0] == "M":
                        _, u, r, c = x
                        bank = ring_wait(x)
                        width = GW if c < sg else (r + 1) * P
                        last = nc.tensor.matmul(bank[:, 0:width],
                                                h.qT[0:STACK, e, (sg * GT + r) * P:(sg * GT + r + 1) * P],
                                                h.kT[0:STACK, c * GW:c * GW + width], start=True, stop=(c < sg))
                        if c == sg:
                            last = nc.tensor.matmul(bank[:, r * P:(r + 1) * P], h.unit[:, :], h.tri[:, :],
                                                    start=False, stop=True)
                        last.then_inc(s["m_full"], 1)
                    elif x[0] == "T":
                        bank = ring_wait(x)
                        pe.wait_ge(s["m3_ready"], n * NU + (x[1] + 1))
                        for r in range(GT):
                            last = nc.tensor.matmul(bank[STACK:STACK + 3, r * P:(r + 1) * P],
                                                    h.m3[:, x[1] % 2, r, :], core.ident16[:, :],
                                                    start=True, stop=True)
                        last.then_inc(s["mt_full"], 1)
                    elif x[0] == "E":
                        _, u, p = x
                        k = sum(2 * sch.units[v][1] + 2 for v in range(u)) + p
                        if p == 0:
                            pe.wait_ge(s["mt_read"], n * NU + (u + 1))
                        if k >= 2:
                            pe.wait_ge(s["exped"], n * NE + (k - 1))
                        for jj in range(2):
                            j = 2 * p + jj
                            lo = max(0, j - GT * sg) * P
                            bank = core.psum[2 * (k % 2) + jj]
                            diag = j >= GT * sg
                            last = nc.tensor.matmul(bank[:, lo:GW], h.kT[:, j * P:(j + 1) * P],
                                                    h.qT[:, e, sg * GW + lo:(sg + 1) * GW], start=True, stop=not diag)
                            if diag:
                                last = nc.tensor.matmul(bank[:, lo:lo + P], h.unit[:, :], h.triT[:, :],
                                                        start=False, stop=True)
                        last.then_inc(s["s_full"], 1)
                    elif x[0] == "A":
                        _, u, p, k = x
                        if residual_on_pool(k):
                            pe.wait_ge(s["low_pool"], n * NPOOL + sum(1 for q in range(k + 1) if residual_on_pool(q)))
                        else:
                            pe.wait_ge(s["low_dve"], n * (NE - NPOOL) + sum(1 for q in range(k + 1) if not residual_on_pool(q)))
                        if p == 0 and u >= 1:
                            pe.wait_ge(s["oT_in"], n * NU + u)
                        for jj in range(2):
                            j = 2 * p + jj
                            lo = max(0, j - GT * sg) * P
                            for part in (h.Phigh, h.Plow):
                                last = nc.tensor.matmul(core.psum[7][0:VW, lo:GW], h.V[:, j, :],
                                                        part[:, k % SLOTS, jj, lo:GW],
                                                        start=(j == 0 and part is h.Phigh),
                                                        stop=(j == GT * sg + GT - 1 and part is h.Plow),
                                                        skip_group_check=True)
                        last.then_inc(s["pv_done"], 1)
                    elif x[0] == "O":
                        u = x[1]
                        bank = ring_wait(x)
                        pe.wait_ge(s["oT_in"], n * NU + (u + 1))
                        for r in range(GT):
                            last = nc.tensor.matmul(bank[:, r * (HD + 1):(r + 1) * (HD + 1)],
                                                    h.oT[:, u % 2, r * P:(r + 1) * P], h.pick[:, :],
                                                    start=True, stop=True)
                        last.then_inc(s["po_full"], 1)
                    elif x[0] == "G":
                        bank = ring_wait(x)
                        pe.wait_ge(s["at_ready"], n * G + (sg + 1))
                        for r in range(GT):
                            last = nc.tensor.transpose(bank[:, r * P:(r + 1) * P], h.at[:, sg * GT + r, :],
                                                       core.ident[:, :])
                        last.then_inc(s["at_turned"], 1)
                    else:
                        bank = ring_wait(x)
                        pe.wait_ge(s["at_copied"], n * G + (sg + 1))
                        for r in range(GT):
                            last = nc.tensor.matmul(bank[:, r * QS:(r + 1) * QS],
                                                    h.atT[:, sg % 2, r * P:(r + 1) * P],
                                                    h.gw[:, ds(n, 1), :].rearrange("p a e -> p (a e)"),
                                                    start=True, stop=True)
                        last.then_inc(s["gate_sums"], 1)

        @block.scalar
        def _(act):
            with act.Fori(0, HEADS) as n:
                act.wait_ge(s["w_ready"], n + 1)

                def take_sx(g):
                    act.wait_ge(s["sx_sums"], n * G + (g + 1))
                    if g >= 2:
                        act.wait_ge(s["v_sums"], n * G + (g - 1))
                    nc.scalar.activation(h.sxs[:, g % 2, :], core.psum[5 + g % 2][0:STACK, :], ACT.Identity,
                                         bias=h.hlb_n[:, :]).then_inc(s["sx_high"], 1)
                    nc.scalar.activation(h.sxT[:, g % 2, :], core.psum[5 + g % 2][0:HD, :], ACT.Identity,
                                         bias=h.hlb_n[0:HD, :]).then_inc(s["sx_high"], 1)

                take_sx(0)
                for g in range(G):
                    if g + 1 < G:
                        take_sx(g + 1)
                    for e in range(QS + 1):
                        u = g * (QS + 1) + e
                        dst = h.qT[0:STACK, e, g * GW:(g + 1) * GW] if e < QS else h.kT[0:STACK, g * GW:(g + 1) * GW]
                        act.wait_ge(s["qk_sums"], n * U + (u + 1))
                        nc.scalar.activation(dst, core.psum[e][0:STACK, :], ACT.Copy,
                                             scale=1.0 / WEIGHT_UNIT).then_inc(s["qk_high"], 1)

                def copy_sums(u):
                    k = sum(2 * sch.units[v][1] + 2 for v in range(u + 1))
                    act.wait_ge(s["pv_done"], n * NE + (k + SLOTS))
                    act.wait_ge(s["po_full"], n * NU + (u + 1))
                    nc.scalar.activation(h.oT[:, u % 2, :], core.psum[7][0:VW, :], ACT.Copy).then_inc(s["oT_in"], 1)

                k, closed, ready = 0, 0, []
                for x in sch.events:
                    if x[0] == "T":
                        u = x[1]
                        e, sg = sch.units[u]
                        act.wait_ge(s["mt_full"], n * NU + (u + 1))
                        nc.scalar.activation(h.qT[STACK:STACK + 3, e, sg * GW:(sg + 1) * GW],
                                             ring_bank(x)[STACK:STACK + 3, :], ACT.Copy).then_inc(s["mt_read"], 1)
                    elif x[0] == "E":
                        _, u, p = x
                        act.wait_ge(s["s_full"], n * NE + (k + 1))
                        act.wait_ge(s["pv_done"], n * NE + (k + 1))
                        b = 2 * (k % 2)
                        for jj, lo in pair_parts(sch.units[u][1], p):
                            last = nc.scalar.activation(h.PT[:, k % SLOTS, jj, lo:GW],
                                                        core.banks[:, b + jj.start:b + jj.stop, lo:GW], ACT.Exp, scale=ROOT)
                        last.then_inc(s["exped"], 1)
                        k += 1
                    elif x[0] == "A" and x[2] == 2 * sch.units[x[1]][1] + 1:
                        copy_sums(x[1])
                    elif x[0] == "G":
                        g = sch.units[x[1]][1]
                        act.wait_ge(s["at_turned"], n * G + (g + 1))
                        if g >= 2:
                            act.wait_ge(s["gate_sums"], n * G + (g - 1))
                        nc.scalar.activation(h.atT[:, g % 2, :], ring_bank(x)[:, :],
                                             ACT.Copy).then_inc(s["at_copied"], 1)
                act.wait_ge(s["shifted"], n + 1)
                nc.scalar.activation(h.gs[:, :, :], h.gs[:, :, :], ACT.Exp).then_inc(s["gs_exp"], 1)
                act.wait_ge(s["var_ready"], n + 1)
                nc.scalar.activation(h.var[:, :], h.var[:, :], ACT.Sqrt).then_inc(s["std_ready"], 1)

        def subtract_high(eng, k, u, p):
            for jj, lo in pair_parts(sch.units[u][1], p):
                last = eng.tensor_tensor(h.Plow[:, k % SLOTS, jj, lo:GW], h.PT[:, k % SLOTS, jj, lo:GW],
                                         h.Phigh[:, k % SLOTS, jj, lo:GW], ALU.subtract)
            return last

        @block.gpsimd
        def _(pool):
            with pool.Fori(0, HEADS) as n:
                for x in sch.events:
                    if x[0] == "A" and residual_on_pool(x[3]):
                        _, u, p, k = x
                        pool.wait_ge(s["exped"], n * NE + (k + 1))
                        subtract_high(pool, k, u, p).then_inc(s["low_pool"], 1)

        @block.vector
        def _(dve):
            for w, split in ((h.wq[:, :, :, :].rearrange("r n e o -> r (n e) o"),
                              h.wqs[:, :, :, :, :].rearrange("r n e k o -> r (n e) k o")),
                             (h.wk[:, :, :], h.wks[:, :, :, :])):
                nc.vector.tensor_scalar(w, w, WEIGHT_UNIT, None, ALU.mult)
                dve.drain()
                nc.vector.tensor_copy(split[:, :, 0, :], w)
                dve.drain()
                nc.vector.tensor_tensor(split[HD:2 * HD, :, 0, :], w[HD:2 * HD, :, :], split[HD:2 * HD, :, 0, :],
                                        ALU.subtract)
                dve.drain()
                for k in (1, 2):
                    nc.vector.tensor_copy(split[:, :, k, :], split[:, :, 0, :])
            with dve.Fori(0, HEADS) as n:
                one = ds(n, 1)
                for k in range(3):
                    nc.vector.tensor_copy(h.hlw_n[:, k:k + 1, :], h.hlw[:, one, :])
                nc.vector.tensor_copy(h.hlb_n[:, :], h.hlb[:, one])
                nc.vector.tensor_copy(h.wvi_n[:, 0:HD].unsqueeze(1), h.wv[:, one, :])
                nc.vector.tensor_copy(h.wvi_n[:, HD:2 * HD], core.ident[0:HD, 0:HD])
                dve.drain().then_inc(s["w_ready"], 1)

                def split_sx(g):
                    low = h.sxs[2 * HD:STACK, g % 2, :]
                    dve.wait_ge(s["sx_high"], n * 2 * G + (2 * g + 2))
                    nc.vector.scalar_tensor_tensor(low, core.psum[5 + g % 2][2 * HD:STACK, :], h.hlb_n[2 * HD:STACK, :],
                                                   low, ALU.add, ALU.subtract).then_inc(s["sx_split"], 1)

                split_sx(0)
                for g in range(G):
                    if g + 1 < G:
                        split_sx(g + 1)
                    for e in range(QS + 1):
                        u = g * (QS + 1) + e
                        lo = 2 * HD if e < QS else HD
                        dst = h.qT[lo:lo + HD, e, g * GW:(g + 1) * GW] if e < QS else h.kT[lo:lo + HD, g * GW:(g + 1) * GW]
                        dve.wait_ge(s["qk_high"], n * U + (u + 1))
                        nc.vector.scalar_tensor_tensor(dst, core.psum[e][lo:lo + HD, :], 1.0 / WEIGHT_UNIT, dst,
                                                       ALU.mult, ALU.subtract).then_inc(s["qk_split"], 1)
                    dve.wait_ge(s["v_sums"], n * G + (g + 1))
                    both = core.psum[7][:, 0:GT * 2 * HD].rearrange("p (r w) -> p r w", w=2 * HD)
                    tiles = slice(g * GT, (g + 1) * GT)
                    v, rest = h.V[:, tiles, :], h.v32[:, g % 2, :, :]
                    nc.vector.tensor_copy(h.sx[:, tiles, :], both[:, :, HD:2 * HD])
                    nc.vector.tensor_copy(v[:, :, 0:HD], both[:, :, 0:HD])
                    dve.drain()
                    nc.vector.tensor_tensor(rest, both[:, :, 0:HD], v[:, :, 0:HD], ALU.subtract).then_inc(s["v_in"], 1)
                    dve.drain()
                    nc.vector.tensor_copy(v[:, :, HD:2 * HD], rest)
                    dve.drain()
                    nc.vector.tensor_tensor(v[:, :, 2 * HD:3 * HD], rest, v[:, :, HD:2 * HD],
                                            ALU.subtract).then_inc(s["low_dve_free"], 1)

                mcount = 0
                for x in sch.dve_events:
                    e, sg = sch.units[x[1]]
                    if x[0] == "M":
                        _, u, r, c = x
                        width = GW if c < sg else (r + 1) * P
                        dve.wait_ge(s["m_full"], n * NM + (mcount + 1))
                        nc.vector.tensor_reduce(h.pm[:, r, c:c + 1], ring_bank(x)[:, 0:width],
                                                AX.X, ALU.max).then_inc(s["m_read"], 1)
                        mcount += 1
                        if r == GT - 1 and c == sg:
                            m3 = h.m3[:, u % 2, :, :]
                            dve.drain()
                            nc.vector.tensor_reduce(h.nm[:, :], h.pm[:, :, 0:sg + 1], AX.X, ALU.max, negate=True)
                            dve.drain()
                            nc.vector.tensor_copy(m3[:, :, 0], h.nm[:, :])
                            dve.drain()
                            nc.vector.tensor_tensor(h.nd[:, :], h.nm[:, :], m3[:, :, 0], ALU.subtract)
                            dve.drain()
                            nc.vector.tensor_copy(m3[:, :, 1], h.nd[:, :])
                            dve.drain()
                            nc.vector.tensor_tensor(m3[:, :, 2], h.nd[:, :], m3[:, :, 1], ALU.subtract)
                            dve.drain().then_inc(s["m3_ready"], 1)
                    elif x[0] == "R":
                        _, u, p, k = x
                        dve.wait_ge(s["exped"], n * NE + (k + 1))
                        subtract_high(nc.vector, k, u, p).then_inc(s["low_dve"], 1)
                    elif x[0] == "O":
                        u = x[1]
                        po = ring_bank(x)[:, 0:GT * (HD + 1)].rearrange("p (r w) -> p r w", w=HD + 1)
                        dve.wait_ge(s["po_full"], n * NU + (u + 3))
                        nc.vector.reciprocal(h.rec[:, :], po[:, :, HD])
                        dve.drain()
                        tiles = slice(sg * GT, (sg + 1) * GT)
                        a = h.at[:, tiles, e * HD:(e + 1) * HD]
                        nc.vector.tensor_tensor(a, po[:, :, 0:HD], over(h.rec[:, :], HD), ALU.mult).then_inc(s["po_read"], 1)
                        dve.drain()
                        nc.vector.scalar_tensor_tensor(a, h.sx[:, tiles, :], 0.0, a, ALU.not_equal, ALU.mult)
                        if e == QS - 1:
                            dve.drain().then_inc(s["at_ready"], 1)
                    elif x[0] == "H":
                        dve.wait_ge(s["gate_sums"], n * G + (sg + 1))
                        nc.vector.tensor_tensor(h.gs[:, sg * GT:(sg + 1) * GT, :],
                                                ring_bank(x)[:, 0:GT * QS].rearrange("p (t e) -> p t e", e=QS),
                                                h.gb[:, one, :].broadcast_to([P, GT, QS]),
                                                ALU.add).then_inc(s["gate_read"], 1)

                dve.drain()
                softmax_rows(nc, dve, h.gs[:, :, :], h.stat[:, :], s["shifted"], s["gs_exp"], n + 1)
                nc.vector.tensor_copy(h.hn[:, :, :], h.sx[:, :, :])
                for e in range(QS):
                    nc.vector.tensor_tensor(h.tmp[:, :, :], h.at[:, :, e * HD:(e + 1) * HD],
                                            over(h.gs[:, :, e], HD), ALU.mult)
                    dve.drain()
                    nc.vector.tensor_tensor(h.hn[:, :, :], h.hn[:, :, :], h.tmp[:, :, :], ALU.add)
                    dve.drain()
                norm_rows(nc, dve, h.hn[:, :, :], h.hn[:, :, :], h.tmp[:, :, :], h.mean[:, :], h.var[:, :], HD,
                          EPS_HEAD, s["var_ready"], s["std_ready"], n + 1)
                nc.vector.tensor_tensor(h.hn[:, :, :], h.hn[:, :, :], rows(h.lng[:, :], T), ALU.mult)
                dve.drain()
                nc.vector.tensor_tensor(h.fx[:, :, ds(n * HD, HD)], h.hn[:, :, :], rows(h.lnb[:, :], T), ALU.add)
                dve.drain()


def head_mix_stage(core, h, bd1, bd2, b1, b2, ng, nb, fg, own):
    nc = core.nc

    def sb(name, shape):
        return own.enter_context(nc.sbuf_tensor("l1m_" + name, shape, FP32))
    fxT, h1, hx, sq = sb("fxT", [P, 2, GW]), sb("h1", [P, 2, GW]), core.xn, core.xT[:, :].rearrange("p (t d) -> p t d", d=D)
    mean, var = sb("mean", [P, T * HEADS]), sb("var", [P, T * HEADS])
    hg, stat = sb("hg", [P, T, HEADS]), sb("stat", [P, T])
    s = {n: core.sem("l1m_" + n) for n in
         ("turned", "fxT_in", "h1_sums", "h1_in", "h1_ready", "h2_sums", "h2_read", "var_ready", "std_ready",
          "out_ready", "out_turned", "out_copied", "fg_sums", "shifted", "exped")}
    blocks = lambda ap: ap.rearrange("p t (n d) -> p (t n) d", d=HD)
    with nc.Block() as block:
        @block.tensor
        def _(pe):
            for g in range(G):
                if g >= 2:
                    pe.wait_ge(s["fxT_in"], g - 1)
                for r in range(GT):
                    last = nc.tensor.transpose(core.psum[g % 2][:, r * P:(r + 1) * P], h.fx[:, g * GT + r, :],
                                               core.ident[:, :])
                last.then_inc(s["turned"], 1)
                pe.wait_ge(s["fxT_in"], g + 1)
                if g >= 2:
                    pe.wait_ge(s["h1_in"], g - 1)
                nc.tensor.matmul(core.psum[2 + g % 2][:, :], bd1[:, :], fxT[:, g % 2, :], start=True,
                                 stop=True).then_inc(s["h1_sums"], 1)
                pe.wait_ge(s["h1_ready"], g + 1)
                if g >= 2:
                    pe.wait_ge(s["h2_read"], g - 1)
                for r in range(GT):
                    last = nc.tensor.matmul(core.psum[4 + g % 2][:, r * P:(r + 1) * P],
                                            h1[:, g % 2, r * P:(r + 1) * P], bd2[:, :], start=True, stop=True)
                last.then_inc(s["h2_sums"], 1)
            pe.wait_ge(s["out_ready"], 1)
            for g in range(G):
                if g >= 2:
                    pe.wait_ge(s["out_copied"], g - 1)
                for r in range(GT):
                    last = nc.tensor.transpose(core.psum[g % 2][:, r * P:(r + 1) * P], hx[:, g * GT + r, :],
                                               core.ident[:, :])
                last.then_inc(s["out_turned"], 1)
                pe.wait_ge(s["out_copied"], g + 1)
                for r in range(GT):
                    t = g * GT + r
                    last = nc.tensor.matmul(core.psum[6][:, t * HEADS:(t + 1) * HEADS],
                                            fxT[:, g % 2, r * P:(r + 1) * P], fg[:, :], start=True, stop=True)
                last.then_inc(s["fg_sums"], 1)

        @block.scalar
        def _(act):
            for g in range(G):
                act.wait_ge(s["turned"], g + 1)
                if g >= 2:
                    act.wait_ge(s["h1_ready"], g - 1)
                nc.scalar.activation(fxT[:, g % 2, :], core.psum[g % 2][:, :], ACT.Copy).then_inc(s["fxT_in"], 1)
                act.wait_ge(s["h1_sums"], g + 1)
                if g >= 2:
                    act.wait_ge(s["h2_sums"], g - 1)
                nc.scalar.activation(h1[:, g % 2, :], core.psum[2 + g % 2][:, :], ACT.Relu,
                                     bias=b1[:, 0:1]).then_inc(s["h1_in"], 1)
            act.wait_ge(s["var_ready"], 1)
            nc.scalar.activation(var[:, :], var[:, :], ACT.Sqrt).then_inc(s["std_ready"], 1)
            for g in range(G):
                act.wait_ge(s["out_turned"], g + 1)
                if g >= 2:
                    act.wait_ge(s["fg_sums"], g - 1)
                nc.scalar.activation(fxT[:, g % 2, :], core.psum[g % 2][:, :], ACT.Copy).then_inc(s["out_copied"], 1)
            act.wait_ge(s["shifted"], 1)
            nc.scalar.activation(hg[:, :, :], hg[:, :, :], ACT.Exp).then_inc(s["exped"], 1)

        @block.vector
        def _(dve):
            for g in range(G):
                a = slice(g * GT, (g + 1) * GT)
                dve.wait_ge(s["h1_in"], g + 1)
                nc.vector.scalar_tensor_tensor(h1[:, g % 2, :], fxT[:, g % 2, :], 0.0, h1[:, g % 2, :],
                                               ALU.not_equal, ALU.mult).then_inc(s["h1_ready"], 1)
                dve.wait_ge(s["h2_sums"], g + 1)
                nc.vector.tensor_tensor(
                    blocks(hx[:, a, :]), core.psum[4 + g % 2][:, :].rearrange("p (n d) -> p n d", d=HD),
                    rows(b2[:, :], GT * HEADS), ALU.add).then_inc(s["h2_read"], 1)
                dve.drain()
                nc.vector.scalar_tensor_tensor(hx[:, a, :], h.fx[:, a, :], 0.0, hx[:, a, :], ALU.not_equal, ALU.mult)
                dve.drain()
                nc.vector.tensor_tensor(hx[:, a, :], hx[:, a, :], h.fx[:, a, :], ALU.add)
            dve.drain()
            norm_rows(nc, dve, blocks(hx[:, :, :]), blocks(hx[:, :, :]), blocks(sq), mean[:, :], var[:, :],
                      HD, EPS_HEAD, s["var_ready"], s["std_ready"], 1)
            nc.vector.tensor_tensor(blocks(hx[:, :, :]), blocks(hx[:, :, :]), rows(ng[:, :], T * HEADS), ALU.mult)
            dve.drain()
            nc.vector.tensor_tensor(blocks(hx[:, :, :]), blocks(hx[:, :, :]), rows(nb[:, :], T * HEADS), ALU.add)
            dve.drain().then_inc(s["out_ready"], 1)
            dve.wait_ge(s["fg_sums"], G)
            nc.vector.tensor_copy(hg[:, :, :], core.psum[6][:, 0:T * HEADS].rearrange("p (t e) -> p t e", e=HEADS))
            dve.drain()
            softmax_rows(nc, dve, hg[:, :, :], stat[:, :], s["shifted"], s["exped"], 1)
            nc.vector.tensor_tensor(blocks(hx[:, :, :]), blocks(hx[:, :, :]),
                                    over(hg[:, :, :].rearrange("p t n -> p (t n)"), HD), ALU.mult)
            dve.drain()
            nc.vector.tensor_tensor(core.x[:, :, :], core.x[:, :, :], hx[:, :, :], ALU.add)


def second_expert_layer(core, w):
    nc = core.nc
    with ExitStack() as own:
        def sb(name, shape):
            return own.enter_context(nc.sbuf_tensor("l1w_" + name, shape, FP32))
        h = HeadTiles(core, own)
        bd1, bd2, b1, b2 = sb("bd1", [P, P]), sb("bd2", [P, P]), sb("b1", [P, 1]), sb("b2", [P, HD])
        ng, nb, fg = sb("ng", [P, HD]), sb("nb", [P, HD]), sb("fg", [D, HEADS])
        with nc.Block() as block:
            @block.gpsimd
            def _(pool):
                nc.gpsimd.memset(bd1[:, :], 0.0)
                nc.gpsimd.memset(bd2[:, :], 0.0)
        attention_constants(core, h)
        loads = [(h.hlw[:, :, :], w["L1_ffn_hl_w"]), (h.hlb[:, :], w["L1_ffn_hl_b"]), (h.wq[:, :, :], w["L1_ffn_wq"]),
                 (h.wk[:, :, :], w["L1_ffn_wk"]), (h.wv[:, :, :], w["L1_ffn_wv"]), (h.gw[:, :, :], w["L1_ffn_gate_w"]),
                 (h.gb[:, :, :].rearrange("p n e -> p (n e)"),
                  w["L1_ffn_gate_b"].rearrange("n e -> (n e)").partition_broadcast(P)),
                 (h.lng[:, :], w["L1_ffn_ln_g"].partition_broadcast(P)),
                 (h.lnb[:, :], w["L1_ffn_ln_b"].partition_broadcast(P)),
                 (b2[:, :], w["L1_ffn_fc2_b"].partition_broadcast(P)),
                 (ng[:, :], w["L1_ffn_fnorm_g"].partition_broadcast(P)),
                 (nb[:, :], w["L1_ffn_fnorm_b"].partition_broadcast(P)), (fg[:, :], w["L1_ffn_fgate_w"])]
        for n in range(HEADS):
            a = slice(n * HD, (n + 1) * HD)
            loads += [(bd1[a, a], w["L1_ffn_fc1_w"]), (bd2[a, a], w["L1_ffn_fc2_w"]),
                      (b1[a, :], w["L1_ffn_fc1_b"].unsqueeze(1))]
        norm_stage(core, loads, "l1n")
        heads_stage(core, h)
        with ExitStack() as mix:
            head_mix_stage(core, h, bd1, bd2, b1, b2, ng, nb, fg, mix)


LAYERS = [first_graph_layer, first_expert_layer, second_graph_layer, second_expert_layer, third_graph_layer,
          third_expert_layer, fourth_graph_layer, fourth_expert_layer]
USED = ["x", "L0_gnn_W1", "L0_gnn_W2", "L0_gnn_b", "adjT", "L0_ffn_Wg", "L0_ffn_bg", "L0_ffn_W1", "L0_ffn_b1",
        "L0_ffn_W2", "L0_ffn_b2", "L1_gnn_W", "L1_gnn_a", "adj", "L1_ffn_hl_w", "L1_ffn_hl_b", "L1_ffn_wq",
        "L1_ffn_wk", "L1_ffn_wv", "L1_ffn_gate_w", "L1_ffn_gate_b", "L1_ffn_ln_g", "L1_ffn_ln_b",
        "L1_ffn_fc2_b", "L1_ffn_fnorm_g", "L1_ffn_fnorm_b", "L1_ffn_fgate_w", "L1_ffn_fc1_w", "L1_ffn_fc2_w",
        "L1_ffn_fc1_b", "L2_gnn_H_v", "L2_ffn_router_w1", "L2_ffn_router_b1", "L2_ffn_router_w2",
        "L2_ffn_router_b2", "L2_ffn_expert_w1", "L2_ffn_expert_w2", "L2_ffn_expert_w3", "L2_ffn_expert_b1",
        "L2_ffn_expert_b2", "L2_ffn_expert_b3", "L3_gnn_W", "L3_gnn_b", "L3_ffn_router_w", "L3_ffn_w1",
        "L3_ffn_w3", "L3_ffn_w2"]


def build(nc, w, out):
    with ExitStack() as ctx:
        core = Core(nc, ctx)
        core.begin_layer()
        load_inputs(core, w["x"])
        core.end_layer()
        for layer in LAYERS:
            core.begin_layer()
            layer(core, w)
            core.end_layer()
        core.begin_layer()
        store_output(core, out)
        core.end_layer()


def kernel(**inputs):
    import numpy as np
    import concourse.bacc as bacc
    from concourse.bass_utils import run_bass_kernel_spmd as run

    t = {name: np.asarray(a) for name, a in inputs.items()}
    tiles = N // P
    t["adjT"] = t["adj"].reshape(tiles, P, tiles, P).transpose(0, 3, 2, 1)
    t["L0_ffn_b1"] = t["L0_ffn_b1"].reshape(8, 2, P).transpose(2, 0, 1)
    t["L2_ffn_expert_b1"] = t["L2_ffn_expert_b1"].T
    t["L2_ffn_expert_b2"] = t["L2_ffn_expert_b2"].T
    t["L1_gnn_a"] = t["L1_gnn_a"].reshape(2, P).T
    t["L3_gnn_W"] = t["L3_gnn_W"].T
    t["L3_ffn_router_w"] = t["L3_ffn_router_w"].T
    for name in ("L3_ffn_w1", "L3_ffn_w3"):
        t[name] = t[name].transpose(2, 0, 1)
    t["L3_ffn_w2"] = t["L3_ffn_w2"].transpose(2, 0, 1)
    t["L1_ffn_hl_w"] = t["L1_ffn_hl_w"].transpose(2, 0, 1)
    t["L1_ffn_hl_b"] = np.tile(t["L1_ffn_hl_b"].T, (3, 1))
    t["L1_ffn_wq"] = np.tile(t["L1_ffn_wq"].transpose(3, 0, 1, 2), (3, 1, 1, 1))
    t["L1_ffn_wk"] = np.tile(t["L1_ffn_wk"].transpose(2, 0, 1), (3, 1, 1))
    t["L1_ffn_wv"] = t["L1_ffn_wv"].transpose(2, 0, 1)
    t["L1_ffn_gate_w"] = t["L1_ffn_gate_w"].transpose(2, 0, 1)
    t["L1_ffn_fc1_w"] = t["L1_ffn_fc1_w"].T
    t["L1_ffn_fc2_w"] = t["L1_ffn_fc2_w"].T
    t["L1_ffn_fgate_w"] = t["L1_ffn_fgate_w"].T
    nc = bacc.Bacc("TRN2", target_bir_lowering=False, num_devices=1)
    arrays, w = {}, {}
    for name in USED:
        a = np.ascontiguousarray(t[name])
        arrays[f"{name}_dram"] = a
        w[name] = nc.dram_tensor(f"{name}_dram", a.shape, mybir.dt.from_np(a.dtype), kind="ExternalInput").ap()
    out = nc.dram_tensor("out_dram", (N, D), FP32, kind="ExternalOutput").ap()
    build(nc, w, out)
    return run(nc, [arrays], core_ids=[0]).results[0]["out_dram"]
```
